# Optimizing a Trainium2 kernel written in Bass

```python
import numpy as np
import jax
import jax.numpy as jnp

def _softmax(x, axis=-1):
    return jax.nn.softmax(x, axis=axis)

def _gelu(x):
    return jax.nn.gelu(x, approximate=True)

def _silu(x):
    return jax.nn.silu(x)

def _sigmoid(x):
    return jax.nn.sigmoid(x)

def _layernorm(x, axis=-1, eps=1e-05):
    m = jnp.mean(x, axis=axis, keepdims=True)
    v = jnp.var(x, axis=axis, keepdims=True)
    return (x - m) / jnp.sqrt(v + eps)

def _scatter_add(tgt, idx, src, axis=0):
    return tgt.at[idx].add(src)

def _segment_sum(src, seg, n):
    return jax.ops.segment_sum(src, seg, n)
kernel_name = 'mk_adj_resnorm_d4_adj_r2_7e273b'

def setup_inputs(seed: int=0):
    np.random.seed(seed)
    _w = jnp.asarray

    def _rec_inputs():
        import jax
        import jax.numpy as jnp
        _gk = jax.random.key(seed)
        x = -0.000929 + 1 * jax.random.normal(jax.random.fold_in(_gk, 1), (4096, 128), jnp.float32)
        _a = jax.random.bernoulli(jax.random.fold_in(_gk, 2), 0.00390625, (4096, 4096))
        _a = jnp.logical_or(_a, jnp.swapaxes(_a, -1, -2))
        _a = jnp.logical_or(_a, jnp.eye(4096, dtype=bool))
        _af = _a.astype(jnp.float32)
        _af = _af * jax.random.uniform(jax.random.fold_in(_gk, 3), (4096, 4096), jnp.float32, 0.05, 0.0598829)
        adj = _af
        return (x, adj)
    x, adj = _rec_inputs()

    def _L0_gnn_setup():
        import jax, jax.numpy as jnp
        import numpy as np
        N, F_DIM, H_DIM = (4096, 128, 128)

        def _gwnn_layer(features, wavelets, wavelets_inv, W, filt):
            xw = features @ W
            spec = wavelets_inv @ xw
            spec = filt[:, None] * spec
            return wavelets @ spec
        key = jax.random.key(seed)
        ks = jax.random.split(key, 7)
        inp = {'input': jax.random.normal(ks[0], (N, F_DIM), dtype=jnp.float32), 'wavelets': jax.random.normal(ks[1], (N, N), dtype=jnp.float32) / np.sqrt(N), 'wavelets_inv': jax.random.normal(ks[2], (N, N), dtype=jnp.float32) / np.sqrt(N), 'W1': jax.random.uniform(ks[3], (F_DIM, H_DIM), dtype=jnp.float32, minval=-np.sqrt(6.0 / (F_DIM + H_DIM)), maxval=np.sqrt(6.0 / (F_DIM + H_DIM))), 'f1': jax.random.uniform(ks[4], (N,), dtype=jnp.float32, minval=0.9, maxval=1.1), 'W2': jax.random.uniform(ks[5], (H_DIM, H_DIM), dtype=jnp.float32, minval=-np.sqrt(6.0 / (H_DIM + H_DIM)), maxval=np.sqrt(6.0 / (H_DIM + H_DIM))), 'f2': jax.random.uniform(ks[6], (N,), dtype=jnp.float32, minval=0.9, maxval=1.1)}
        return inp
    _L0_gnn_all = _L0_gnn_setup()
    _L0_gnn_in = {k: v for k, v in _L0_gnn_all.items() if k in ('W1', 'f1', 'W2', 'f2')}
    del _L0_gnn_all

    def _L1_gnn_setup():
        import jax, jax.numpy as jnp
        import numpy as np
        K = 2
        NEG = -9000000000000000.0
        N, C, CO = (3072, 128, 128)

        def _ln(x, g, b, eps=1e-05):
            m = x.mean(-1, keepdims=True)
            v = ((x - m) ** 2).mean(-1, keepdims=True)
            return (x - m) / jnp.sqrt(v + eps) * g + b
        key = jax.random.key(seed)
        ks = jax.random.split(key, 6)
        x = jax.random.normal(ks[0], (N, C), jnp.float32)
        adj = (jax.random.uniform(ks[1], (N, N)) < 0.01).astype(jnp.float32)
        ff0_w = jax.random.normal(ks[2], (K, C, C), jnp.float32) / np.float32(np.sqrt(C))
        ff1_w = jax.random.normal(ks[3], (K, CO, C), jnp.float32) / np.float32(np.sqrt(C))
        attn_w = jax.random.normal(ks[4], (K, 2 * C), jnp.float32) / np.float32(np.sqrt(2 * C))
        return dict(x=x, adj=adj, ff0_w=ff0_w, ff1_w=ff1_w, attn_w=attn_w, g1=jnp.ones((C,), jnp.float32), b1=jnp.zeros((C,), jnp.float32), g2=jnp.ones((C,), jnp.float32), b2=jnp.zeros((C,), jnp.float32))
    _L1_gnn_all = _L1_gnn_setup()
    _L1_gnn_in = {k: v for k, v in _L1_gnn_all.items() if k in ('ff0_w', 'ff1_w', 'attn_w', 'g1', 'b1', 'g2', 'b2')}
    del _L1_gnn_all

    def _L2_gnn_setup():
        import jax, jax.numpy as jnp
        import numpy as np
        CUTOFF = 0.5
        key = jax.random.key(seed)
        k_z, k_d, k_w, k_mu, k_sg = jax.random.split(key, 5)
        N, D_IN, D_OUT = (4096, 128, 128)
        z = jax.random.normal(k_z, (N, D_IN), dtype=jnp.float32)
        dist_matrix = jax.random.uniform(k_d, (N, N), dtype=jnp.float32)
        W = jax.random.normal(k_w, (D_IN, D_OUT), dtype=jnp.float32)
        B = jnp.zeros((D_OUT,), dtype=jnp.float32)
        mu = jax.random.normal(k_mu, (1,), dtype=jnp.float32)
        sigma = jax.random.normal(k_sg, (1,), dtype=jnp.float32)
        return {'z': z, 'dist_matrix': dist_matrix, 'W': W, 'B': B, 'mu': mu, 'sigma': sigma}
    _L2_gnn_all = _L2_gnn_setup()
    _L2_gnn_in = {k: v for k, v in _L2_gnn_all.items() if k in ('W', 'B', 'mu', 'sigma')}
    del _L2_gnn_all

    def _L3_gnn_setup():
        import jax, jax.numpy as jnp
        import numpy as np
        N = 4096
        F_IN = 128
        F_OUT = 128
        BLOCK = 64

        def _graph_pool(out, adj):
            neg = jnp.asarray(jnp.finfo(out.dtype).min, out.dtype)

            def body(_, adj_blk):
                masked = jnp.where(adj_blk[:, :, None] != 0, out[None, :, :], neg)
                return (None, jnp.max(masked, axis=1))
            _, blocks = jax.lax.scan(body, None, adj.reshape(N // BLOCK, BLOCK, N))
            return blocks.reshape(N, out.shape[-1])
        key = jax.random.key(seed)
        k_in, k_adj, k_w, k_b = jax.random.split(key, 4)
        x = jax.random.normal(k_in, (N, F_IN), dtype=jnp.float32)
        adj = (jax.random.uniform(k_adj, (N, N)) < 0.01).astype(jnp.float32)
        adj = adj.at[jnp.arange(N), jnp.arange(N)].set(1.0)
        stdv = 1.0 / np.sqrt(F_OUT)
        weight = jax.random.uniform(k_w, (F_IN, F_OUT), minval=-stdv, maxval=stdv, dtype=jnp.float32)
        bias = jax.random.uniform(k_b, (F_OUT,), minval=-stdv, maxval=stdv, dtype=jnp.float32)
        return {'input': x, 'adj': adj, 'weight': weight, 'bias': bias}
    _L3_gnn_all = _L3_gnn_setup()
    _L3_gnn_in = {k: v for k, v in _L3_gnn_all.items() if k in ('weight', 'bias')}
    del _L3_gnn_all
    return {'x': x, 'adj': adj, 'L0_gnn_W1': _L0_gnn_in['W1'], 'L0_gnn_f1': _L0_gnn_in['f1'], 'L0_gnn_W2': _L0_gnn_in['W2'], 'L0_gnn_f2': _L0_gnn_in['f2'], 'L1_gnn_ff0_w': _L1_gnn_in['ff0_w'], 'L1_gnn_ff1_w': _L1_gnn_in['ff1_w'], 'L1_gnn_attn_w': _L1_gnn_in['attn_w'], 'L1_gnn_g1': _L1_gnn_in['g1'], 'L1_gnn_b1': _L1_gnn_in['b1'], 'L1_gnn_g2': _L1_gnn_in['g2'], 'L1_gnn_b2': _L1_gnn_in['b2'], 'L2_gnn_W': _L2_gnn_in['W'], 'L2_gnn_B': _L2_gnn_in['B'], 'L2_gnn_mu': _L2_gnn_in['mu'], 'L2_gnn_sigma': _L2_gnn_in['sigma'], 'L3_gnn_weight': _L3_gnn_in['weight'], 'L3_gnn_bias': _L3_gnn_in['bias']}

def reference(x, adj, L0_gnn_W1, L0_gnn_f1, L0_gnn_W2, L0_gnn_f2, L1_gnn_ff0_w, L1_gnn_ff1_w, L1_gnn_attn_w, L1_gnn_g1, L1_gnn_b1, L1_gnn_g2, L1_gnn_b2, L2_gnn_W, L2_gnn_B, L2_gnn_mu, L2_gnn_sigma, L3_gnn_weight, L3_gnn_bias):
    import jax
    import jax.numpy as jnp

    def _L0_gnn_ref(input, wavelets, wavelets_inv, W1, f1, W2, f2):
        import jax, jax.numpy as jnp
        import numpy as np
        N, F_DIM, H_DIM = (4096, 128, 128)

        def _gwnn_layer(features, wavelets, wavelets_inv, W, filt):
            xw = features @ W
            spec = wavelets_inv @ xw
            spec = filt[:, None] * spec
            return wavelets @ spec
        h1 = jax.nn.relu(_gwnn_layer(input, wavelets, wavelets_inv, W1, f1))
        out = _gwnn_layer(h1, wavelets, wavelets_inv, W2, f2)
        return out

    def _L1_gnn_ref(x, adj, ff0_w, ff1_w, attn_w, g1, b1, g2, b2):
        import jax, jax.numpy as jnp
        import numpy as np
        K = 2
        NEG = -9000000000000000.0
        N, C, CO = (3072, 128, 128)

        def _ln(x, g, b, eps=1e-05):
            m = x.mean(-1, keepdims=True)
            v = ((x - m) ** 2).mean(-1, keepdims=True)
            return (x - m) / jnp.sqrt(v + eps) * g + b
        n, c = x.shape
        co = ff1_w.shape[1]
        x_norm = _ln(x, g1, b1)
        mask = (adj > 0) | jnp.eye(n, dtype=bool)
        h_next = jnp.zeros((n, co), x.dtype)
        for i in range(K):
            h = x_norm @ ff0_w[i].T
            s_src = h @ attn_w[i, :c]
            s_dst = h @ attn_w[i, c:]
            e = jax.nn.leaky_relu(s_src[:, None] + s_dst[None, :])
            e = jnp.where(mask, e, jnp.float32(NEG))
            atten = jax.nn.softmax(e, axis=1)
            att = atten @ h + x
            att = _ln(att, g2, b2)
            h_next = h_next + jax.nn.elu(att @ ff1_w[i].T) / K
        return h_next

    def _L2_gnn_ref(z, dist_matrix, W, B, mu, sigma):
        import jax, jax.numpy as jnp
        import numpy as np
        CUTOFF = 0.5
        N = dist_matrix.shape[0]
        h = z @ W + B
        mask = (dist_matrix < CUTOFF) & ~jnp.eye(N, dtype=bool)
        r = jnp.where(mask, dist_matrix, 1.0)
        sens = jnp.exp(-(1.0 / r - 1.0 / mu[0]) ** 2 / (2.0 * sigma[0] ** 2))
        S = jnp.where(mask, sens, 0.0)
        return S @ h

    def _L3_gnn_ref(input, adj, weight, bias):
        import jax, jax.numpy as jnp
        import numpy as np
        N = 4096
        F_IN = 128
        F_OUT = 128
        BLOCK = 64

        def _graph_pool(out, adj):
            neg = jnp.asarray(jnp.finfo(out.dtype).min, out.dtype)

            def body(_, adj_blk):
                masked = jnp.where(adj_blk[:, :, None] != 0, out[None, :, :], neg)
                return (None, jnp.max(masked, axis=1))
            _, blocks = jax.lax.scan(body, None, adj.reshape(N // BLOCK, BLOCK, N))
            return blocks.reshape(N, out.shape[-1])
        h = input @ weight
        out = jnp.maximum(adj @ h + bias, 0.0)
        return _graph_pool(out, adj)
    x = _layernorm(x + _L0_gnn_ref(x, adj, adj, L0_gnn_W1, L0_gnn_f1, L0_gnn_W2, L0_gnn_f2), axis=-1)
    x = _layernorm(x + _L1_gnn_ref(x, adj, L1_gnn_ff0_w, L1_gnn_ff1_w, L1_gnn_attn_w, L1_gnn_g1, L1_gnn_b1, L1_gnn_g2, L1_gnn_b2), axis=-1)
    x = _layernorm(x + _L2_gnn_ref(x, adj, L2_gnn_W, L2_gnn_B, L2_gnn_mu, L2_gnn_sigma), axis=-1)
    x = _layernorm(x + _L3_gnn_ref(x, adj, L3_gnn_weight, L3_gnn_bias), axis=-1)
    return x

_drawn_inputs = setup_inputs


def setup_inputs(seed=0):
    import zlib

    import numpy as np

    out = dict(_drawn_inputs(seed))
    spreads = {'L1_gnn_g1': (1.0, 0.2),
     'L1_gnn_b1': (0.0, 0.1),
     'L1_gnn_g2': (1.0, 0.2),
     'L1_gnn_b2': (0.0, 0.1),
     'L2_gnn_B': (0.0, 0.1)}
    factors = {}
    for name, (base, spread) in spreads.items():
        noise = np.random.default_rng([zlib.crc32(name.encode()), seed]).standard_normal(out[name].shape)
        drawn = base * np.exp(spread * noise) if base else spread * noise
        out[name] = jnp.asarray(drawn.astype(out[name].dtype))
    for name, factor in factors.items():
        out[name] = (out[name] * factor).astype(out[name].dtype)
    return out
```

```python
from contextlib import ExitStack

import concourse.bass as bass
from concourse import mybir

P = 128
N = 4096
NT = N // P
HALF = N // 2
BANK = 512
NBUF = 4
ITERS = HALF // BANK
SLOTS = 2
REST = 16
QC = 1024
RANK = 200.0
SPREAD = 60.0
EPS = 1e-5
BIG = 3.4028234663852886e38
TINY = 1e-15

F32 = mybir.dt.float32
BF16 = mybir.dt.bfloat16
FP8 = mybir.dt.float8e4
I32 = mybir.dt.int32
U32 = mybir.dt.uint32
ALU = mybir.AluOpType
ACT = mybir.ActivationFunctionType
AX = mybir.AxisListType
RMAX = bass.bass_isa.ReduceOp.max
ds = bass.ds

USES_L0 = 0
USES_L2 = 4 * 2 * ITERS
USES_L3 = USES_L2 + 2 * ITERS
USES_POOL = USES_L3 + 2 * ITERS
L1_LOADS = 4 * 8


def program(nc, x, xT, adj, adjT, W1, f1, W2, f2, ff0, ff0T, ff1T, attc, g1, b1, g2, b2,
            L2W, L2B, mu, sigma, L3W, L3b, out, upto=9, spread=SPREAD, limit=0.0):
    with ExitStack() as ctx:
        def sb(name, shape, dt=F32):
            return ctx.enter_context(nc.sbuf_tensor(name, shape, dt))

        def sem(name):
            return ctx.enter_context(nc.semaphore(name))

        onehot_d = nc.dram_tensor("onehot_d", (SLOTS * NT * 2 * P, HALF // 4), F32, kind="Internal").ap()
        cand_d = nc.dram_tensor("cand_d", (P, NT * NT * 8), BF16, kind="Internal").ap()
        smax_d = nc.dram_tensor("smax_d", (2 * NT, P), F32, kind="Internal").ap()
        table_d = nc.dram_tensor("table_d", (N + P, P), F32, kind="Internal").ap()

        A = [sb(f"A{b}", [P, N]) for b in range(NBUF)]
        X = sb("X", [P, NT, P])
        V = sb("V", [P, NT, P])
        OT = sb("OT", [P, N])
        VS = sb("VS", [P, NBUF, 2, P])
        ident = sb("ident", [P, P])
        notid = sb("notid", [P, P])
        identb = sb("identb", [P, P], BF16)
        rankw = sb("rankw", [P, P], BF16)
        Wt = sb("Wt", [P, 4, P])
        RH = sb("RH", [P, 2 * P + 5])
        ff1s = sb("ff1s", [P, 2, P])
        cols = sb("cols", [P, 16])
        SRt = sb("SRt", [P, 2, P])
        fcol = sb("fcol", [P, 2, NT])
        st6 = sb("st6", [P, 2, NT, 6])
        mv = sb("mv", [P, 2, NT, 2])
        rstd = sb("rstd", [P, 2, NT])
        REGION = 21184
        R = sb("R", [P, REGION])

        def region(at, words, dt=F32):
            v = R[:, at:at + words]
            return v if dt == F32 else v.bitcast(dt)

        PS = ctx.enter_context(nc.psum_tensor("PS", [P, 8 * BANK], F32))
        acc = PS[:, 0:4 * BANK]

        def bank(k, n=BANK):
            return PS[:, k * BANK:k * BANK + n]

        w_in = sem("w_in")
        x_in = sem("x_in")
        consts = sem("consts")
        a_in = [sem(f"a_in{b}") for b in range(NBUF)]
        a_out = [sem(f"a_out{b}") for b in range(NBUF)]
        vs_in = [sem(f"vs_in{b}") for b in range(NBUF)]
        v_ready = sem("v_ready")
        acc_free = sem("acc_free")
        ot_ready = sem("ot_ready")
        ms_full = sem("ms_full")
        ms_free = sem("ms_free")
        mk = [sem(f"mk{w}") for w in range(2)]
        y_done = sem("y_done")
        y_act = sem("y_act")
        k_made = sem("k_made")
        t_done = sem("t_done")
        m8_done = sem("m8_done")
        c_cp = [sem(f"c_cp{w}") for w in range(2)]
        s_st = [[sem(f"s_st{w}{k}") for k in range(2)] for w in range(2)]
        cand_out = sem("cand_out")
        dv = sem("dv")
        ac = sem("ac")
        ln_var = sem("ln_var")
        ln_std = sem("ln_std")
        x_ready = sem("x_ready")
        out_st = sem("out_st")
        h_made = sem("h_made")
        sr_made = sem("sr_made")
        ext_made = sem("ext_made")
        ext_all = sem("ext_all")
        flag_made = sem("flag_made")
        gen_in = sem("gen_in")
        gen_used = sem("gen_used")
        mx_made = sem("mx_made")
        mxt_made = sem("mxt_made")
        smax_out = sem("smax_out")
        smax_in = sem("smax_in")
        src_full = sem("src_full")
        src_used = sem("src_used")
        b_made = sem("b_made")
        q_made = sem("q_made")
        mask_made = sem("mask_made")
        r_made = sem("r_made")
        p_made = sem("p_made")
        p_used = sem("p_used")
        rd_made = sem("rd_made")
        att_out = sem("att_out")
        att_done = sem("att_done")
        qt_made = sem("qt_made")
        e_neg = sem("e_neg")
        e_exp = sem("e_exp")
        ch = sem("ch")
        gen_own = sem("gen_own")
        gen_row = sem("gen_row")
        l2c_in = sem("l2c_in")
        dd_made = sem("dd_made")
        lnr = sem("lnr")
        u_made = sem("u_made")
        t_made = sem("t_made")
        n_made = sem("n_made")
        sq_made = sem("sq_made")
        e_made = sem("e_made")
        s_own = sem("s_own")
        s_made = sem("s_made")
        inv_made = sem("inv_made")
        cand_in = sem("cand_in")
        seg_made = sem("seg_made")
        lw = sem("lw")
        idx_made = sem("idx_made")
        o_ready = sem("o_ready")
        zero_made = sem("zero_made")
        tab_out = sem("tab_out")
        part_a = sem("part_a")
        part_d = sem("part_d")
        ix_cp = sem("ix_cp")
        g_in = [sem(f"g_in{w}") for w in range(2)]
        g_used = [sem(f"g_used{w}") for w in range(2)]
        px_full = sem("px_full")
        px_free = sem("px_free")
        bad_made = sem("bad_made")
        bad_all = sem("bad_all")
        flag2 = sem("flag2")
        dn_in = sem("dn_in")
        dn_used = sem("dn_used")
        dn = sem("dn")
        dnv = sem("dnv")

        block = ctx.enter_context(nc.Block())

        def settled(engine):
            engine.nop(nofuse=True)

        class Run:
            def __init__(self):
                self.n = 0

        Vb = region(0, 4096).rearrange("p (t c) -> p t c", c=P)
        Mk = region(4096, 2048, BF16).rearrange("p (w n) -> p w n", w=2)
        M01 = region(6144, 2048, BF16).rearrange("p (w n) -> p w n", w=2)
        Kb = region(8192, 512, BF16).rearrange("p (w n) -> p w n", w=2)
        SB = region(8704, 2048, FP8).rearrange("p (w k n) -> p w k n", w=2, k=2)
        SBw = region(8704, 2048).rearrange("p (w k n) -> p w k n", w=2, k=2)
        m8 = region(10752, 128, BF16).rearrange("p (w t e) -> p w t e", w=2, e=8)
        cand = region(10880, 4096, BF16).rearrange("p (t j e) -> p t j e", t=NT, j=NT)
        xT_s = OT

        HW = 2 * P + 5
        Hs = region(0, NT * HW).rearrange("p (t c) -> p t c", c=HW)
        at = NT * HW
        Bx = region(at, 4 * QC).rearrange("p (k e n) -> p k e n", k=2, e=2)
        at += 4 * QC
        QA = region(at, 4 * QC).rearrange("p (w k n) -> p w k n", w=2, k=2)
        QB = region(at + 4 * QC, 4 * QC).rearrange("p (w k n) -> p w k n", w=2, k=2)
        QT = region(at, 8 * QC).rearrange("p (k n) -> p k n", k=2)
        at += 8 * QC
        dst2 = region(at, 2 * NT).rearrange("p (t k) -> p t k", k=2)
        MX = region(at + 2 * NT, 2 * NT).rearrange("p (k t) -> p k t", k=2)
        MXT = region(at + 4 * NT, P)
        ext = region(at + 4 * NT + P, 16)
        at += 4 * NT + P + 16
        attw = region(at, 4)
        rden = region(at + 4, 16)
        assert at + 20 <= REGION
        Mt = VS[:, 0:2, :, :].rearrange("p a b c -> p (a b c)")
        Mt = VS[:, :, :, :].rearrange("p a b c -> p (a b c)").bitcast(BF16).rearrange("p (w n) -> p w n", w=2)
        SRv = SRt

        U = region(0, 8 * HALF).rearrange("p (w n) -> p w n", w=8)
        T = region(8 * HALF, 2 * HALF).rearrange("p (w n) -> p w n", w=2)
        BB = region(10 * HALF, P)
        DD = region(10 * HALF + P, 2 * P)

        OP = region(0, 3 * NT * P // 2, BF16).rearrange("p (e t c) -> p e t c", e=3, t=NT)
        OPw = region(0, 3 * NT * P // 2).rearrange("p (e t c) -> p e t c", e=3, t=NT)
        HOTW = HALF * SLOTS // 2
        pat = 3 * NT * P // 2
        cand2 = region(pat, 4096, BF16).rearrange("p (t n) -> p t n", t=NT)
        r1 = region(pat + 4096, 4096)
        G = region(pat + 8192, 2 * REST * P).rearrange("p (w k c) -> p w k c", w=2, k=REST)
        pat += 8192 + 2 * REST * P
        LST = region(pat, NT * REST).rearrange("p (t e) -> p t e", e=REST)
        IDX = region(pat + NT * REST, NT * REST, U32).rearrange("p (t e) -> p t e", e=REST)
        pat += 2 * NT * REST
        K1 = region(pat, 256)
        K2 = region(pat + 256, 256)
        segb = region(pat + 512, 256)
        segi = region(pat + 768, 256, I32)
        pat += 1024
        m8x = region(pat, 32)
        ixs = region(pat + 32, 2 * REST, U32).rearrange("p (w e) -> p w e", w=2)
        bad = region(pat + 64, 16)
        rowm = region(pat + 80, NT)
        assert pat + 80 + NT <= REGION
        e_t = region(0, 4 * BANK).rearrange("p (w n) -> p w n", w=4)
        r_t = region(4 * BANK, 4 * BANK).rearrange("p (w n) -> p w n", w=4)

        def v_of(p):
            return V[:, :, :] if p % 2 == 0 else Vb

        def swapped(p):
            return 1 if p >= 2 else 0

        def blk(h, it, b):
            return (16 * h + 8 * it + 2 * b) % NT

        NGRP = NBUF * 2 * SLOTS
        A_L1 = 2 * ITERS

        @block.sync
        def _(sp):
            sp.dma_start(xT_s[:, :], xT).then_inc(x_in, 16)
            sp.dma_start(X[:, :, :], x.rearrange("(t p) c -> p t c", p=P)).then_inc(x_in, 16)

            def load_A(u, b, j, h):
                sp.dma_start(A[b][:, :].rearrange("p (k n) -> p k n", k=2),
                             adjT[ds(j * P, 2 * P), ds(h * HALF, HALF)].rearrange("(k p) n -> p k n", p=P))\
                    .then_inc(a_in[b], 16)

            def load_V(b, j, v):
                sp.dma_start(VS[:, b, :, :], v[:, ds(j, 2), :]).then_inc(vs_in[b], 16)

            def product_loads(u0, v, swap, ready, units, aofs=0):
                for b in range(NBUF):
                    if aofs and b == 0:
                        sp.wait_ge(mask_made, L1_LOADS * 4)
                    sp.wait_ge(a_out[b], u0)
                    if units and b % 2 == 0:
                        sp.wait_ge(mk[b // 2], u0)
                    load_A(u0, b, blk(0, 0, b ^ swap), 0)
                sp.wait_ge(v_ready, ready)
                for b in range(NBUF):
                    load_V(b, blk(0, 0, b ^ swap), v)
                with sp.Fori(1, 2 * ITERS) as n:
                    h = sp.snap(n // ITERS)
                    first = sp.snap((n * 8 + h * 16) % NT, max_val=NT - 8)
                    for b in range(NBUF):
                        j = sp.snap(first + 2 * (b ^ swap), max_val=NT - 2)
                        sp.wait_ge(a_out[b], n + u0)
                        if units and b % 2 == 0:
                            sp.wait_ge(mk[b // 2], n + u0)
                        load_A(n, b, j, h)
                        load_V(b, j, v)

            for p in range(4):
                product_loads(USES_L0 + 2 * ITERS * p, v_of(p), swapped(p), p + 1, True)
            for w in range(2):
                sp.wait_ge(c_cp[w], USES_L2)
            sp.dma_start(cand_d, cand.rearrange("p t j e -> p (t j e)")).then_inc(cand_out, 16)
            if upto == 0:
                sp.wait_ge(x_ready, 1)
                sp.wait_ge(cand_out, 16)
                for w in range(2):
                    for k in range(2):
                        sp.wait_ge(s_st[w][k], 16 * USES_L2)
                sp.dma_start(out.rearrange("(t p) c -> p t c", p=P), X[:, :, :]).then_inc(out_st, 16)
                sp.wait_ge(out_st, 16)
                return

            def load_chunk(b, q, j0):
                sp.dma_start(A[b][:, :].rearrange("p (k n) -> p k n", k=4),
                             adjT[ds(j0 * P, 4 * P), ds(q * QC, QC)].rearrange("(k p) n -> p k n", p=P))\
                    .then_inc(a_in[b], 16)

            sp.wait_ge(flag_made, 1)
            flag = sp.value_load(ext[0:1, 12:13].bitcast(I32), min_val=0, max_val=1)
            for b in range(NBUF):
                sp.wait_ge(a_out[b], USES_L2)
            with sp.If(flag > 0):
                for k in range(2):
                    sp.dma_start(smax_d[k * NT:(k + 1) * NT, :].rearrange("t p -> p t"),
                                 Hs[:, :, 2 * P + 2 + 2 * k], allow_slow_non_contiguous=True).then_inc(gen_in, 16)
                sp.wait_ge(gen_in, 32)
                for k in range(2):
                    sp.dma_start(A[1 + k][:, :],
                                 smax_d[k * NT:(k + 1) * NT, :].rearrange("(a t) p -> a (t p)", a=1).partition_broadcast(P))\
                        .then_inc(gen_in, 16)
                with sp.Fori(0, NT) as t:
                    sp.wait_ge(gen_used, t)
                    sp.dma_start(A[0][:, :], adj[ds(t * P, P), :]).then_inc(gen_row, 16)
                sp.wait_ge(gen_used, NT)
            with sp.Else():
                pass
            sp.wait_ge(mxt_made, 1)
            sp.dma_start(smax_d, MXT[0:2 * NT, :]).then_inc(smax_out, 16)
            sp.wait_ge(smax_out, 16)
            for b in range(NBUF):
                load_chunk(b, 0, 4 * b)
            with sp.Fori(0, 4) as q:
                sp.wait_ge(q_made, 64 * q)
                for k in range(2):
                    sp.dma_start(Bx[:, k, 1, :],
                                 smax_d[ds(k * NT + 8 * q, 8), :].rearrange("(a t) p -> a (t p)", a=1).partition_broadcast(P))\
                        .then_inc(smax_in, 16)
                for n in range(4, 8):
                    sp.wait_ge(mask_made, 32 * q + (4 * (n - 4) + 4))
                    load_chunk(n % NBUF, q, sp.snap((8 * q + 4 * n) % NT, max_val=NT - 4))
                with sp.If(q < 3):
                    for n in range(4):
                        sp.wait_ge(mask_made, 32 * q + (4 * (n + 4) + 4))
                        load_chunk(n, sp.snap((q + 1) % 4), sp.snap((8 * q + (4 * n + 8)) % NT, max_val=NT - 4))
                with sp.Else():
                    pass
            def finish(n):
                sp.wait_ge(x_ready, n)
                sp.dma_start(out.rearrange("(t p) c -> p t c", p=P), X[:, :, :]).then_inc(out_st, 16)
                sp.wait_ge(out_st, 16)

            if upto == 1:
                finish(2)
                return

            sp.wait_ge(x_ready, 2)
            sp.dma_start(BB, L2B.partition_broadcast(P)).then_inc(l2c_in, 16)
            product_loads(USES_L2, V[:, :, :], 0, 6, False, aofs=8)
            if upto == 2:
                finish(3)
                return

            for b in range(NBUF):
                sp.wait_ge(a_out[b], USES_L3)
            sp.dma_start(cand2.rearrange("p t n -> p (t n)"), cand_d).then_inc(cand_in, 16)
            product_loads(USES_L3, V[:, :, :], 0, 7, False)
            sp.wait_ge(zero_made, 1)
            sp.dma_start(table_d[N:N + P, :], K1[:, 0:P]).then_inc(tab_out, 16)
            sp.wait_ge(v_ready, 8)
            sp.dma_start(table_d[0:N, :].rearrange("(t p) c -> p t c", p=P), V[:, :, :]).then_inc(tab_out, 16)
            one_v = onehot_d.rearrange("(k j h p) n -> p k j h n", k=SLOTS, j=NT, h=2)
            with sp.Fori(0, 2 * ITERS) as n:
                h = sp.snap(n // ITERS)
                for b in range(NBUF):
                    sp.wait_ge(a_out[b], n + USES_POOL)
                    j = sp.snap((n * 8 + 2 * b) % NT, max_val=NT - 2)
                    dst = A[b][:, 0:HOTW].rearrange("p (k j n) -> p k j n", k=SLOTS, j=2)
                    for k in range(SLOTS):
                        sp.dma_start(dst[:, k, :, :], one_v[:, k, ds(j, 2), ds(h, 1), :].rearrange("p j h n -> p j (h n)"))\
                            .then_inc(a_in[b], 16)
                    if b == 0:
                        sp.wait_ge(part_a, 3)
                    sp.dma_start(A[b][:, HOTW:HOTW + 3 * P].rearrange("p (e j c) -> p e j c", e=3, j=2),
                                 OPw[:, :, ds(j, 2), :]).then_inc(a_in[b], 16)
            sp.wait_ge(flag2, 1)
            flag = sp.value_load(bad[0:1, 8:9].bitcast(I32), min_val=0, max_val=1)
            with sp.If(flag > 0):
                with sp.Fori(0, NT) as t:
                    with sp.Fori(0, NT * 4) as c:
                        sp.wait_ge(dn_used, 2 * (t * (NT * 4) + c))
                        sp.dma_start(A[0][:, :], table_d[ds(c * 32, 32), :].rearrange("(a j) c -> a (j c)", a=1)
                                     .partition_broadcast(P)).then_inc(dn_in, 16)
                        sp.dma_start(A[1][:, 0:32], adj[ds(t * P, P), ds(c * 32, 32)]).then_inc(dn_in, 16)
            with sp.Else():
                pass
            finish(5)

        @block.gpsimd
        def _(pool):
            n = Run()

            def step(ins):
                n.n += 1
                ins.then_inc(consts, 1)
                pool.wait_ge(consts, n.n)

            step(pool.memset(ident[:, :], 0.0))
            step(pool.affine_select(out=ident[:, :], in_=ident[:, :], compare_op=ALU.not_equal, fill=1.0,
                                    base=0, pattern=[[-1, P]], channel_multiplier=1))
            step(pool.memset(notid[:, :], 1.0))
            step(pool.affine_select(out=notid[:, :], in_=notid[:, :], compare_op=ALU.not_equal, fill=0.0,
                                    base=0, pattern=[[-1, P]], channel_multiplier=1))
            rk = R[:, 0:P]
            step(pool.memset(rk, -1.0))
            step(pool.affine_select(out=rk, in_=rk, compare_op=ALU.is_gt, fill=0.0,
                                    base=0, pattern=[[1, P]], channel_multiplier=-1))
            step(pool.affine_select(out=rk, in_=rk, compare_op=ALU.not_equal, fill=RANK,
                                    base=0, pattern=[[-1, P]], channel_multiplier=1))
            step(pool.tensor_copy(rankw[:, :], rk))
            step(pool.tensor_copy(identb[:, :], ident[:, :]))
            step(pool.memset(cols[:, 5:6], EPS))
            step(pool.memset(cols[:, 7:8], 1.0 - RANK))
            step(pool.memset(cols[:, 13:14], TINY))
            step(pool.iota(cols[:, 14:15].bitcast(I32), pattern=[[0, 1]], base=1, channel_multiplier=1))
            step(pool.tensor_copy(cols[:, 6:7], cols[:, 14:15].bitcast(I32)))
            pool.dma_start(Wt[:, 0, :], W1).then_inc(w_in, 16)
            pool.dma_start(Wt[:, 1, :], W2).then_inc(w_in, 16)
            pool.dma_start(Wt[:, 2, :], L2W).then_inc(w_in, 16)
            pool.dma_start(Wt[:, 3, :], L3W).then_inc(w_in, 16)
            pool.dma_start(fcol[:, 0, :], f1).then_inc(w_in, 16)
            pool.dma_start(fcol[:, 1, :], f2).then_inc(w_in, 16)
            for c, src in enumerate((g1, b1, g2, b2, L3b)):
                pool.dma_start(cols[:, c:c + 1], src).then_inc(w_in, 16)
            pool.dma_start(cols[:, 8:9], mu.partition_broadcast(P)).then_inc(w_in, 16)
            pool.dma_start(cols[:, 9:10], sigma.partition_broadcast(P)).then_inc(w_in, 16)
            pool.dma_start(RH[:, 0:P], ff0T[0]).then_inc(w_in, 16)
            pool.dma_start(RH[:, P + 1:2 * P + 1], ff0T[1]).then_inc(w_in, 16)
            pool.dma_start(ff1s[:, :, :], ff1T.rearrange("k c o -> c k o")).then_inc(w_in, 16)

            for p in range(4):
                with pool.Fori(0, 2 * ITERS) as n:
                    it = pool.snap(n + 2 * ITERS * p)
                    h = pool.snap(n // ITERS)
                    first = pool.snap((n * 8 + h * 16) % NT, max_val=NT - 8)
                    for w in range(2):
                        row = pool.snap(((first + 2 * ((2 * w) ^ swapped(p)) + p % 2) * 2 + h) * P, max_val=(2 * NT - 1) * P)
                        pool.wait_ge(y_act, 8 * it + (4 * w + 5))
                        pool.dma_start(onehot_d[ds(row, P), :], SBw[:, w, 0, :]).then_inc(s_st[w][0], 16)
                        pool.wait_ge(k_made, 8 * it + (4 * w + 4))
                        pool.dma_start(onehot_d[ds(row + 2 * NT * P, P), :], SBw[:, w, 1, :])\
                            .then_inc(s_st[w][1], 16)
            if upto == 0:
                return
            for w in range(2):
                for k in range(2):
                    pool.wait_ge(s_st[w][k], 16 * USES_L2)
            pool.wait_ge(x_ready, 1)
            pool.wait_ge(cand_out, 16)
            pool.dma_start(QB[:, 0, 0, 0:2 * P].rearrange("p (k c) -> p k c", k=2),
                           ff0.rearrange("k o c -> o k c")).then_inc(w_in, 16)
            pool.dma_start(attw, attc).then_inc(w_in, 16)
            pool.wait_ge(ext_made, 1)
            pool.partition_all_reduce(ext[:, 4:8], ext[:, 0:4], P, RMAX).then_inc(ext_all, 1)
            if upto == 1:
                return

            pool.wait_ge(x_ready, 2)
            pool.tensor_copy(DD[:, 0:P], notid[:, :])
            pool.memset(DD[:, P:2 * P], 1.0).then_inc(dd_made, 1)
            with pool.Fori(0, 2 * ITERS) as n:
                for k in range(8):
                    b, jj = k // 2, k % 2
                    pool.wait_ge(u_made, 8 * n + (k + 1))
                    pool.wait_ge(a_in[b], 16 * n + 16 * (USES_L2 + A_L1 + 1))
                    pool.wait_ge(n_made, 8 * n + k)
                    pool.tensor_tensor(T[:, k % 2, :], A[b][:, jj * HALF:(jj + 1) * HALF], U[:, k, :], ALU.mult)\
                        .then_inc(t_made, 1)
            if upto == 2:
                return

            for b in range(NBUF):
                pool.wait_ge(a_out[b], USES_L3)
            pool.iota(segi.rearrange("p (s e) -> p s e", e=8), pattern=[[P, NT], [0, 8]], base=0,
                      channel_multiplier=0).then_inc(seg_made, 1)
            pool.wait_ge(seg_made, 1)
            pool.tensor_copy(segb, segi).then_inc(seg_made, 1)
            pool.wait_ge(idx_made, 1)
            pool.wait_ge(tab_out, 32)
            with pool.Fori(0, NT // 2) as n:
                for w in range(2):
                    pool.wait_ge(g_used[w], n)
                    pool.wait_ge(g_in[w], 16 * REST * n)
                    pool.tensor_copy(ixs[:, w, :], IDX[:, ds(2 * n + w, 1), :].squeeze(1)).then_inc(ix_cp, 1)
                    pool.wait_ge(ix_cp, 2 * n + (w + 1))
                    settled(pool)
                    for e in range(REST):
                        pool.indirect_dma_start(G[:, w, e, :], None, table_d,
                                                bass.IndirectOffsetOnAxis(ap=ixs[:, w, e:e + 1], axis=0))\
                            .then_inc(g_in[w], 16)
            pool.wait_ge(bad_made, 1)
            pool.partition_all_reduce(bad[:, 4:5], bad[:, 0:1], P, RMAX).then_inc(bad_all, 1)

        @block.tensor
        def _(pe):
            ms = Run()

            drained = [0]

            def drain():
                pe.wait_ge(ms_free, ms.n)
                drained[0] = ms.n

            def misc(n=BANK):
                if ms.n - 3 > drained[0]:
                    pe.wait_ge(ms_free, ms.n - 3)
                k = 4 + ms.n % 4
                ms.n += 1
                return bank(k, n)

            def transposes(src):
                for g in range(8):
                    m = misc()
                    for k in range(4):
                        t = 4 * g + k
                        last = pe.transpose(m[:, k * P:(k + 1) * P], src(t), ident[:, :])
                    last.then_inc(ms_full, 1)

            def features(lhsT, rhs):
                for g in range(8):
                    m = misc()
                    for k in range(4):
                        last = pe.matmul(m[:, k * P:(k + 1) * P], lhsT(4 * g + k), rhs, start=True, stop=True)
                    last.then_inc(ms_full, 1)

            def unit_step(w, s, it):
                g = 8 * it + (4 * w + s)
                if s < 4:
                    if s == 0:
                        pe.wait_ge(mk[w], it + 1)
                    pe.wait_ge(y_act, g)
                    pe.matmul(bank(4 + s % 2), rankw[:, :], M01[:, w, s * BANK:(s + 1) * BANK],
                              start=True, stop=True).then_inc(y_done, 1)
                if s > 0:
                    pe.wait_ge(k_made, g)
                    pe.wait_ge(m8_done, g - 1)
                    half = (s - 1) % 2
                    tb = bank(6 + half).bitcast(BF16)[:, 0:BANK]
                    for k in range(4):
                        last = pe.transpose(tb[:, k * P:(k + 1) * P],
                                            Kb[:, half, k * P:(k + 1) * P], identb[:, :])
                    last.then_inc(t_done, 1)

            UNIT_AT = {2 + 3 * s + 16 * w: (w, s) for w in range(2) for s in range(5)}

            def product(u0, aofs=0, p=None, weights=False):
                with pe.Fori(0, 2) as h:
                    pe.wait_ge(acc_free, 4 * (u0 // (2 * ITERS)) * 2 + 4 * h)

                    def one(it, first, last):
                        u = pe.snap(h * ITERS + it)
                        for b in range(NBUF):
                            if not weights:
                                pe.wait_ge(a_in[b], 16 * u + 16 * (u0 + 1 + aofs))
                            pe.wait_ge(vs_in[b], 16 * u + 16 * (u0 + 1))
                            for m in range(8):
                                jj, k = m // 4, m % 4
                                if weights:
                                    if k == 0:
                                        pe.wait_ge(s_made, 8 * u + (2 * b + jj + 1))
                                    rhs = U[:, 2 * b + jj, k * BANK:(k + 1) * BANK]
                                else:
                                    rhs = A[b][:, jj * HALF + k * BANK:jj * HALF + (k + 1) * BANK]
                                ins = pe.matmul(bank(k), VS[:, b, jj, :], rhs,
                                                start=first and b == 0 and jj == 0,
                                                stop=last and b == NBUF - 1 and jj == 1)
                                if m == 7:
                                    ins.then_inc(a_out[b], 1)
                                if p is not None and 8 * b + m in UNIT_AT:
                                    unit_step(*UNIT_AT[8 * b + m], u + u0)

                    one(0, True, False)
                    with pe.Fori(1, ITERS - 1) as it:
                        one(it, False, False)
                    one(ITERS - 1, False, True)

            pe.wait_ge(x_in, 32)
            pe.wait_ge(w_in, 16 * 16)
            pe.wait_ge(consts, 14)
            features(lambda t: xT_s[:, t * P:(t + 1) * P], Wt[:, 0, :])
            for p in range(4):
                product(2 * ITERS * p, p=p)
                pe.wait_ge(ot_ready, 8 * (p + 1))
                pe.wait_ge(y_act, 8 * 2 * ITERS * (p + 1) + 1)
                pe.wait_ge(m8_done, 8 * 2 * ITERS * (p + 1) + 1)
                if p == 1:
                    features(lambda t: OT[:, t * P:(t + 1) * P], Wt[:, 1, :])
                else:
                    transposes(lambda t: OT[:, t * P:(t + 1) * P])
                drain()
            if upto == 0:
                return

            pe.wait_ge(x_ready, 1)
            pe.wait_ge(ln_std, 2)
            pe.wait_ge(v_ready, 5)
            transposes(lambda t: V[:, t, :])
            pe.wait_ge(w_in, 16 * 18)
            m = misc()
            for k in range(2):
                last = pe.matmul(m[:, 2 * k:2 * k + 2], QB[:, 0, 0, k * P:(k + 1) * P], attw[:, 2 * k:2 * k + 2],
                                 start=True, stop=True)
            last.then_inc(ms_full, 1)
            pe.wait_ge(ot_ready, 33)
            pe.wait_ge(sr_made, 1)
            for t in range(NT):
                m = misc(HW)
                pe.matmul(m, OT[:, t * P:(t + 1) * P], RH[:, :], start=True, stop=True).then_inc(ms_full, 1)
            pe.wait_ge(mx_made, 1)
            drain()
            m = misc(P)
            pe.transpose(m[0:2 * NT, :], MX.rearrange("p k t -> p (k t)"), ident[:, :]).then_inc(ms_full, 1)
            drain()

            def source_rows(q):
                for k in range(2):
                    pe.wait_ge(src_used, 2 * q + k)
                    for e in range(2):
                        last = pe.matmul(bank(6 + e), SRv[:, k, :], OT[:, ds(q * QC + e * BANK, BANK)],
                                         start=True, stop=True)
                    last.then_inc(src_full, 1)

            def region_of(k, it):
                r = 8 * k + it
                return PS[:, (r // 3) * BANK + (r % 3) * (P + 1):(r // 3) * BANK + (r % 3 + 1) * (P + 1)]

            pe.wait_ge(h_made, 1)
            with pe.Fori(0, 4) as q:
                source_rows(q)
                pe.wait_ge(att_out, 16 * q)
                for s in range(32):
                    j = pe.snap((8 * q + s) % NT, max_val=NT - 1)
                    for k in range(2):
                        pe.wait_ge(p_made, 64 * q + (2 * s + k + 1))
                        for it in range(8):
                            last = pe.matmul(region_of(k, it), QA[:, s % 2, k, it * P:(it + 1) * P],
                                             Hs[:, ds(j, 1), k * P:k * P + P + 1],
                                             start=s == 0 and (8 * k + it) % 3 == 0, stop=s == 31,
                                             skip_group_check=True)
                        last.then_inc(p_used, 1)

            for k in range(2):
                pe.wait_ge(att_done, k + 1)
                src = V[:, :, :] if k == 0 else OT[:, :].rearrange("p (t c) -> p t c", c=P)
                transposes(lambda t: src[:, t, :])
            drain()
            for k in range(2):
                pe.wait_ge(qt_made, k + 1)
                features(lambda t: QT[:, k, t * P:(t + 1) * P], ff1s[:, k, :])
            drain()
            if upto == 1:
                return

            pe.wait_ge(x_ready, 2)
            transposes(lambda t: X[:, t, :])
            drain()
            pe.wait_ge(ot_ready, 34)
            features(lambda t: OT[:, t * P:(t + 1) * P], Wt[:, 2, :])
            product(USES_L2, weights=True)
            pe.wait_ge(ot_ready, 42)
            drain()
            transposes(lambda t: OT[:, t * P:(t + 1) * P])
            drain()
            if upto == 2:
                return

            pe.wait_ge(x_ready, 3)
            transposes(lambda t: X[:, t, :])
            drain()
            pe.wait_ge(ot_ready, 43)
            features(lambda t: OT[:, t * P:(t + 1) * P], Wt[:, 3, :])
            product(USES_L3, aofs=A_L1)
            pe.wait_ge(ot_ready, 51)
            drain()
            transposes(lambda t: OT[:, t * P:(t + 1) * P])
            drain()
            with pe.Fori(0, 2 * ITERS) as n:
                for b in range(NBUF):
                    pe.wait_ge(a_in[b], 48 * n + (16 * (USES_POOL + A_L1) + 48))
                    ob = A[b][:, HOTW:HOTW + 3 * P].bitcast(BF16).rearrange("p (e j c) -> p e j c", e=3, j=2)
                    hot = A[b][:, 0:HOTW].bitcast(FP8).rearrange("p (k j n) -> p k j n", k=SLOTS, j=2)
                    for jj in range(2):
                        for k in range(SLOTS):
                            g = (b * 2 + jj) * SLOTS + k
                            pe.wait_ge(px_free, NGRP * n + (g + 1))
                            settled(pe)
                            for e in range(3):
                                for c in range(4):
                                    last = pe.matmul(bank(4 * (g % 2) + c), ob[:, e, jj, :],
                                                     hot[:, k, jj, c * BANK:(c + 1) * BANK],
                                                     start=e == 0, stop=e == 2)
                            if g % (2 * SLOTS) == 2 * SLOTS - 1:
                                last.then_inc(a_out[b], 1)
                            else:
                                last.then_inc(px_full, 1)
            pe.wait_ge(px_free, NGRP * 2 * ITERS + 2)
            pe.wait_ge(x_ready, 4)
            transposes(lambda t: OT[:, t * P:(t + 1) * P])

        def half_out(act, n, u0, func, **kw):
            if isinstance(n, int):
                act.wait_ge(a_out[NBUF - 1], u0 + n + 1)
                for k in range(4):
                    at = n // ITERS * HALF + k * BANK
                    act.activation(OT[:, at:at + BANK], bank(k), func, **kw).then_inc(acc_free, 1)
                return
            with act.If(n == ITERS - 1):
                act.wait_ge(a_out[NBUF - 1], u0 + ITERS)
                for k in range(4):
                    act.activation(OT[:, k * BANK:(k + 1) * BANK], bank(k), func, **kw).then_inc(acc_free, 1)
            with act.Else():
                pass

        @block.scalar
        def _(act):
            ms = Run()

            def misc(n=BANK):
                ms.n += 1
                act.wait_ge(ms_full, ms.n)
                return bank(4 + (ms.n - 1) % 4, n)

            act.wait_ge(consts, 14)
            act.sem_inc(y_act, 1)

            def unit_chunk(w, s, it):
                act.wait_ge(y_done, 8 * it + (4 * w + s + 1))
                settled(act)
                if s == 0:
                    act.wait_ge(s_st[w][0], 16 * it)
                    settled(act)
                act.activation(SB[:, w, 0, s * BANK:(s + 1) * BANK], bank(4 + s % 2), ACT.Relu,
                               bias=cols[:, 7:8], saturate=False).then_inc(y_act, 1)

            def keep_cand(w, it, h, j):
                act.wait_ge(m8_done, 8 * it + (4 * w + 5))
                dst = cand.rearrange("p (h t) j e -> p h t j e", h=2)
                act.activation(dst[:, ds(h, 1), :, ds(j, 1), :], m8[:, w, :, :].unsqueeze(1), ACT.Copy)\
                    .then_inc(c_cp[w], 1)

            def evacuate(n_half, func, **kw):
                with act.Fori(0, 2) as h:
                    if n_half[2] is not None:
                        p = n_half[2]
                        with act.Fori(0, ITERS) as k:
                            it = act.snap(h * ITERS + k + 2 * ITERS * p)
                            first = act.snap((h * 16 + k * 8) % NT, max_val=NT - 8)
                            jb = [act.snap(first + 2 * ((2 * w) ^ swapped(p)) + p % 2) for w in range(2)]
                            for w in range(2):
                                for s in range(4):
                                    unit_chunk(w, s, it)
                                    if w == 1 and s == 1:
                                        keep_cand(0, it, h, jb[0])
                            keep_cand(1, it, h, jb[1])
                    act.wait_ge(a_out[NBUF - 1], n_half[0] + ITERS + ITERS * h)
                    for k in range(4):
                        act.activation(OT[:, ds(h * HALF + k * BANK, BANK)], bank(k), func, **kw)\
                            .then_inc(acc_free, 1)

            def to_v(v, scale=None, last=True):
                for g in range(8):
                    m = misc()
                    if scale is None:
                        act.activation(v[:, 4 * g:4 * g + 4, :], m.rearrange("p (t c) -> p t c", c=P),
                                       ACT.Copy).then_inc(ms_free, 1)
                    else:
                        for k in range(4):
                            t = 4 * g + k
                            ins = act.activation(v[:, t, :], m[:, k * P:(k + 1) * P], ACT.Copy,
                                                 scale=scale[:, t:t + 1])
                        ins.then_inc(ms_free, 1)
                act.wait_ge(ms_free, ms.n)
                act.sem_inc(v_ready, 1)

            to_v(v_of(0))
            for p in range(4):
                evacuate((2 * ITERS * p, 0, p), ACT.Relu if p == 1 else ACT.Copy)
                act.wait_ge(acc_free, 8 * (p + 1))
                act.sem_inc(ot_ready, 8)
                if p == 0:
                    to_v(v_of(1), fcol[:, 0, :])
                elif p == 1:
                    to_v(v_of(2))
                elif p == 2:
                    to_v(v_of(3), fcol[:, 1, :])
            act.wait_ge(ln_var, 1)
            act.activation(rstd[:, 0, :], rstd[:, 0, :], ACT.Sqrt).then_inc(ln_std, 1)
            if upto == 0:
                return

            def std(n, slot=0):
                act.wait_ge(ln_var, n)
                act.activation(rstd[:, slot, :], rstd[:, slot, :], ACT.Sqrt).then_inc(ln_std, 1)

            def turned(dst, scale, bias):
                for g in range(8):
                    m = misc()
                    act.activation(dst[:, g * BANK:(g + 1) * BANK], m, ACT.Identity, scale=scale, bias=bias)\
                        .then_inc(ms_free, 1)
                act.wait_ge(ms_free, ms.n)

            std(2)
            ms.n += 8
            turned(OT, cols[:, 0:1], cols[:, 1:2])
            act.sem_inc(ot_ready, 1)
            m = misc(4)
            act.activation(RH[:, 2 * P + 1:2 * P + 5], m, ACT.Copy).then_inc(ms_free, 1)
            act.wait_ge(ms_free, ms.n)
            act.sem_inc(sr_made, 1)
            for t in range(NT):
                m = misc(HW)
                act.activation(Hs[:, t, :], m, ACT.Copy).then_inc(ms_free, 1)
            act.wait_ge(ms_free, ms.n)
            act.sem_inc(h_made, 1)
            ms.n += 1
            with act.Fori(0, 4) as q:
                act.wait_ge(b_made, 2 * q + 2)
                for s in range(32):
                    j = act.snap((8 * q + s) % NT, max_val=NT - 1)
                    if s < 2:
                        act.wait_ge(p_used, 64 * q)
                    else:
                        act.wait_ge(p_used, 64 * q + 2 * (s - 1))
                    for k in range(2):
                        act.activation(QA[:, s % 2, k, :], Bx[:, k, 0, :], ACT.Exp,
                                       bias=Hs[:, ds(j, 1), 2 * P + 2 + 2 * k:2 * P + 3 + 2 * k].squeeze(1))
                        act.activation(QB[:, s % 2, k, :], Bx[:, k, 1, :], ACT.Exp,
                                       bias=dst2[:, ds(j, 1), k:k + 1].squeeze(1)).then_inc(q_made, 1)
            for k in range(2):
                std(3 + k, k)
            for k in range(2):
                turned(QT[:, k, :], cols[:, 2:3], cols[:, 3:4])
                act.sem_inc(qt_made, 1)
            for g in range(16):
                act.wait_ge(e_neg, g + 1)
                act.activation(e_t[:, g % 4, :], e_t[:, g % 4, :], ACT.Exp).then_inc(e_exp, 1)
            ms.n += 16
            std(5)
            if upto == 1:
                return

            for g in range(8):
                m = misc()
                act.activation(OT[:, g * BANK:(g + 1) * BANK], m, ACT.Copy).then_inc(ms_free, 1)
            act.wait_ge(ms_free, ms.n)
            act.sem_inc(ot_ready, 1)
            ms.n += 8
            act.wait_ge(inv_made, 1)

            def guess(k, n, step):
                b, jj = k // 2, k % 2
                if step == 0:
                    act.wait_ge(a_in[b], 16 * n + 16 * (USES_L2 + A_L1 + 1))
                    act.wait_ge(a_out[b], n + USES_L2)
                    act.activation(U[:, k, :], A[b][:, jj * HALF:(jj + 1) * HALF], ACT.Ln, bias=cols[:, 13:14])\
                        .then_inc(lnr, 1)
                else:
                    act.wait_ge(lnr, 8 * n + (k + 1))
                    act.activation(U[:, k, :], U[:, k, :], ACT.Exp, scale=-1.0).then_inc(u_made, 1)

            def weight(k, n, step):
                if step == 0:
                    act.wait_ge(n_made, 8 * n + (k + 2))
                    act.activation(U[:, k, :], U[:, k, :], ACT.Square, scale=cols[:, 11:12], bias=cols[:, 12:13])\
                        .then_inc(sq_made, 1)
                else:
                    act.wait_ge(sq_made, 8 * n + (k + 1))
                    act.activation(U[:, k, :], U[:, k, :], ACT.Exp, scale=-1.0).then_inc(e_made, 1)

            def l2_units(n, last):
                for k in range(8):
                    ahead = (k + 2) % 8
                    more = not last or k + 2 < 8
                    nn = n if k + 2 < 8 else n + 1
                    for step in range(2):
                        if more:
                            guess(ahead, nn, step)
                        weight(k, n, step)

            for k in range(2):
                for step in range(2):
                    guess(k, 0, step)
            with act.Fori(0, 2 * ITERS - 1) as n:
                l2_units(n, False)
                half_out(act, n, USES_L2, ACT.Copy)
            l2_units(2 * ITERS - 1, True)
            half_out(act, 2 * ITERS - 1, USES_L2, ACT.Copy)
            act.wait_ge(acc_free, 40)
            act.sem_inc(ot_ready, 8)
            ms.n += 8
            std(6)
            if upto == 2:
                return

            for g in range(8):
                m = misc()
                act.activation(OT[:, g * BANK:(g + 1) * BANK], m, ACT.Copy).then_inc(ms_free, 1)
            act.wait_ge(ms_free, ms.n)
            act.sem_inc(ot_ready, 1)
            to_v(V[:, :, :])
            evacuate((USES_L3, 0, None), ACT.Relu, bias=cols[:, 4:5])
            act.wait_ge(acc_free, 48)
            act.sem_inc(ot_ready, 8)
            to_v(V[:, :, :])
            act.activation(OP[:, 0, :, :], V[:, :, :], ACT.Copy).then_inc(part_a, 1)
            r1v = r1.rearrange("p (t c) -> p t c", c=P)
            act.wait_ge(part_d, 1)
            act.activation(OP[:, 1, :, :], r1v, ACT.Copy).then_inc(part_a, 1)
            act.wait_ge(part_d, 2)
            act.activation(OP[:, 2, :, :], r1v, ACT.Copy).then_inc(part_a, 1)
            std(7)
        @block.vector
        def _(dve):
            own = Run()
            ms = Run()
            lns = Run()

            def did(ins):
                own.n += 1
                ins.then_inc(dv, 1)
                return own.n

            def after(n):
                dve.wait_ge(dv, n)

            dve.wait_ge(consts, 14)
            dve.sem_inc(m8_done, 1)

            def unit(w, it):
                dve.wait_ge(a_in[2 * w], 16 * it + 16)
                a = A[2 * w][:, :]
                jj = unit.p % 2
                a = a[:, jj * HALF:(jj + 1) * HALF]
                dve.tensor_scalar(Mk[:, w, :], a, 0.0, cols[:, 6:7], ALU.not_equal, ALU.mult)
                dve.tensor_scalar(M01[:, w, :], a, 0.0, None, ALU.not_equal).then_inc(mk[w], 1)
                dve.wait_ge(s_st[w][1], 16 * it)
                dve.wait_ge(c_cp[w], it)
                dve.wait_ge(mk[w], it + 1)
                for s in range(5):
                    g = 8 * it + (4 * w + s)
                    if s < 4:
                        dve.wait_ge(y_act, g + 2)
                        settled(dve)
                        y = bank(4 + s % 2)
                        dve.tensor_scalar(SB[:, w, 1, s * BANK:(s + 1) * BANK], y, RANK - 1, None,
                                          ALU.is_equal, saturate=False)
                        dve.scalar_tensor_tensor(out=Kb[:, s % 2, :], in0=y, scalar=RANK - 1.5,
                                                 in1=Mk[:, w, s * BANK:(s + 1) * BANK],
                                                 op0=ALU.is_lt, op1=ALU.mult).then_inc(k_made, 1)
                    if s > 0:
                        dve.wait_ge(t_done, g)
                        settled(dve)
                        half = (s - 1) % 2
                        tb = bank(6 + half).bitcast(BF16)[:, 0:BANK]
                        for k in range(4):
                            last = dve.max(m8[:, w, 4 * (s - 1) + k, :], tb[:, k * P:(k + 1) * P])
                        last.then_inc(m8_done, 1)

            for p in range(4):
                unit.p = p
                with dve.Fori(2 * ITERS * p, 2 * ITERS * (p + 1)) as it:
                    unit(0, it)
                    unit(1, it)

            def norm(src, slot, tiles=NT):
                last = 0
                for t in range(tiles):
                    last = did(dve.bn_stats(st6[:, slot, t, :], src[:, t, :]))
                after(last)
                for t in range(tiles):
                    last = did(dve.bn_aggr(mv[:, slot, t, :], st6[:, slot, t, :]))
                after(last)
                dve.tensor_scalar(rstd[:, slot, :], mv[:, slot, :, 1], EPS, None, ALU.add).then_inc(ln_var, 1)
                lns.n += 1
                dve.wait_ge(ln_std, lns.n)
                after(did(dve.reciprocal(rstd[:, slot, :], rstd[:, slot, :])))
                for t in range(tiles):
                    last = did(dve.tensor_scalar(src[:, t, :], src[:, t, :], mv[:, slot, t, 0:1],
                                                 rstd[:, slot, t:t + 1], ALU.subtract, ALU.mult))
                after(last)

            def elu_end(dve, g, own, did, after):
                dve.wait_ge(e_exp, g + 1)
                dve.wait_ge(ms_free, 8 * 6 + 1 + NT + 1 + 16 + g + 1)
                e = e_t[:, g % 4, :]
                after(did(dve.scalar_tensor_tensor(out=e, in0=e, scalar=-1.0, in1=r_t[:, g % 4, :],
                                                   op0=ALU.add, op1=ALU.add)))
                v = V[:, 4 * (g % 8):4 * (g % 8) + 4, :]
                xx = X[:, 4 * (g % 8):4 * (g % 8) + 4, :]
                e = e.rearrange("p (t c) -> p t c", c=P)
                after(did(dve.scalar_tensor_tensor(out=xx, in0=e, scalar=0.5, in1=xx, op0=ALU.mult, op1=ALU.add)))

            def add_misc(n0):
                for g in range(8):
                    dve.wait_ge(ms_full, n0 + g + 1)
                    m = bank(4 + (n0 + g) % 4).rearrange("p (t c) -> p t c", c=P)
                    dve.tensor_tensor(X[:, 4 * g:4 * g + 4, :], X[:, 4 * g:4 * g + 4, :], m, ALU.add)\
                        .then_inc(ms_free, 1)
                dve.wait_ge(ms_free, n0 + 8)

            dve.wait_ge(x_in, 32)
            add_misc(32)
            norm(X, 0)
            dve.sem_inc(x_ready, 1)
            if upto == 0:
                return

            def norm_to(dst, src, slot):
                last = 0
                for t in range(NT):
                    last = did(dve.bn_stats(st6[:, slot, t, :], src[:, t, :]))
                after(last)
                for t in range(NT):
                    last = did(dve.bn_aggr(mv[:, slot, t, :], st6[:, slot, t, :]))
                after(last)
                dve.tensor_scalar(rstd[:, slot, :], mv[:, slot, :, 1], EPS, None, ALU.add).then_inc(ln_var, 1)
                lns.n += 1
                dve.wait_ge(ln_std, lns.n)
                after(did(dve.reciprocal(rstd[:, slot, :], rstd[:, slot, :])))
                for t in range(NT):
                    last = did(dve.tensor_scalar(dst[:, t, :], src[:, t, :], mv[:, slot, t, 0:1],
                                                 rstd[:, slot, t:t + 1], ALU.subtract, ALU.mult))
                after(last)

            after(did(dve.memset(RH[:, P:P + 1], 0.0)))
            norm_to(V, X, 0)
            dve.sem_inc(v_ready, 1)
            dve.wait_ge(sr_made, 1)
            after(did(dve.memset(SRt[:, :, :], 1.0)))
            for k in range(2):
                last = did(dve.tensor_scalar(SRt[:, k, :], SRt[:, k, :], RH[:, 2 * P + 1 + 2 * k:2 * P + 2 + 2 * k],
                                             None, ALU.mult))
            after(last)
            dve.wait_ge(h_made, 1)
            dsts = Hs[:, :, 2 * P + 2:2 * P + 5:2].rearrange("p t k -> p k t")
            did(dve.memset(Hs[:, :, P:P + 1], 1.0))
            did(dve.tensor_scalar(dst2.rearrange("p t k -> p k t"), dsts, 0.01, None, ALU.mult))
            did(dve.tensor_reduce(ext[:, 0:2], dsts, AX.X, ALU.max))
            after(did(dve.tensor_reduce(ext[:, 2:4], dsts, AX.X, ALU.min)))
            dve.tensor_scalar(ext[:, 2:4], ext[:, 2:4], -1.0, None, ALU.mult).then_inc(ext_made, 1)
            dve.wait_ge(ext_all, 1)
            after(did(dve.tensor_tensor(ext[:, 8:10], ext[:, 4:6], ext[:, 6:8], ALU.add)))
            after(did(dve.tensor_reduce(ext[:, 10:11], ext[:, 8:10], AX.X, ALU.max)))
            dve.tensor_scalar(ext[:, 12:13].bitcast(I32), ext[:, 10:11], spread, None, ALU.is_gt)\
                .then_inc(flag_made, 1)
            after(did(dve.memset(MX[:, :, :], 0.0)))
            for k in range(2):
                last = did(dve.tensor_scalar(MX[:, k, :], MX[:, k, :], ext[:, 4 + k:5 + k], None, ALU.add))
            after(last)
            dve.wait_ge(flag_made, 1)
            flag = dve.value_load(ext[0:1, 12:13].bitcast(I32), min_val=0, max_val=1)
            with dve.If(flag > 0):
                dve.wait_ge(gen_in, 16 * 4)
                for k in range(2):
                    dve.tensor_scalar(A[1 + k][:, :], A[1 + k][:, :], ext[:, 6 + k:7 + k], None, ALU.add)\
                        .then_inc(gen_own, 1)
                dve.wait_ge(gen_own, 2)
                with dve.Fori(0, NT) as t:
                    dve.wait_ge(gen_row, 16 * t + 16)
                    for k in range(2):
                        c = 2 + t * 6 + 3 * k
                        dve.scalar_tensor_tensor(out=A[3][:, :], in0=A[0][:, :], scalar=0.0, in1=A[1 + k][:, :],
                                                 op0=ALU.is_gt, op1=ALU.mult).then_inc(gen_own, 1)
                        dve.wait_ge(gen_own, c + 1)
                        dve.tensor_reduce(ext[:, 13:14], A[3][:, :], AX.X, ALU.max).then_inc(gen_own, 1)
                        dve.wait_ge(gen_own, c + 2)
                        ins = dve.scalar_tensor_tensor(out=MX[:, k, ds(t, 1)], in0=ext[:, 13:14],
                                                       scalar=ext[:, 6 + k:7 + k],
                                                       in1=Hs[:, ds(t, 1), 2 * P + 2 + 2 * k:2 * P + 3 + 2 * k].squeeze(1),
                                                       op0=ALU.subtract, op1=ALU.max).then_inc(gen_own, 1)
                        dve.wait_ge(gen_own, c + 3)
                    dve.sem_inc(gen_used, 1)
            with dve.Else():
                pass
            dve.sem_inc(mx_made, 1)
            n_m = 8 * 6 + 1 + NT
            dve.wait_ge(ms_full, n_m + 1)
            dve.tensor_copy(MXT[0:2 * NT, :], bank(4 + n_m % 4)[0:2 * NT, 0:P]).then_inc(ms_free, 1)
            dve.wait_ge(ms_free, n_m + 1)
            dve.sem_inc(mxt_made, 1)

            def region_of(k, it):
                r = 8 * k + it
                return PS[:, (r // 3) * BANK + (r % 3) * (P + 1):(r // 3) * BANK + (r % 3 + 1) * (P + 1)]

            OTr = OT[:, :].rearrange("p (t c) -> p t c", c=P)
            with dve.Fori(0, 4) as q:
                dve.wait_ge(smax_in, 32 * q + 32)
                for k in range(2):
                    dve.wait_ge(src_full, 2 * q + (k + 1))
                    src = PS[:, 6 * BANK:8 * BANK]
                    b1_, b2_ = Bx[:, k, 0, :], Bx[:, k, 1, :]
                    dve.tensor_tensor(b1_, src, b2_, ALU.add).then_inc(ch, 1)
                    dve.wait_ge(ch, 14 * q + (3 * k + 1))
                    dve.scalar_tensor_tensor(out=b2_, in0=b1_, scalar=0.01, in1=b1_, op0=ALU.mult, op1=ALU.max)\
                        .then_inc(ch, 1)
                    dve.wait_ge(ch, 14 * q + (3 * k + 2))
                    dve.tensor_tensor(b1_, src, b2_, ALU.subtract).then_inc(ch, 1)
                    dve.scalar_tensor_tensor(out=b2_, in0=src, scalar=0.01, in1=b2_, op0=ALU.mult,
                                             op1=ALU.subtract).then_inc(b_made, 1)
                    dve.wait_ge(ch, 14 * q + (3 * k + 3))
                    dve.wait_ge(b_made, 2 * q + (k + 1))
                    dve.sem_inc(src_used, 1)
                for s in range(32):
                    b, w = (s // 4) % NBUF, s % 2
                    if s % 4 == 0:
                        dve.wait_ge(a_in[b], 16 * (USES_L2 + s // 16 + 1) + 32 * q)
                    a = A[b][:, (s % 4) * QC:(s % 4 + 1) * QC]
                    dve.tensor_scalar(Mt[:, w, :], a, 0.0, None, ALU.is_gt).then_inc(mask_made, 1)
                    dve.wait_ge(mask_made, 32 * q + (s + 1))
                    if s < 8:
                        d = Mt[:, w, s * P:(s + 1) * P]
                        dve.tensor_tensor(d, d, identb[:, :], ALU.max).then_inc(ch, 1)
                        dve.wait_ge(ch, 14 * q + (7 + s))
                    for k in range(2):
                        dve.wait_ge(q_made, 64 * q + (2 * s + k + 1))
                        dve.tensor_tensor(QA[:, w, k, :], QA[:, w, k, :], QB[:, w, k, :], ALU.max)\
                            .then_inc(r_made, 1)
                    for k in range(2):
                        dve.wait_ge(r_made, 64 * q + (2 * s + k + 1))
                        dve.scalar_tensor_tensor(out=QA[:, w, k, :], in0=QA[:, w, k, :], scalar=1.0,
                                                 in1=Mt[:, w, :], op0=ALU.min, op1=ALU.mult).then_inc(p_made, 1)
                dve.wait_ge(p_used, 64 * q + 64)
                for k in range(2):
                    for it in range(8):
                        r = region_of(k, it)
                        dve.reciprocal(rden[:, 8 * k + it:8 * k + it + 1], r[:, P:P + 1] if k == 0 else r[:, 0:1])\
                            .then_inc(rd_made, 1)
                for k in range(2):
                    for it in range(8):
                        r = region_of(k, it)
                        dve.wait_ge(rd_made, 16 * q + (8 * k + it + 1))
                        dst = V if k == 0 else OTr
                        dve.scalar_tensor_tensor(out=dst[:, ds(8 * q + it, 1), :].squeeze(1),
                                                 in0=r[:, 0:P] if k == 0 else r[:, 1:P + 1],
                                                 scalar=rden[:, 8 * k + it:8 * k + it + 1],
                                                 in1=X[:, ds(8 * q + it, 1), :].squeeze(1),
                                                 op0=ALU.mult, op1=ALU.add).then_inc(att_out, 1)
                dve.wait_ge(att_out, 16 * q + 16)
            norm_to(V, V, 0)
            dve.sem_inc(att_done, 1)
            norm_to(OTr, OTr, 1)
            dve.sem_inc(att_done, 1)
            n_m += 1 + 16
            for g in range(16):
                m = bank(4 + (n_m + g) % 4)
                if g >= 4:
                    dve.wait_ge(e_exp, g - 3)
                dve.wait_ge(ms_full, n_m + g + 1)
                dve.tensor_scalar(e_t[:, g % 4, :], m, 0.0, None, ALU.min).then_inc(e_neg, 1)
                dve.tensor_scalar(r_t[:, g % 4, :], m, 0.0, None, ALU.max).then_inc(ms_free, 1)
                if g >= 1:
                    elu_end(dve, g - 1, own, did, after)
            elu_end(dve, 15, own, did, after)
            norm(X, 0)
            dve.sem_inc(x_ready, 1)
            if upto == 1:
                return

            dve.sem_inc(n_made, 1)
            did(dve.reciprocal(cols[:, 10:11], cols[:, 8:9]))
            after(did(dve.reciprocal(cols[:, 11:12], cols[:, 9:10])))
            after(did(dve.tensor_scalar(cols[:, 11:12], cols[:, 11:12], -(0.5 ** 0.5), None, ALU.mult)))
            after(did(dve.tensor_tensor(cols[:, 12:13], cols[:, 10:11], cols[:, 11:12], ALU.mult)))
            dve.sem_inc(inv_made, 1)
            dve.wait_ge(l2c_in, 16)
            dve.wait_ge(dd_made, 1)
            n_m = 114 + 8
            for g in range(8):
                dve.wait_ge(ms_full, n_m + g + 1)
                m = bank(4 + (n_m + g) % 4).rearrange("p (t c) -> p t c", c=P)
                dve.tensor_tensor(V[:, 4 * g:4 * g + 4, :], m, BB.unsqueeze(1).broadcast_to([P, 4, P]), ALU.add)\
                    .then_inc(ms_free, 1)
            dve.wait_ge(ms_free, n_m + 8)
            dve.sem_inc(v_ready, 1)

            def newton(k, n):
                dve.wait_ge(t_made, 8 * n + (k + 1))
                dve.scalar_tensor_tensor(out=U[:, k, :], in0=T[:, k % 2, :], scalar=2.0, in1=U[:, k, :],
                                         op0=ALU.subtract, op1=ALU.mult).then_inc(n_made, 1)

            def mask(k, n):
                b, jj = k // 2, k % 2
                dve.wait_ge(e_made, 8 * n + (k + 1))
                dve.wait_ge(a_in[b], 16 * n + 16 * (USES_L2 + A_L1 + 1))
                dve.scalar_tensor_tensor(out=U[:, k, :], in0=A[b][:, jj * HALF:(jj + 1) * HALF], scalar=0.5,
                                         in1=U[:, k, :], op0=ALU.is_lt, op1=ALU.mult).then_inc(s_own, 1)
                dve.wait_ge(s_own, 8 * n + (k + 1))
                if isinstance(n, int):
                    col, diag = (8 * n + k) % 16 * P, (n % 4) // 2 * P
                    d, dd = U[:, k, col:col + P], DD[:, diag:diag + P]
                else:
                    d = U[:, k, ds(dve.snap((n * 8 + k) % 16 * P, max_val=15 * P), P)]
                    dd = DD[:, ds(dve.snap((n % 4) // 2 * P, max_val=P), P)]
                dve.tensor_tensor(d, d, dd, ALU.mult).then_inc(s_made, 1)

            newton(0, 0)
            newton(1, 0)
            with dve.Fori(0, 2 * ITERS - 1) as n:
                for k in range(8):
                    newton((k + 2) % 8, n if k + 2 < 8 else n + 1)
                    mask(k, n)
            for k in range(8):
                if k + 2 < 8:
                    newton(k + 2, 2 * ITERS - 1)
                mask(k, 2 * ITERS - 1)
            add_misc(n_m + 8)
            norm(X, 0)
            dve.sem_inc(x_ready, 1)
            if upto == 2:
                return

            own_l = [0]

            def lists(ins, n=None):
                own_l[0] += 1
                ins.then_inc(lw, 1)
                dve.wait_ge(lw, own_l[0] if n is None else n + own_l[0])
                if n is not None:
                    settled(dve)

            dve.wait_ge(cand_in, 16)
            dve.wait_ge(seg_made, 2)
            lists(dve.tensor_reduce(bad[:, 1:2], cand2.rearrange("p t (j e) -> p (t j) e", e=8)[:, :, 7], AX.X, ALU.max))
            lists(dve.memset(bad[:, 2:3], 0.0))
            base = own_l[0]
            STEPS = 9
            with dve.Fori(0, NT) as t:
                own_l[0] = base
                at_ = t * STEPS
                c = cand2[:, ds(t, 1), :].squeeze(1)
                lists(dve.scalar_tensor_tensor(out=K1, in0=c, scalar=0.0, in1=segb, op0=ALU.is_gt, op1=ALU.mult), at_)
                lists(dve.tensor_tensor(K1, K1, c, ALU.add), at_)
                lists(dve.max(m8x[:, 0:8], K1), at_)
                lists(dve.match_replace(out=K2, in_to_replace=m8x[:, 0:8], in_values=K1, imm_value=0.0), at_)
                lists(dve.max(m8x[:, 8:16], K2), at_)
                lists(dve.match_replace(out=K1, in_to_replace=m8x[:, 8:16], in_values=K2, imm_value=0.0), at_)
                lists(dve.max(m8x[:, 16:24], K1), at_)
                lists(dve.tensor_copy(LST[:, ds(t, 1), :].squeeze(1), m8x[:, 0:REST]), at_)
                lists(dve.tensor_tensor(bad[:, 2:3], bad[:, 2:3], m8x[:, REST:REST + 1], ALU.max), at_)
            own_l[0] = base + STEPS * NT
            flat = LST.rearrange("p t e -> p (t e)")
            tmp = r1[:, 0:NT * REST]
            lists(dve.tensor_scalar(tmp, flat, 0.0, float(N + 1), ALU.is_equal, ALU.mult))
            dve.scalar_tensor_tensor(out=IDX.rearrange("p t e -> p (t e)"), in0=flat, scalar=-1.0, in1=tmp,
                                     op0=ALU.add, op1=ALU.add).then_inc(idx_made, 1)
            dve.memset(K1[:, 0:P], 0.0).then_inc(zero_made, 1)

            dve.wait_ge(v_ready, 8)
            dve.wait_ge(idx_made, 1)
            dve.wait_ge(part_a, 1)
            Vf = V[:, :, :].rearrange("p t c -> p (t c)")
            dve.tensor_tensor(r1, Vf, OP[:, 0, :, :].rearrange("p t c -> p (t c)"), ALU.subtract).then_inc(part_d, 1)
            dve.wait_ge(part_d, 1)
            dve.wait_ge(part_a, 2)
            dve.tensor_tensor(r1, r1, OP[:, 1, :, :].rearrange("p t c -> p (t c)"), ALU.subtract).then_inc(part_d, 1)
            dve.wait_ge(tab_out, 32)
            dve.wait_ge(ot_ready, 51)
            dve.wait_ge(v_ready, 8)
            after(did(dve.memset(OT[:, :], 0.0)))
            dve.sem_inc(px_free, 2)
            with dve.Fori(0, 2 * ITERS) as n:
                half = OT[:, ds(n // ITERS * HALF, HALF)]
                for g in range(NGRP):
                    b = g // (2 * SLOTS)
                    full = 2 * SLOTS - 1
                    if g % (2 * SLOTS) == full:
                        dve.wait_ge(a_out[b], n + (USES_POOL + 1))
                    else:
                        dve.wait_ge(px_full, n * (NBUF * full) + (b * full + g % (2 * SLOTS) + 1))
                    dve.wait_ge(px_free, NGRP * n + (g + 2))
                    src = PS[:, 4 * (g % 2) * BANK:(4 * (g % 2) + 4) * BANK]
                    dve.tensor_tensor(half, half, src, ALU.max).then_inc(px_free, 1)
                    if g % 4 == 3:
                        w = g // 4 % 2
                        r = 2 * n + g // 8
                        dve.wait_ge(g_in[w], 16 * REST * (r + 1))
                        dve.tensor_reduce(V[:, ds(4 * n + g // 4, 1), :].squeeze(1),
                                          G[:, w, :, :].rearrange("p k c -> p c k"), AX.X, ALU.max)\
                            .then_inc(g_used[w], 1)
            dve.wait_ge(px_free, NGRP * 2 * ITERS + 2)
            for w in range(2):
                dve.wait_ge(g_used[w], NT // 2)
            dve.sem_inc(x_ready, 1)
            n_m = 162
            for g in range(8):
                dve.wait_ge(ms_full, n_m + g + 1)
                m = bank(4 + (n_m + g) % 4).rearrange("p (t c) -> p t c", c=P)
                dve.tensor_tensor(V[:, 4 * g:4 * g + 4, :], V[:, 4 * g:4 * g + 4, :], m, ALU.max)\
                    .then_inc(ms_free, 1)
            dve.wait_ge(ms_free, n_m + 8)
            after(did(dve.tensor_reduce(rowm, V[:, :, :], AX.X, ALU.max)))
            after(did(dve.tensor_reduce(bad[:, 3:4], rowm, AX.X, ALU.min)))
            after(did(dve.tensor_scalar(bad[:, 3:4], bad[:, 3:4], 0.0, None, ALU.is_equal)))
            after(did(dve.tensor_reduce(bad[:, 0:1], bad[:, 1:4], AX.X, ALU.max)))
            dve.sem_inc(bad_made, 1)
            dve.wait_ge(bad_all, 1)
            dve.tensor_scalar(bad[:, 8:9].bitcast(I32), bad[:, 4:5], limit, None, ALU.is_gt).then_inc(flag2, 1)
            dve.wait_ge(flag2, 1)
            flag = dve.value_load(bad[0:1, 8:9].bitcast(I32), min_val=0, max_val=1)
            with dve.If(flag > 0):
                tmpv = A[2][:, :].rearrange("p (c j) -> p c j", j=32)
                part = A[3][:, 0:P]
                msk = A[3][:, P:P + 32]
                has = A[3][:, 2 * P:2 * P + 1]
                hc = A[3][:, 2 * P + 1:2 * P + 2]
                with dve.Fori(0, NT) as t:
                    v = V[:, ds(t, 1), :].squeeze(1)
                    t0 = t * (5 * 4 * NT + 4)
                    dve.tensor_copy(v, K1[:, 0:P]).then_inc(dn, 1)
                    dve.memset(has, 0.0).then_inc(dn, 1)
                    with dve.Fori(0, 4 * NT) as c:
                        c0 = t0 + c * 5
                        dve.wait_ge(dn, t0 + 2)
                        dve.wait_ge(dn_in, 32 * (t * (4 * NT) + c + 1))
                        dve.tensor_scalar(msk, A[1][:, 0:32], 0.0, None, ALU.not_equal).then_inc(dn, 1)
                        dve.wait_ge(dn, c0 + 3)
                        dve.tensor_tensor(tmpv, A[0][:, :].rearrange("p (j c) -> p c j", c=P),
                                          msk.unsqueeze(1).broadcast_to([P, P, 32]), ALU.mult).then_inc(dn, 1)
                        dve.tensor_reduce(hc, msk, AX.X, ALU.max).then_inc(dn, 1)
                        dve.wait_ge(dn, c0 + 5)
                        dve.sem_inc(dn_used, 2)
                        dve.tensor_reduce(part, tmpv, AX.X, ALU.max).then_inc(dn, 1)
                        dve.tensor_tensor(has, has, hc, ALU.max).then_inc(dn, 1)
                        dve.wait_ge(dn, c0 + 7)
                        dve.tensor_tensor(v, v, part, ALU.max).then_inc(dnv, 1)
                        dve.wait_ge(dnv, t * (4 * NT) + c + 1)
                    t1 = t0 + 5 * 4 * NT
                    dve.tensor_scalar(has, has, -1.0, BIG, ALU.add, ALU.mult).then_inc(dn, 1)
                    dve.wait_ge(dn, t1 + 3)
                    dve.tensor_scalar(v, v, has, None, ALU.add).then_inc(dn, 1)
                    dve.wait_ge(dn, t1 + 4)
            with dve.Else():
                pass
            after(did(dve.tensor_tensor(X[:, :, :], X[:, :, :], V[:, :, :], ALU.add)))
            norm(X, 0)
            dve.sem_inc(x_ready, 1)


_INS = ["x", "xT", "adj", "adjT", "W1", "f1", "W2", "f2", "ff0", "ff0T", "ff1T", "attc", "g1", "b1", "g2", "b2",
        "L2W", "L2B", "mu", "sigma", "L3W", "L3b"]


def laid_out(x, adj, L0_gnn_W1, L0_gnn_f1, L0_gnn_W2, L0_gnn_f2, L1_gnn_ff0_w, L1_gnn_ff1_w, L1_gnn_attn_w,
             L1_gnn_g1, L1_gnn_b1, L1_gnn_g2, L1_gnn_b2, L2_gnn_W, L2_gnn_B, L2_gnn_mu, L2_gnn_sigma,
             L3_gnn_weight, L3_gnn_bias):
    import numpy as np

    def a(v):
        return np.asarray(v)

    return {
        "x": a(x), "xT": a(x).T, "adj": a(adj), "adjT": a(adj).T,
        "W1": a(L0_gnn_W1), "f1": a(L0_gnn_f1).reshape(NT, P).T, "W2": a(L0_gnn_W2),
        "f2": a(L0_gnn_f2).reshape(NT, P).T,
        "ff0": a(L1_gnn_ff0_w), "ff0T": a(L1_gnn_ff0_w).transpose(0, 2, 1),
        "ff1T": a(L1_gnn_ff1_w).transpose(0, 2, 1),
        "attc": a(L1_gnn_attn_w).reshape(4, P).T,
        "g1": a(L1_gnn_g1).reshape(P, 1), "b1": a(L1_gnn_b1).reshape(P, 1),
        "g2": a(L1_gnn_g2).reshape(P, 1), "b2": a(L1_gnn_b2).reshape(P, 1),
        "L2W": a(L2_gnn_W), "L2B": a(L2_gnn_B).reshape(1, P),
        "mu": a(L2_gnn_mu), "sigma": a(L2_gnn_sigma),
        "L3W": a(L3_gnn_weight), "L3b": a(L3_gnn_bias).reshape(P, 1),
    }


def kernel(**inputs):
    import numpy as np
    import concourse.bacc as bacc
    from concourse.bass_utils import run_bass_kernel_spmd as run

    nc = bacc.Bacc("TRN2", target_bir_lowering=False, num_devices=1)
    arrays, args = {}, []
    for name, v in laid_out(**inputs).items():
        arrays[f"in_{name}"] = np.ascontiguousarray(v)
        args.append(nc.dram_tensor(f"in_{name}", v.shape, mybir.dt.from_np(v.dtype), kind="ExternalInput").ap())
    args.append(nc.dram_tensor("out", (N, P), F32, kind="ExternalOutput").ap())
    program(nc, *args)
    r = run(nc, [arrays], core_ids=[0])
    return r.results[0]["out"]
```

```python
from contextlib import ExitStack

import concourse.bass as bass
from concourse import mybir

P = 128
N = 4096
NT = N // P
HALF = N // 2
BANK = 512
NBUF = 4
ITERS = HALF // BANK
SLOTS = 2
REST = 16
SPARE = 8
STEP = 2
QC = 1024
RANK = 200.0
DVE_SQUARES = (0, 2, 4, 6)
SPREAD = 60.0
EPS = 1e-5
BIG = 3.4028234663852886e38
TINY = 1e-15

F32 = mybir.dt.float32
BF16 = mybir.dt.bfloat16
FP8 = mybir.dt.float8e4
I32 = mybir.dt.int32
U32 = mybir.dt.uint32
ALU = mybir.AluOpType
ACT = mybir.ActivationFunctionType
AX = mybir.AxisListType
RMAX = bass.bass_isa.ReduceOp.max
ds = bass.ds

USES_L0 = 0
USES_L2 = 4 * 2 * ITERS
USES_L3 = USES_L2 + 2 * ITERS
USES_POOL = USES_L3 + 2 * ITERS
L1_LOADS = 4 * 8


def program(nc, x, xT, adj, adjT, W1, f1, W2, f2, ff0, ff0T, ff1T, attc, g1, b1, g2, b2,
            L2W, L2B, mu, sigma, L3W, L3b, out, upto=9, spread=SPREAD, limit=0.0):
    with ExitStack() as ctx:
        def sb(name, shape, dt=F32):
            return ctx.enter_context(nc.sbuf_tensor(name, shape, dt))

        def sem(name):
            return ctx.enter_context(nc.semaphore(name))

        onehot_d = nc.dram_tensor("onehot_d", (SLOTS * NT * 2 * P, HALF // 4), F32, kind="Internal").ap()
        cand_d = nc.dram_tensor("cand_d", (P, NT * NT * 8), BF16, kind="Internal").ap()
        smax_d = nc.dram_tensor("smax_d", (2 * NT, P), F32, kind="Internal").ap()
        table_d = nc.dram_tensor("table_d", (N + P, P), F32, kind="Internal").ap()

        A = [sb(f"A{b}", [P, N]) for b in range(NBUF)]
        X = sb("X", [P, NT, P])
        V = sb("V", [P, NT, P])
        OT = sb("OT", [P, N])
        VS = sb("VS", [P, NBUF, 2, P])
        ident = sb("ident", [P, P])
        notid = sb("notid", [P, P])
        identb = sb("identb", [P, P], BF16)
        rankw = sb("rankw", [P, P], BF16)
        Wt = sb("Wt", [P, 4, P])
        RH = sb("RH", [P, 2 * P + 5])
        ff1s = sb("ff1s", [P, 2, P])
        cols = sb("cols", [P, 16])
        SRt = sb("SRt", [P, 2, P])
        fcol = sb("fcol", [P, 2, NT])
        st6 = sb("st6", [P, 2, NT, 6])
        mv = sb("mv", [P, 2, NT, 2])
        rstd = sb("rstd", [P, 2, NT])
        REGION = 21184
        R = sb("R", [P, REGION])

        def region(at, words, dt=F32):
            v = R[:, at:at + words]
            return v if dt == F32 else v.bitcast(dt)

        PS = ctx.enter_context(nc.psum_tensor("PS", [P, 8 * BANK], F32))
        acc = PS[:, 0:4 * BANK]

        def bank(k, n=BANK):
            return PS[:, k * BANK:k * BANK + n]

        w_in = sem("w_in")
        x_in = sem("x_in")
        consts = sem("consts")
        a_in = [sem(f"a_in{b}") for b in range(NBUF)]
        a_out = [sem(f"a_out{b}") for b in range(NBUF)]
        vs_in = [sem(f"vs_in{b}") for b in range(NBUF)]
        v_ready = sem("v_ready")
        acc_free = sem("acc_free")
        ot_ready = sem("ot_ready")
        ms_full = sem("ms_full")
        ms_free = sem("ms_free")
        mk = [sem(f"mk{w}") for w in range(2)]
        y_done = sem("y_done")
        y_act = sem("y_act")
        k_made = sem("k_made")
        t_done = sem("t_done")
        m8_done = sem("m8_done")
        c_cp = [sem(f"c_cp{w}") for w in range(2)]
        s_st = [[sem(f"s_st{w}{k}") for k in range(2)] for w in range(2)]
        cand_out = sem("cand_out")
        dv = sem("dv")
        ac = sem("ac")
        ln_var = sem("ln_var")
        ln_std = sem("ln_std")
        ln_mean = sem("ln_mean")
        ln_dve = sem("ln_dve")
        ln_act = sem("ln_act")
        x_ready = sem("x_ready")
        out_st = sem("out_st")
        h_made = sem("h_made")
        sr_made = sem("sr_made")
        ext_made = sem("ext_made")
        ext_all = sem("ext_all")
        flag_made = sem("flag_made")
        gen_in = sem("gen_in")
        gen_used = sem("gen_used")
        mx_made = sem("mx_made")
        mxt_made = sem("mxt_made")
        smax_out = sem("smax_out")
        smax_in = sem("smax_in")
        src_full = sem("src_full")
        src_used = sem("src_used")
        b_made = sem("b_made")
        q_made = sem("q_made")
        mask_made = sem("mask_made")
        r_made = sem("r_made")
        p_made = [sem(f"p_made{k}") for k in range(2)]
        p_used = sem("p_used")
        rd_made = sem("rd_made")
        att_out = sem("att_out")
        qt_made = sem("qt_made")
        e_neg = sem("e_neg")
        e_exp = sem("e_exp")
        ch = sem("ch")
        gen_own = sem("gen_own")
        gen_row = sem("gen_row")
        gen_q = sem("gen_q")
        l2c_in = sem("l2c_in")
        dd_made = sem("dd_made")
        lnr = sem("lnr")
        u_made = sem("u_made")
        t_made = sem("t_made")
        n_made = sem("n_made")
        sq_made = sem("sq_made")
        sqd_made = sem("sqd_made")
        sq_own = sem("sq_own")
        e_made = sem("e_made")
        s_own = sem("s_own")
        s_made = sem("s_made")
        inv_made = sem("inv_made")
        cand_in = sem("cand_in")
        seg_made = sem("seg_made")
        lw = sem("lw")
        idx_made = sem("idx_made")
        used_made = sem("used_made")
        o_ready = sem("o_ready")
        zero_made = sem("zero_made")
        tab_out = sem("tab_out")
        part_a = sem("part_a")
        part_d = sem("part_d")
        ix_cp = sem("ix_cp")
        g_in = [sem(f"g_in{w}") for w in range(2)]
        g_more = [sem(f"g_more{w}") for w in range(2)]
        g_seen = [sem(f"g_seen{w}") for w in range(2)]
        g_used = [sem(f"g_used{w}") for w in range(2)]
        px_full = sem("px_full")
        px_free = sem("px_free")
        bad_made = sem("bad_made")
        bad_all = sem("bad_all")
        flag2 = sem("flag2")
        dn_in = sem("dn_in")
        dn_used = sem("dn_used")
        dn = sem("dn")
        dnv = sem("dnv")

        block = ctx.enter_context(nc.Block())

        def settled(engine):
            engine.nop(nofuse=True)

        class Run:
            def __init__(self):
                self.n = 0

        Vb = region(0, 4096).rearrange("p (t c) -> p t c", c=P)
        Mk = region(4096, 2048, BF16).rearrange("p (w n) -> p w n", w=2)
        M01 = region(6144, 2048, BF16).rearrange("p (w n) -> p w n", w=2)
        Kb = region(8192, 512, BF16).rearrange("p (w n) -> p w n", w=2)
        SB = region(8704, 2048, FP8).rearrange("p (w k n) -> p w k n", w=2, k=2)
        SBw = region(8704, 2048).rearrange("p (w k n) -> p w k n", w=2, k=2)
        m8 = region(10752, 128, BF16).rearrange("p (w t e) -> p w t e", w=2, e=8)
        cand = region(10880, 4096, BF16).rearrange("p (t j e) -> p t j e", t=NT, j=NT)
        xT_s = OT

        HW = 2 * P + 5
        Hs = region(0, NT * HW).rearrange("p (t c) -> p t c", c=HW)
        at = NT * HW
        Bx = region(at, 4 * QC).rearrange("p (k e n) -> p k e n", k=2, e=2)
        at += 4 * QC
        QA = region(at, 6 * QC).rearrange("p (w k n) -> p w k n", w=3, k=2)
        QB = region(at + 6 * QC, 2 * QC).rearrange("p (k n) -> p k n", k=2)
        QT = region(at, 8 * QC).rearrange("p (k n) -> p k n", k=2)
        at += 8 * QC
        dst2 = region(at, 2 * NT).rearrange("p (t k) -> p t k", k=2)
        MX = region(at + 2 * NT, 2 * NT).rearrange("p (k t) -> p k t", k=2)
        MXT = region(at + 4 * NT, P)
        ext = region(at + 4 * NT + P, 16)
        at += 4 * NT + P + 16
        attw = region(at, 4)
        rden = region(at + 4, 16)
        assert at + 20 <= REGION
        Mt = VS[:, :, :, :].rearrange("p a b c -> p (a b c)").bitcast(BF16).rearrange("p (w n) -> p w n", w=2)
        SRv = SRt

        U = region(0, 8 * HALF).rearrange("p (w n) -> p w n", w=8)
        T = region(8 * HALF, 2 * HALF).rearrange("p (w n) -> p w n", w=2)
        BB = region(10 * HALF, P)
        DD = region(10 * HALF + P, 2 * P)

        OP = region(0, 3 * NT * P // 2, BF16).rearrange("p (e t c) -> p e t c", e=3, t=NT)
        OPw = region(0, 3 * NT * P // 2).rearrange("p (e t c) -> p e t c", e=3, t=NT)
        HOTW = HALF * SLOTS // 2
        pat = 3 * NT * P // 2
        cand2 = region(pat, 4096, BF16).rearrange("p (t n) -> p t n", t=NT)
        r1 = region(pat + 4096, 4096)
        G = region(pat + 8192, 2 * REST * P).rearrange("p (w k c) -> p w k c", w=2, k=REST)
        pat += 8192 + 2 * REST * P
        LST = region(pat, NT * REST).rearrange("p (t e) -> p t e", e=REST)
        IDX = region(pat + NT * REST, NT * REST, U32).rearrange("p (t e) -> p t e", e=REST)
        pat += 2 * NT * REST
        K1 = region(pat, 256)
        K2 = region(pat + 256, 256)
        segb = region(pat + 512, 256)
        segi = region(pat + 768, 256, I32)
        pat += 1024
        m8x = region(pat, 32)
        ixs = region(pat + 32, 2 * REST, U32).rearrange("p (w e) -> p w e", w=2)
        bad = region(pat + 64, 16)
        rowm = region(pat + 80, NT)
        assert pat + 80 + NT <= REGION
        steps = m8x.bitcast(I32)
        assert NT * REST // STEP <= 256
        lists_any, lists_all, used = K2[:, 0:NT * REST // STEP], segb[:, 0:NT * REST // STEP], segi[:, 0:NT * REST // STEP]
        e_t = region(0, 4 * BANK).rearrange("p (w n) -> p w n", w=4)
        r_t = region(4 * BANK, 4 * BANK).rearrange("p (w n) -> p w n", w=4)

        def v_of(p):
            return V[:, :, :] if p % 2 == 0 else Vb

        def swapped(p):
            return 1 if p >= 2 else 0

        def blk(h, it, b):
            return (16 * h + 8 * it + 2 * b) % NT

        NGRP = NBUF * 2 * SLOTS
        A_L1 = 2 * ITERS

        @block.sync
        def _(sp):
            sp.dma_start(xT_s[:, :], xT).then_inc(x_in, 16)
            sp.dma_start(X[:, :, :], x.rearrange("(t p) c -> p t c", p=P)).then_inc(x_in, 16)

            def load_A(u, b, j, h):
                sp.dma_start(A[b][:, :].rearrange("p (k n) -> p k n", k=2),
                             adjT[ds(j * P, 2 * P), ds(h * HALF, HALF)].rearrange("(k p) n -> p k n", p=P))\
                    .then_inc(a_in[b], 16)

            def load_V(b, j, v):
                sp.dma_start(VS[:, b, :, :], v[:, ds(j, 2), :]).then_inc(vs_in[b], 16)

            def product_loads(u0, v, swap, ready, units, aofs=0):
                for b in range(NBUF):
                    if aofs and b == 0:
                        sp.wait_ge(mask_made, L1_LOADS * 4)
                    sp.wait_ge(a_out[b], u0)
                    if units and b % 2 == 0:
                        sp.wait_ge(mk[b // 2], u0)
                    load_A(u0, b, blk(0, 0, b ^ swap), 0)
                sp.wait_ge(v_ready, ready)
                for b in range(NBUF):
                    load_V(b, blk(0, 0, b ^ swap), v)
                with sp.Fori(1, 2 * ITERS) as n:
                    h = sp.snap(n // ITERS)
                    first = sp.snap((n * 8 + h * 16) % NT, max_val=NT - 8)
                    for b in range(NBUF):
                        j = sp.snap(first + 2 * (b ^ swap), max_val=NT - 2)
                        sp.wait_ge(a_out[b], n + u0)
                        if units and b % 2 == 0:
                            sp.wait_ge(mk[b // 2], n + u0)
                        load_A(n, b, j, h)
                        load_V(b, j, v)

            for p in range(4):
                product_loads(USES_L0 + 2 * ITERS * p, v_of(p), swapped(p), p + 1, True)
            for w in range(2):
                sp.wait_ge(c_cp[w], USES_L2)
            sp.dma_start(cand_d, cand.rearrange("p t j e -> p (t j e)")).then_inc(cand_out, 16)
            if upto == 0:
                sp.wait_ge(x_ready, 1)
                sp.wait_ge(cand_out, 16)
                for w in range(2):
                    for k in range(2):
                        sp.wait_ge(s_st[w][k], 16 * USES_L2)
                sp.dma_start(out.rearrange("(t p) c -> p t c", p=P), X[:, :, :]).then_inc(out_st, 16)
                sp.wait_ge(out_st, 16)
                return

            def load_chunk(b, q, j0):
                sp.dma_start(A[b][:, :].rearrange("p (k n) -> p k n", k=4),
                             adjT[ds(j0 * P, 4 * P), ds(q * QC, QC)].rearrange("(k p) n -> p k n", p=P))\
                    .then_inc(a_in[b], 16)

            sp.wait_ge(flag_made, 1)
            flag = sp.value_load(ext[0:1, 12:13].bitcast(I32), min_val=0, max_val=1)
            for b in range(NBUF):
                sp.wait_ge(a_out[b], USES_L2)
            with sp.If(flag > 0):
                for k in range(2):
                    sp.dma_start(smax_d[k * NT:(k + 1) * NT, :].rearrange("t p -> p t"),
                                 Hs[:, :, 2 * P + 2 + 2 * k], allow_slow_non_contiguous=True).then_inc(gen_in, 16)
                sp.wait_ge(gen_in, 32)
                for k in range(2):
                    sp.dma_start(A[1 + k][:, :],
                                 smax_d[k * NT:(k + 1) * NT, :].rearrange("(a t) p -> a (t p)", a=1).partition_broadcast(P))\
                        .then_inc(gen_in, 16)
                with sp.Fori(0, NT) as t:
                    sp.wait_ge(gen_used, t)
                    sp.dma_start(A[0][:, :], adj[ds(t * P, P), :]).then_inc(gen_row, 16)
                sp.wait_ge(gen_used, NT)
            with sp.Else():
                pass
            sp.wait_ge(mxt_made, 1)
            sp.dma_start(smax_d, MXT[0:2 * NT, :]).then_inc(smax_out, 16)
            sp.wait_ge(smax_out, 16)
            for b in range(NBUF):
                load_chunk(b, 0, 4 * b)
            with sp.Fori(0, 4) as q:
                with sp.If(flag > 0):
                    sp.wait_ge(q_made, 64 * q)
                    for k in range(2):
                        sp.dma_start(Bx[:, k, 1, :],
                                     smax_d[ds(k * NT + 8 * q, 8), :].rearrange("(a t) p -> a (t p)", a=1).partition_broadcast(P))\
                            .then_inc(smax_in, 16)
                with sp.Else():
                    pass
                for n in range(4, 8):
                    sp.wait_ge(mask_made, 32 * q + (4 * (n - 4) + 4))
                    load_chunk(n % NBUF, q, sp.snap((8 * q + 4 * n) % NT, max_val=NT - 4))
                with sp.If(q < 3):
                    for n in range(4):
                        sp.wait_ge(mask_made, 32 * q + (4 * (n + 4) + 4))
                        load_chunk(n, sp.snap((q + 1) % 4), sp.snap((8 * q + (4 * n + 8)) % NT, max_val=NT - 4))
                with sp.Else():
                    pass
            def finish(n):
                sp.wait_ge(x_ready, n)
                sp.dma_start(out.rearrange("(t p) c -> p t c", p=P), X[:, :, :]).then_inc(out_st, 16)
                sp.wait_ge(out_st, 16)

            if upto == 1:
                finish(2)
                return

            sp.wait_ge(x_ready, 2)
            sp.dma_start(BB, L2B.partition_broadcast(P)).then_inc(l2c_in, 16)
            sp.wait_ge(mask_made, L1_LOADS * 4)
            for b in range(NBUF):
                load_A(0, b, 2 * b, 0)
            sp.wait_ge(v_ready, 6)
            for b in range(NBUF):
                load_V(b, 2 * b, V[:, :, :])
            with sp.Fori(1, 2 * ITERS) as n:
                h = sp.snap(n // ITERS)
                first = sp.snap((n * 8 + h * 16) % NT, max_val=NT - 8)
                for step in range(NBUF + 2):
                    if step < NBUF:
                        sp.wait_ge(t_made, 8 * n + (2 * step - 6))
                        load_A(n, step, sp.snap(first + 2 * step, max_val=NT - 2), h)
                    if step >= 2:
                        b = step - 2
                        sp.wait_ge(a_out[b], n + USES_L2)
                        load_V(b, sp.snap(first + 2 * b, max_val=NT - 2), V[:, :, :])
            if upto == 2:
                finish(3)
                return

            for b in range(NBUF):
                sp.wait_ge(a_out[b], USES_L3)
            sp.dma_start(cand2.rearrange("p t n -> p (t n)"), cand_d).then_inc(cand_in, 16)
            product_loads(USES_L3, V[:, :, :], 0, 7, False)
            sp.wait_ge(zero_made, 1)
            sp.dma_start(table_d[N:N + P, :], K1[:, 0:P]).then_inc(tab_out, 16)
            sp.wait_ge(v_ready, 8)
            sp.dma_start(table_d[0:N, :].rearrange("(t p) c -> p t c", p=P), V[:, :, :]).then_inc(tab_out, 16)
            one_v = onehot_d.rearrange("(k j h p) n -> p k j h n", k=SLOTS, j=NT, h=2)
            with sp.Fori(0, 2 * ITERS) as n:
                h = sp.snap(n // ITERS)
                for b in range(NBUF):
                    sp.wait_ge(a_out[b], n + USES_POOL)
                    j = sp.snap((n * 8 + 2 * b) % NT, max_val=NT - 2)
                    dst = A[b][:, 0:HOTW].rearrange("p (k j n) -> p k j n", k=SLOTS, j=2)
                    for k in range(SLOTS):
                        sp.dma_start(dst[:, k, :, :], one_v[:, k, ds(j, 2), ds(h, 1), :].rearrange("p j h n -> p j (h n)"))\
                            .then_inc(a_in[b], 16)
                    if b == 0:
                        sp.wait_ge(part_a, 3)
                    sp.dma_start(A[b][:, HOTW:HOTW + 3 * P].rearrange("p (e j c) -> p e j c", e=3, j=2),
                                 OPw[:, :, ds(j, 2), :]).then_inc(a_in[b], 16)
            sp.wait_ge(flag2, 1)
            flag = sp.value_load(bad[0:1, 8:9].bitcast(I32), min_val=0, max_val=1)
            with sp.If(flag > 0):
                with sp.Fori(0, NT) as t:
                    with sp.Fori(0, NT * 4) as c:
                        sp.wait_ge(dn_used, 2 * (t * (NT * 4) + c))
                        sp.dma_start(A[0][:, :], table_d[ds(c * 32, 32), :].rearrange("(a j) c -> a (j c)", a=1)
                                     .partition_broadcast(P)).then_inc(dn_in, 16)
                        sp.dma_start(A[1][:, 0:32], adj[ds(t * P, P), ds(c * 32, 32)]).then_inc(dn_in, 16)
            with sp.Else():
                pass
            finish(5)

        @block.gpsimd
        def _(pool):
            n = Run()

            def step(ins):
                n.n += 1
                ins.then_inc(consts, 1)
                pool.wait_ge(consts, n.n)

            step(pool.memset(ident[:, :], 0.0))
            step(pool.affine_select(out=ident[:, :], in_=ident[:, :], compare_op=ALU.not_equal, fill=1.0,
                                    base=0, pattern=[[-1, P]], channel_multiplier=1))
            step(pool.memset(notid[:, :], 1.0))
            step(pool.affine_select(out=notid[:, :], in_=notid[:, :], compare_op=ALU.not_equal, fill=0.0,
                                    base=0, pattern=[[-1, P]], channel_multiplier=1))
            rk = R[:, 0:P]
            step(pool.memset(rk, -1.0))
            step(pool.affine_select(out=rk, in_=rk, compare_op=ALU.is_gt, fill=0.0,
                                    base=0, pattern=[[1, P]], channel_multiplier=-1))
            step(pool.affine_select(out=rk, in_=rk, compare_op=ALU.not_equal, fill=RANK,
                                    base=0, pattern=[[-1, P]], channel_multiplier=1))
            step(pool.tensor_copy(rankw[:, :], rk))
            step(pool.tensor_copy(identb[:, :], ident[:, :]))
            step(pool.memset(cols[:, 5:6], EPS))
            step(pool.memset(cols[:, 7:8], 1.0 - RANK))
            step(pool.memset(cols[:, 13:14], TINY))
            step(pool.iota(cols[:, 14:15].bitcast(I32), pattern=[[0, 1]], base=1, channel_multiplier=1))
            step(pool.tensor_copy(cols[:, 6:7], cols[:, 14:15].bitcast(I32)))
            pool.dma_start(Wt[:, 0, :], W1).then_inc(w_in, 16)
            pool.dma_start(Wt[:, 1, :], W2).then_inc(w_in, 16)
            pool.dma_start(Wt[:, 2, :], L2W).then_inc(w_in, 16)
            pool.dma_start(Wt[:, 3, :], L3W).then_inc(w_in, 16)
            pool.dma_start(fcol[:, 0, :], f1).then_inc(w_in, 16)
            pool.dma_start(fcol[:, 1, :], f2).then_inc(w_in, 16)
            for c, src in enumerate((g1, b1, g2, b2, L3b)):
                pool.dma_start(cols[:, c:c + 1], src).then_inc(w_in, 16)
            pool.dma_start(cols[:, 8:9], mu.partition_broadcast(P)).then_inc(w_in, 16)
            pool.dma_start(cols[:, 9:10], sigma.partition_broadcast(P)).then_inc(w_in, 16)
            pool.dma_start(RH[:, 0:P], ff0T[0]).then_inc(w_in, 16)
            pool.dma_start(RH[:, P + 1:2 * P + 1], ff0T[1]).then_inc(w_in, 16)
            pool.dma_start(ff1s[:, :, :], ff1T.rearrange("k c o -> c k o")).then_inc(w_in, 16)

            for p in range(4):
                with pool.Fori(0, 2 * ITERS) as n:
                    it = pool.snap(n + 2 * ITERS * p)
                    h = pool.snap(n // ITERS)
                    first = pool.snap((n * 8 + h * 16) % NT, max_val=NT - 8)
                    for w in range(2):
                        row = pool.snap(((first + 2 * ((2 * w) ^ swapped(p)) + p % 2) * 2 + h) * P, max_val=(2 * NT - 1) * P)
                        pool.wait_ge(y_act, 8 * it + (4 * w + 5))
                        pool.dma_start(onehot_d[ds(row, P), :], SBw[:, w, 0, :]).then_inc(s_st[w][0], 16)
                        pool.wait_ge(k_made, 8 * it + (4 * w + 4))
                        pool.dma_start(onehot_d[ds(row + 2 * NT * P, P), :], SBw[:, w, 1, :])\
                            .then_inc(s_st[w][1], 16)
            if upto == 0:
                return
            for w in range(2):
                for k in range(2):
                    pool.wait_ge(s_st[w][k], 16 * USES_L2)
            pool.wait_ge(x_ready, 1)
            pool.wait_ge(cand_out, 16)
            pool.dma_start(QB[:, 0, 0:2 * P].rearrange("p (k c) -> p k c", k=2),
                           ff0.rearrange("k o c -> o k c")).then_inc(w_in, 16)
            pool.dma_start(attw, attc).then_inc(w_in, 16)
            pool.wait_ge(ext_made, 1)
            pool.partition_all_reduce(ext[:, 4:8], ext[:, 0:4], P, RMAX).then_inc(ext_all, 1)
            with pool.Fori(0, 4) as q:
                for s in range(32):
                    pool.wait_ge(r_made, 64 * q + (2 * s + 2))
                    pool.wait_ge(mask_made, 32 * q + (s + 1))
                    pool.tensor_tensor(QA[:, s % 3, 1, :], QA[:, s % 3, 1, :], Mt[:, s % 2, :], ALU.mult)\
                        .then_inc(p_made[1], 1)
            if upto == 1:
                return

            pool.wait_ge(x_ready, 2)
            pool.tensor_copy(DD[:, 0:P], notid[:, :])
            pool.memset(DD[:, P:2 * P], 1.0).then_inc(dd_made, 1)
            with pool.Fori(0, 2 * ITERS) as n:
                for k in range(8):
                    b, jj = k // 2, k % 2
                    pool.wait_ge(u_made, 8 * n + (k + 1))
                    pool.wait_ge(n_made, 8 * n + k)
                    pool.tensor_tensor(T[:, k % 2, :], A[b][:, jj * HALF:(jj + 1) * HALF], U[:, k, :], ALU.mult)\
                        .then_inc(t_made, 1)
            if upto == 2:
                return

            for b in range(NBUF):
                pool.wait_ge(a_out[b], USES_L3)
            pool.iota(segi.rearrange("p (s e) -> p s e", e=8), pattern=[[P, NT], [0, 8]], base=0,
                      channel_multiplier=0).then_inc(seg_made, 1)
            pool.wait_ge(seg_made, 1)
            pool.tensor_copy(segb, segi).then_inc(seg_made, 1)
            pool.wait_ge(idx_made, 1)
            pool.partition_all_reduce(lists_all, lists_any, P, RMAX).then_inc(used_made, 1)
            pool.wait_ge(used_made, 1)
            pool.tensor_scalar(lists_all, lists_all, 0.0, None, ALU.is_gt).then_inc(used_made, 1)
            pool.wait_ge(used_made, 2)
            pool.tensor_copy(used, lists_all).then_inc(used_made, 1)
            pool.wait_ge(used_made, 3)
            pool.wait_ge(tab_out, 32)
            with pool.Fori(0, NT // 2) as n:
                for w in range(2):
                    pool.wait_ge(g_used[w], n)
                    pool.tensor_copy(ixs[:, w, :], IDX[:, ds(2 * n + w, 1), :].squeeze(1)).then_inc(ix_cp, 1)
                    pool.wait_ge(ix_cp, 2 * n + (w + 1))
                    settled(pool)
                    def gather(e, landed):
                        pool.indirect_dma_start(G[:, w, e, :], None, table_d,
                                                bass.IndirectOffsetOnAxis(ap=ixs[:, w, e:e + 1], axis=0))\
                            .then_inc(landed, 16)

                    for e in range(REST - SPARE):
                        gather(e, g_in[w])
                    for e in range(REST - SPARE, REST, STEP):
                        some = pool.value_load(used[0:1, ds(pool.snap((2 * n + w) * (REST // STEP) + e // STEP), 1)],
                                               min_val=0, max_val=1)
                        with pool.If(some > 0):
                            for i in range(STEP):
                                gather(e + i, g_more[w])
                            pool.sem_inc(g_seen[w], 1)
                        with pool.Else():
                            pool.memset(G[:, w, e:e + STEP, :], 0.0).then_inc(g_seen[w], 1)
            pool.wait_ge(bad_made, 1)
            pool.partition_all_reduce(bad[:, 4:5], bad[:, 0:1], P, RMAX).then_inc(bad_all, 1)

        @block.tensor
        def _(pe):
            ms = Run()

            drained = [0]

            def drain():
                pe.wait_ge(ms_free, ms.n)
                drained[0] = ms.n

            def misc(n=BANK):
                if ms.n - 3 > drained[0]:
                    pe.wait_ge(ms_free, ms.n - 3)
                k = 4 + ms.n % 4
                ms.n += 1
                return bank(k, n)

            def transposes(src, norm=0):
                for g in range(8):
                    if norm:
                        pe.wait_ge(ln_act if g % 2 else ln_dve, 4 * (norm - 1) + g // 2 + 1)
                    m = misc()
                    for k in range(4):
                        t = 4 * g + k
                        last = pe.transpose(m[:, k * P:(k + 1) * P], src(t), ident[:, :])
                    last.then_inc(ms_full, 1)

            def features(lhsT, rhs):
                for g in range(8):
                    m = misc()
                    for k in range(4):
                        last = pe.matmul(m[:, k * P:(k + 1) * P], lhsT(4 * g + k), rhs, start=True, stop=True)
                    last.then_inc(ms_full, 1)

            def unit_step(w, s, it):
                g = 8 * it + (4 * w + s)
                if s < 4:
                    if s == 0:
                        pe.wait_ge(mk[w], it + 1)
                    pe.wait_ge(y_act, g)
                    pe.matmul(bank(4 + s % 2), rankw[:, :], M01[:, w, s * BANK:(s + 1) * BANK],
                              start=True, stop=True).then_inc(y_done, 1)
                if s > 0:
                    pe.wait_ge(k_made, g)
                    pe.wait_ge(m8_done, g - 1)
                    half = (s - 1) % 2
                    tb = bank(6 + half).bitcast(BF16)[:, 0:BANK]
                    for k in range(4):
                        last = pe.transpose(tb[:, k * P:(k + 1) * P],
                                            Kb[:, half, k * P:(k + 1) * P], identb[:, :])
                    last.then_inc(t_done, 1)

            UNIT_AT = {2 + 3 * s + 16 * w: (w, s) for w in range(2) for s in range(5)}

            def product(u0, aofs=0, p=None, weights=False):
                with pe.Fori(0, 2) as h:
                    pe.wait_ge(acc_free, 4 * (u0 // (2 * ITERS)) * 2 + 4 * h)

                    def one(it, first, last):
                        u = pe.snap(h * ITERS + it)
                        for b in range(NBUF):
                            if not weights:
                                pe.wait_ge(a_in[b], 16 * u + 16 * (u0 + 1 + aofs))
                            pe.wait_ge(vs_in[b], 16 * u + 16 * (u0 + 1))
                            for m in range(8):
                                jj, k = m // 4, m % 4
                                if weights:
                                    if k == 0:
                                        pe.wait_ge(e_made, 8 * u + (2 * b + jj + 1))
                                    rhs = U[:, 2 * b + jj, k * BANK:(k + 1) * BANK]
                                else:
                                    rhs = A[b][:, jj * HALF + k * BANK:jj * HALF + (k + 1) * BANK]
                                ins = pe.matmul(bank(k), VS[:, b, jj, :], rhs,
                                                start=first and b == 0 and jj == 0,
                                                stop=last and b == NBUF - 1 and jj == 1)
                                if m == 7:
                                    ins.then_inc(a_out[b], 1)
                                if p is not None and 8 * b + m in UNIT_AT:
                                    unit_step(*UNIT_AT[8 * b + m], u + u0)

                    one(0, True, False)
                    with pe.Fori(1, ITERS - 1) as it:
                        one(it, False, False)
                    one(ITERS - 1, False, True)

            pe.wait_ge(x_in, 32)
            pe.wait_ge(w_in, 16 * 16)
            pe.wait_ge(consts, 14)
            features(lambda t: xT_s[:, t * P:(t + 1) * P], Wt[:, 0, :])
            for p in range(4):
                product(2 * ITERS * p, p=p)
                pe.wait_ge(ot_ready, 8 * (p + 1))
                pe.wait_ge(y_act, 8 * 2 * ITERS * (p + 1) + 1)
                pe.wait_ge(m8_done, 8 * 2 * ITERS * (p + 1) + 1)
                if p == 1:
                    features(lambda t: OT[:, t * P:(t + 1) * P], Wt[:, 1, :])
                else:
                    transposes(lambda t: OT[:, t * P:(t + 1) * P])
                drain()
            if upto == 0:
                return

            transposes(lambda t: V[:, t, :], norm=2)
            pe.wait_ge(w_in, 16 * 18)
            m = misc()
            for k in range(2):
                last = pe.matmul(m[:, 2 * k:2 * k + 2], QB[:, 0, k * P:(k + 1) * P], attw[:, 2 * k:2 * k + 2],
                                 start=True, stop=True)
            last.then_inc(ms_full, 1)
            pe.wait_ge(ot_ready, 33)
            pe.wait_ge(sr_made, 1)
            for t in range(NT):
                m = misc(HW)
                pe.matmul(m, OT[:, t * P:(t + 1) * P], RH[:, :], start=True, stop=True).then_inc(ms_full, 1)
            pe.wait_ge(mx_made, 1)
            drain()
            m = misc(P)
            pe.transpose(m[0:2 * NT, :], MX.rearrange("p k t -> p (k t)"), ident[:, :]).then_inc(ms_full, 1)
            drain()

            def source_rows(q, k, used):
                pe.wait_ge(src_used, used)
                for e in range(2):
                    last = pe.matmul(bank(6 + e), SRv[:, k, :], OT[:, ds(q * QC + e * BANK, BANK)],
                                     start=True, stop=True)
                last.then_inc(src_full, 1)

            def region_of(k, it):
                r = 8 * k + it
                return PS[:, (r // 3) * BANK + (r % 3) * (P + 1):(r // 3) * BANK + (r % 3 + 1) * (P + 1)]

            pe.wait_ge(h_made, 1)
            pe.sem_inc(p_used, 4)
            for k in range(2):
                source_rows(0, k, k)
            with pe.Fori(0, 4) as q:
                pe.wait_ge(att_out, 16 * q)
                for s in range(32):
                    j = pe.snap((8 * q + s) % NT, max_val=NT - 1)
                    for k in range(2):
                        pe.wait_ge(p_made[k], 32 * q + (s + 1))
                        for it in range(8):
                            last = pe.matmul(region_of(k, it), QA[:, s % 3, k, it * P:(it + 1) * P],
                                             Hs[:, ds(j, 1), k * P:k * P + P + 1],
                                             start=s == 0 and (8 * k + it) % 3 == 0, stop=s == 31,
                                             skip_group_check=True)
                        last.then_inc(p_used, 1)
                        if (s, k) in ((30, 1), (31, 0)):
                            with pe.If(q < 3):
                                head = 1 if s == 31 else 0
                                source_rows(pe.snap((q + 1) % 4), head, 2 * q + (2 + head))
                            with pe.Else():
                                pass

            for k in range(2):
                src = V[:, :, :] if k == 0 else OT[:, :].rearrange("p (t c) -> p t c", c=P)
                transposes(lambda t: src[:, t, :], norm=3 + k)
            drain()
            for k in range(2):
                pe.wait_ge(qt_made, k + 1)
                features(lambda t: QT[:, k, t * P:(t + 1) * P], ff1s[:, k, :])
            drain()
            if upto == 1:
                return

            transposes(lambda t: X[:, t, :], norm=5)
            drain()
            pe.wait_ge(ot_ready, 34)
            features(lambda t: OT[:, t * P:(t + 1) * P], Wt[:, 2, :])
            product(USES_L2, weights=True)
            pe.wait_ge(ot_ready, 42)
            drain()
            transposes(lambda t: OT[:, t * P:(t + 1) * P])
            drain()
            if upto == 2:
                return

            transposes(lambda t: X[:, t, :], norm=6)
            drain()
            pe.wait_ge(ot_ready, 43)
            features(lambda t: OT[:, t * P:(t + 1) * P], Wt[:, 3, :])
            product(USES_L3, aofs=A_L1)
            pe.wait_ge(ot_ready, 51)
            drain()
            transposes(lambda t: OT[:, t * P:(t + 1) * P])
            drain()
            with pe.Fori(0, 2 * ITERS) as n:
                for b in range(NBUF):
                    pe.wait_ge(a_in[b], 48 * n + (16 * (USES_POOL + A_L1) + 48))
                    ob = A[b][:, HOTW:HOTW + 3 * P].bitcast(BF16).rearrange("p (e j c) -> p e j c", e=3, j=2)
                    hot = A[b][:, 0:HOTW].bitcast(FP8).rearrange("p (k j n) -> p k j n", k=SLOTS, j=2)
                    for jj in range(2):
                        for k in range(SLOTS):
                            g = (b * 2 + jj) * SLOTS + k
                            pe.wait_ge(px_free, NGRP * n + (g + 1))
                            settled(pe)
                            for e in range(3):
                                for c in range(4):
                                    last = pe.matmul(bank(4 * (g % 2) + c), ob[:, e, jj, :],
                                                     hot[:, k, jj, c * BANK:(c + 1) * BANK],
                                                     start=e == 0, stop=e == 2)
                            if g % (2 * SLOTS) == 2 * SLOTS - 1:
                                last.then_inc(a_out[b], 1)
                            else:
                                last.then_inc(px_full, 1)
            pe.wait_ge(px_free, NGRP * 2 * ITERS + 2)
            pe.wait_ge(x_ready, 4)
            transposes(lambda t: OT[:, t * P:(t + 1) * P])

        def half_out(act, n, u0, func, **kw):
            if isinstance(n, int):
                act.wait_ge(a_out[NBUF - 1], u0 + n + 1)
                for k in range(4):
                    at = n // ITERS * HALF + k * BANK
                    act.activation(OT[:, at:at + BANK], bank(k), func, **kw).then_inc(acc_free, 1)
                return
            with act.If(n == ITERS - 1):
                act.wait_ge(a_out[NBUF - 1], u0 + ITERS)
                for k in range(4):
                    act.activation(OT[:, k * BANK:(k + 1) * BANK], bank(k), func, **kw).then_inc(acc_free, 1)
            with act.Else():
                pass

        @block.scalar
        def _(act):
            ms = Run()

            def misc(n=BANK):
                ms.n += 1
                act.wait_ge(ms_full, ms.n)
                return bank(4 + (ms.n - 1) % 4, n)

            act.wait_ge(consts, 14)
            act.sem_inc(y_act, 1)

            def unit_chunk(w, s, it):
                act.wait_ge(y_done, 8 * it + (4 * w + s + 1))
                settled(act)
                if s == 0:
                    act.wait_ge(s_st[w][0], 16 * it)
                    settled(act)
                act.activation(SB[:, w, 0, s * BANK:(s + 1) * BANK], bank(4 + s % 2), ACT.Relu,
                               bias=cols[:, 7:8], saturate=False).then_inc(y_act, 1)

            def keep_cand(w, it, h, j):
                act.wait_ge(m8_done, 8 * it + (4 * w + 5))
                dst = cand.rearrange("p (h t) j e -> p h t j e", h=2)
                act.activation(dst[:, ds(h, 1), :, ds(j, 1), :], m8[:, w, :, :].unsqueeze(1), ACT.Copy)\
                    .then_inc(c_cp[w], 1)

            def evacuate(n_half, func, **kw):
                with act.Fori(0, 2) as h:
                    if n_half[2] is not None:
                        p = n_half[2]
                        with act.Fori(0, ITERS) as k:
                            it = act.snap(h * ITERS + k + 2 * ITERS * p)
                            first = act.snap((h * 16 + k * 8) % NT, max_val=NT - 8)
                            jb = [act.snap(first + 2 * ((2 * w) ^ swapped(p)) + p % 2) for w in range(2)]
                            for w in range(2):
                                for s in range(4):
                                    unit_chunk(w, s, it)
                                    if w == 1 and s == 1:
                                        keep_cand(0, it, h, jb[0])
                            keep_cand(1, it, h, jb[1])
                    act.wait_ge(a_out[NBUF - 1], n_half[0] + ITERS + ITERS * h)
                    for k in range(4):
                        act.activation(OT[:, ds(h * HALF + k * BANK, BANK)], bank(k), func, **kw)\
                            .then_inc(acc_free, 1)

            def to_v(v, scale=None, last=True):
                for g in range(8):
                    m = misc()
                    if scale is None:
                        act.activation(v[:, 4 * g:4 * g + 4, :], m.rearrange("p (t c) -> p t c", c=P),
                                       ACT.Copy).then_inc(ms_free, 1)
                    else:
                        for k in range(4):
                            t = 4 * g + k
                            ins = act.activation(v[:, t, :], m[:, k * P:(k + 1) * P], ACT.Copy,
                                                 scale=scale[:, t:t + 1])
                        ins.then_inc(ms_free, 1)
                act.wait_ge(ms_free, ms.n)
                act.sem_inc(v_ready, 1)

            to_v(v_of(0))
            for p in range(4):
                evacuate((2 * ITERS * p, 0, p), ACT.Relu if p == 1 else ACT.Copy)
                act.wait_ge(acc_free, 8 * (p + 1))
                act.sem_inc(ot_ready, 8)
                if p == 0:
                    to_v(v_of(1), fcol[:, 0, :])
                elif p == 1:
                    to_v(v_of(2))
                elif p == 2:
                    to_v(v_of(3), fcol[:, 1, :])
            def normalise(n, dst, src, slot=0):
                act.wait_ge(ln_var, n)
                act.activation(rstd[:, slot, :], rstd[:, slot, :], ACT.Sqrt).then_inc(ln_std, 1)
                act.wait_ge(ln_mean, n)
                for g in range(1, 8, 2):
                    for t in range(4 * g, 4 * g + 4):
                        ins = act.activation(dst[:, t, :], src[:, t, :], ACT.Identity,
                                             scale=rstd[:, slot, t:t + 1], bias=st6[:, slot, t, 0:1])
                    ins.then_inc(ln_act, 1)

            normalise(1, X, X)
            if upto == 0:
                return

            def turned(dst, scale, bias):
                for g in range(8):
                    m = misc()
                    act.activation(dst[:, g * BANK:(g + 1) * BANK], m, ACT.Identity, scale=scale, bias=bias)\
                        .then_inc(ms_free, 1)
                act.wait_ge(ms_free, ms.n)

            normalise(2, V, X)
            ms.n += 8
            turned(OT, cols[:, 0:1], cols[:, 1:2])
            act.sem_inc(ot_ready, 1)
            m = misc(4)
            act.activation(RH[:, 2 * P + 1:2 * P + 5], m, ACT.Copy).then_inc(ms_free, 1)
            act.wait_ge(ms_free, ms.n)
            act.sem_inc(sr_made, 1)
            for t in range(NT):
                m = misc(HW)
                act.activation(Hs[:, t, :], m, ACT.Copy).then_inc(ms_free, 1)
            act.wait_ge(ms_free, ms.n)
            act.sem_inc(h_made, 1)
            ms.n += 1
            with act.Fori(0, 4) as q:
                for s in range(32):
                    j = act.snap((8 * q + s) % NT, max_val=NT - 1)
                    if s != 2:
                        act.wait_ge(p_used, 64 * q + (2 + 2 * s if s < 2 else 2 * s))
                    for k in range(2):
                        if s == 0:
                            act.wait_ge(b_made, 2 * q + (k + 1))
                            act.wait_ge(r_made, 64 * q)
                        else:
                            act.wait_ge(r_made, 64 * q + (2 * s - 1 + k))
                        act.activation(QA[:, s % 3, k, :], Bx[:, k, 0, :], ACT.Exp,
                                       bias=Hs[:, ds(j, 1), 2 * P + 2 + 2 * k:2 * P + 3 + 2 * k].squeeze(1))
                        act.activation(QB[:, k, :], Bx[:, k, 1, :], ACT.Exp,
                                       bias=dst2[:, ds(j, 1), k:k + 1].squeeze(1)).then_inc(q_made, 1)
            OTr = OT[:, :].rearrange("p (t c) -> p t c", c=P)
            for k, rows in enumerate((V, OTr)):
                normalise(3 + k, rows, rows, k)
                turned(QT[:, k, :], cols[:, 2:3], cols[:, 3:4])
                act.sem_inc(qt_made, 1)
            for g in range(16):
                act.wait_ge(e_neg, g + 1)
                act.activation(e_t[:, g % 4, :], e_t[:, g % 4, :], ACT.Exp).then_inc(e_exp, 1)
            ms.n += 16
            normalise(5, X, X)
            if upto == 1:
                return

            for g in range(8):
                m = misc()
                act.activation(OT[:, g * BANK:(g + 1) * BANK], m, ACT.Copy).then_inc(ms_free, 1)
            act.wait_ge(ms_free, ms.n)
            act.sem_inc(ot_ready, 1)
            ms.n += 8
            act.wait_ge(inv_made, 1)

            def guess(k, n, step):
                b, jj = k // 2, k % 2
                if step == 0:
                    act.wait_ge(s_made, 8 * n + (k + 1))
                    act.wait_ge(a_out[b], n + USES_L2)
                    act.activation(U[:, k, :], A[b][:, jj * HALF:(jj + 1) * HALF], ACT.Ln, bias=cols[:, 13:14])\
                        .then_inc(lnr, 1)
                else:
                    act.wait_ge(lnr, 8 * n + (k + 1))
                    act.activation(U[:, k, :], U[:, k, :], ACT.Exp, scale=-1.0).then_inc(u_made, 1)

            def weight(k, n, step):
                if step == 0:
                    if k in DVE_SQUARES:
                        return
                    act.wait_ge(n_made, 8 * n + (k + 2))
                    act.activation(U[:, k, :], U[:, k, :], ACT.Square, scale=cols[:, 11:12], bias=cols[:, 12:13])\
                        .then_inc(sq_made, 1)
                else:
                    if k in DVE_SQUARES:
                        act.wait_ge(sqd_made, len(DVE_SQUARES) * n + (DVE_SQUARES.index(k) + 1))
                    else:
                        rest = [i for i in range(8) if i not in DVE_SQUARES]
                        act.wait_ge(sq_made, len(rest) * n + (rest.index(k) + 1))
                    act.activation(U[:, k, :], U[:, k, :], ACT.Exp, scale=-1.0).then_inc(e_made, 1)

            def batch(first, n, before):
                for k in range(first, first + 4):
                    guess(k, n, 0)
                for k in range(4):
                    guess(first + k, n, 1)
                    if before is not None:
                        for step in range(2):
                            weight(4 - first + k, before, step)

            batch(0, 0, None)
            with act.Fori(0, 2 * ITERS - 1) as n:
                batch(4, n, n)
                batch(0, n + 1, n)
                half_out(act, n, USES_L2, ACT.Copy)
            batch(4, 2 * ITERS - 1, 2 * ITERS - 1)
            for k in range(4, 8):
                for step in range(2):
                    weight(k, 2 * ITERS - 1, step)
            half_out(act, 2 * ITERS - 1, USES_L2, ACT.Copy)
            act.wait_ge(acc_free, 40)
            act.sem_inc(ot_ready, 8)
            ms.n += 8
            normalise(6, X, X)
            if upto == 2:
                return

            for g in range(8):
                m = misc()
                act.activation(OT[:, g * BANK:(g + 1) * BANK], m, ACT.Copy).then_inc(ms_free, 1)
            act.wait_ge(ms_free, ms.n)
            act.sem_inc(ot_ready, 1)
            to_v(V[:, :, :])
            evacuate((USES_L3, 0, None), ACT.Relu, bias=cols[:, 4:5])
            act.wait_ge(acc_free, 48)
            act.sem_inc(ot_ready, 8)
            to_v(V[:, :, :])
            act.activation(OP[:, 0, :, :], V[:, :, :], ACT.Copy).then_inc(part_a, 1)
            r1v = r1.rearrange("p (t c) -> p t c", c=P)
            act.wait_ge(part_d, 1)
            act.activation(OP[:, 1, :, :], r1v, ACT.Copy).then_inc(part_a, 1)
            act.wait_ge(part_d, 2)
            act.activation(OP[:, 2, :, :], r1v, ACT.Copy).then_inc(part_a, 1)
            normalise(7, X, X)
        @block.vector
        def _(dve):
            own = Run()
            ms = Run()
            lns = Run()

            def did(ins):
                own.n += 1
                ins.then_inc(dv, 1)
                return own.n

            def after(n):
                dve.wait_ge(dv, n)

            dve.wait_ge(consts, 14)
            dve.sem_inc(m8_done, 1)

            def unit(w, it):
                dve.wait_ge(a_in[2 * w], 16 * it + 16)
                a = A[2 * w][:, :]
                jj = unit.p % 2
                a = a[:, jj * HALF:(jj + 1) * HALF]
                dve.tensor_scalar(Mk[:, w, :], a, 0.0, cols[:, 6:7], ALU.not_equal, ALU.mult)
                dve.tensor_scalar(M01[:, w, :], a, 0.0, None, ALU.not_equal).then_inc(mk[w], 1)
                dve.wait_ge(s_st[w][1], 16 * it)
                dve.wait_ge(c_cp[w], it)
                dve.wait_ge(mk[w], it + 1)
                for s in range(5):
                    g = 8 * it + (4 * w + s)
                    if s < 4:
                        dve.wait_ge(y_act, g + 2)
                        settled(dve)
                        y = bank(4 + s % 2)
                        dve.tensor_scalar(SB[:, w, 1, s * BANK:(s + 1) * BANK], y, RANK - 1, None,
                                          ALU.is_equal, saturate=False)
                        dve.scalar_tensor_tensor(out=Kb[:, s % 2, :], in0=y, scalar=RANK - 1.5,
                                                 in1=Mk[:, w, s * BANK:(s + 1) * BANK],
                                                 op0=ALU.is_lt, op1=ALU.mult).then_inc(k_made, 1)
                    if s > 0:
                        dve.wait_ge(t_done, g)
                        settled(dve)
                        half = (s - 1) % 2
                        tb = bank(6 + half).bitcast(BF16)[:, 0:BANK]
                        for k in range(4):
                            last = dve.max(m8[:, w, 4 * (s - 1) + k, :], tb[:, k * P:(k + 1) * P])
                        last.then_inc(m8_done, 1)

            for p in range(4):
                unit.p = p
                with dve.Fori(2 * ITERS * p, 2 * ITERS * (p + 1)) as it:
                    unit(0, it)
                    unit(1, it)

            def normalise(dst, src, slot=0):
                lns.n += 1
                last = 0
                for t in range(NT):
                    last = did(dve.bn_stats(st6[:, slot, t, :], src[:, t, :]))
                after(last)
                for t in range(NT):
                    last = did(dve.bn_aggr(mv[:, slot, t, :], st6[:, slot, t, :]))
                after(last)
                dve.tensor_scalar(rstd[:, slot, :], mv[:, slot, :, 1], EPS, None, ALU.add).then_inc(ln_var, 1)
                dve.wait_ge(ln_std, lns.n)
                after(did(dve.reciprocal(rstd[:, slot, :], rstd[:, slot, :])))
                dve.scalar_tensor_tensor(out=st6[:, slot, :, 0], in0=mv[:, slot, :, 0], scalar=-1.0,
                                         in1=rstd[:, slot, :], op0=ALU.mult, op1=ALU.mult).then_inc(ln_mean, 1)
                for g in range(0, 8, 2):
                    for t in range(4 * g, 4 * g + 4):
                        ins = dve.tensor_scalar(dst[:, t, :], src[:, t, :], mv[:, slot, t, 0:1],
                                                rstd[:, slot, t:t + 1], ALU.subtract, ALU.mult)
                    ins.then_inc(ln_dve, 1)
                dve.wait_ge(ln_dve, 4 * lns.n)
                dve.wait_ge(ln_act, 4 * lns.n)

            def elu_end(dve, g, own, did, after):
                dve.wait_ge(e_exp, g + 1)
                dve.wait_ge(ms_free, 8 * 6 + 1 + NT + 1 + 16 + g + 1)
                e = e_t[:, g % 4, :]
                after(did(dve.scalar_tensor_tensor(out=e, in0=e, scalar=-1.0, in1=r_t[:, g % 4, :],
                                                   op0=ALU.add, op1=ALU.add)))
                v = V[:, 4 * (g % 8):4 * (g % 8) + 4, :]
                xx = X[:, 4 * (g % 8):4 * (g % 8) + 4, :]
                e = e.rearrange("p (t c) -> p t c", c=P)
                after(did(dve.scalar_tensor_tensor(out=xx, in0=e, scalar=0.5, in1=xx, op0=ALU.mult, op1=ALU.add)))

            def add_misc(n0):
                for g in range(8):
                    dve.wait_ge(ms_full, n0 + g + 1)
                    m = bank(4 + (n0 + g) % 4).rearrange("p (t c) -> p t c", c=P)
                    dve.tensor_tensor(X[:, 4 * g:4 * g + 4, :], X[:, 4 * g:4 * g + 4, :], m, ALU.add)\
                        .then_inc(ms_free, 1)
                dve.wait_ge(ms_free, n0 + 8)

            dve.wait_ge(x_in, 32)
            add_misc(32)
            normalise(X, X)
            dve.sem_inc(x_ready, 1)
            if upto == 0:
                return

            after(did(dve.memset(RH[:, P:P + 1], 0.0)))
            normalise(V, X)
            dve.sem_inc(v_ready, 1)
            dve.wait_ge(sr_made, 1)
            after(did(dve.memset(SRt[:, :, :], 1.0)))
            for k in range(2):
                last = did(dve.tensor_scalar(SRt[:, k, :], SRt[:, k, :], RH[:, 2 * P + 1 + 2 * k:2 * P + 2 + 2 * k],
                                             None, ALU.mult))
            after(last)
            dve.wait_ge(h_made, 1)
            dsts = Hs[:, :, 2 * P + 2:2 * P + 5:2].rearrange("p t k -> p k t")
            did(dve.memset(Hs[:, :, P:P + 1], 1.0))
            did(dve.tensor_scalar(dst2.rearrange("p t k -> p k t"), dsts, 0.01, None, ALU.mult))
            did(dve.tensor_reduce(ext[:, 0:2], dsts, AX.X, ALU.max))
            after(did(dve.tensor_reduce(ext[:, 2:4], dsts, AX.X, ALU.min)))
            dve.tensor_scalar(ext[:, 2:4], ext[:, 2:4], -1.0, None, ALU.mult).then_inc(ext_made, 1)
            dve.wait_ge(ext_all, 1)
            after(did(dve.tensor_tensor(ext[:, 8:10], ext[:, 4:6], ext[:, 6:8], ALU.add)))
            after(did(dve.tensor_reduce(ext[:, 10:11], ext[:, 8:10], AX.X, ALU.max)))
            dve.tensor_scalar(ext[:, 12:13].bitcast(I32), ext[:, 10:11], spread, None, ALU.is_gt)\
                .then_inc(flag_made, 1)
            after(did(dve.memset(MX[:, :, :], 0.0)))
            for k in range(2):
                last = did(dve.tensor_scalar(MX[:, k, :], MX[:, k, :], ext[:, 4 + k:5 + k], None, ALU.add))
            after(last)
            dve.wait_ge(flag_made, 1)
            flag = dve.value_load(ext[0:1, 12:13].bitcast(I32), min_val=0, max_val=1)
            with dve.If(flag > 0):
                dve.wait_ge(gen_in, 16 * 4)
                for k in range(2):
                    dve.tensor_scalar(A[1 + k][:, :], A[1 + k][:, :], ext[:, 6 + k:7 + k], None, ALU.add)\
                        .then_inc(gen_own, 1)
                dve.wait_ge(gen_own, 2)
                with dve.Fori(0, NT) as t:
                    dve.wait_ge(gen_row, 16 * t + 16)
                    for k in range(2):
                        c = 2 + t * 6 + 3 * k
                        dve.scalar_tensor_tensor(out=A[3][:, :], in0=A[0][:, :], scalar=0.0, in1=A[1 + k][:, :],
                                                 op0=ALU.is_gt, op1=ALU.mult).then_inc(gen_own, 1)
                        dve.wait_ge(gen_own, c + 1)
                        dve.tensor_reduce(ext[:, 13:14], A[3][:, :], AX.X, ALU.max).then_inc(gen_own, 1)
                        dve.wait_ge(gen_own, c + 2)
                        ins = dve.scalar_tensor_tensor(out=MX[:, k, ds(t, 1)], in0=ext[:, 13:14],
                                                       scalar=ext[:, 6 + k:7 + k],
                                                       in1=Hs[:, ds(t, 1), 2 * P + 2 + 2 * k:2 * P + 3 + 2 * k].squeeze(1),
                                                       op0=ALU.subtract, op1=ALU.max).then_inc(gen_own, 1)
                        dve.wait_ge(gen_own, c + 3)
                    dve.sem_inc(gen_used, 1)
            with dve.Else():
                pass
            dve.sem_inc(mx_made, 1)
            n_m = 8 * 6 + 1 + NT
            dve.wait_ge(ms_full, n_m + 1)
            dve.tensor_copy(MXT[0:2 * NT, :], bank(4 + n_m % 4)[0:2 * NT, 0:P]).then_inc(ms_free, 1)
            dve.wait_ge(ms_free, n_m + 1)
            dve.sem_inc(mxt_made, 1)

            def region_of(k, it):
                r = 8 * k + it
                return PS[:, (r // 3) * BANK + (r % 3) * (P + 1):(r // 3) * BANK + (r % 3 + 1) * (P + 1)]

            OTr = OT[:, :].rearrange("p (t c) -> p t c", c=P)

            def row_parts(q, general):
                for k in range(2):
                    dve.wait_ge(src_full, 2 * q + (k + 1))
                    dve.wait_ge(q_made, 64 * q)
                    src = PS[:, 6 * BANK:8 * BANK]
                    b1_, b2_ = Bx[:, k, 0, :], Bx[:, k, 1, :]
                    if general:
                        dve.wait_ge(smax_in, 32 * q + 32)
                        dve.tensor_tensor(b1_, src, b2_, ALU.add).then_inc(ch, 1)
                    else:
                        dve.tensor_scalar(b1_, src, ext[:, 4 + k:5 + k], None, ALU.add).then_inc(ch, 1)
                    dve.wait_ge(ch, 14 * q + (3 * k + 1))
                    dve.scalar_tensor_tensor(out=b2_, in0=b1_, scalar=0.01, in1=b1_, op0=ALU.mult, op1=ALU.max)\
                        .then_inc(ch, 1)
                    dve.wait_ge(ch, 14 * q + (3 * k + 2))
                    dve.tensor_tensor(b1_, src, b2_, ALU.subtract).then_inc(ch, 1)
                    dve.scalar_tensor_tensor(out=b2_, in0=src, scalar=0.01, in1=b2_, op0=ALU.mult,
                                             op1=ALU.subtract).then_inc(b_made, 1)
                    dve.wait_ge(ch, 14 * q + (3 * k + 3))
                    dve.wait_ge(b_made, 2 * q + (k + 1))
                    dve.sem_inc(src_used, 1)

            def mask_of(q, s):
                b, w = (s // 4) % NBUF, s % 2
                if s % 4 == 0:
                    dve.wait_ge(a_in[b], 16 * (USES_L2 + s // 16 + 1) + 32 * q)
                dve.wait_ge(p_made[1], 32 * q + max(s - 1, 0))
                dve.tensor_scalar(Mt[:, w, :], A[b][:, (s % 4) * QC:(s % 4 + 1) * QC], 0.0, None, ALU.is_gt)\
                    .then_inc(mask_made, 1)
                dve.wait_ge(mask_made, 32 * q + (s + 1))
                if s < 8:
                    d = Mt[:, w, s * P:(s + 1) * P]
                    dve.tensor_tensor(d, d, identb[:, :], ALU.max).then_inc(ch, 1)
                    dve.wait_ge(ch, 14 * q + (7 + s))

            def chunks(general):
                row_parts(0, general)
                with dve.Fori(0, 4) as q:
                    for s in range(32):
                        w = s % 3
                        if s == 0:
                            mask_of(q, 0)
                        for k in range(2):
                            dve.wait_ge(q_made, 64 * q + (2 * s + k + 1))
                            if general:
                                dve.tensor_scalar(QB[:, k, :], QB[:, k, :], 1.0, None, ALU.min).then_inc(gen_q, 1)
                                dve.wait_ge(gen_q, 64 * q + (2 * s + k + 1))
                            dve.scalar_tensor_tensor(out=QA[:, w, k, :], in0=QA[:, w, k, :], scalar=1.0,
                                                     in1=QB[:, k, :], op0=ALU.min, op1=ALU.max).then_inc(r_made, 1)
                        dve.wait_ge(r_made, 64 * q + (2 * s + 1))
                        dve.tensor_tensor(QA[:, w, 0, :], QA[:, w, 0, :], Mt[:, s % 2, :], ALU.mult)\
                            .then_inc(p_made[0], 1)
                        if s < 31:
                            mask_of(q, s + 1)
                    with dve.If(q < 3):
                        row_parts(dve.snap(q + 1), general)
                    with dve.Else():
                        pass
                    dve.wait_ge(p_used, 64 * q + 68)
                    for k in range(2):
                        for it in range(8):
                            r = region_of(k, it)
                            dve.reciprocal(rden[:, 8 * k + it:8 * k + it + 1],
                                           r[:, P:P + 1] if k == 0 else r[:, 0:1]).then_inc(rd_made, 1)
                    for k in range(2):
                        for it in range(8):
                            r = region_of(k, it)
                            dve.wait_ge(rd_made, 16 * q + (8 * k + it + 1))
                            dst = V if k == 0 else OTr
                            dve.scalar_tensor_tensor(out=dst[:, ds(8 * q + it, 1), :].squeeze(1),
                                                     in0=r[:, 0:P] if k == 0 else r[:, 1:P + 1],
                                                     scalar=rden[:, 8 * k + it:8 * k + it + 1],
                                                     in1=X[:, ds(8 * q + it, 1), :].squeeze(1),
                                                     op0=ALU.mult, op1=ALU.add).then_inc(att_out, 1)
                    dve.wait_ge(att_out, 16 * q + 16)

            with dve.If(flag > 0):
                chunks(True)
            with dve.Else():
                chunks(False)
            normalise(V, V, 0)
            normalise(OTr, OTr, 1)
            n_m += 1 + 16
            for g in range(16):
                m = bank(4 + (n_m + g) % 4)
                if g >= 4:
                    dve.wait_ge(e_exp, g - 3)
                dve.wait_ge(ms_full, n_m + g + 1)
                dve.tensor_scalar(e_t[:, g % 4, :], m, 0.0, None, ALU.min).then_inc(e_neg, 1)
                dve.tensor_scalar(r_t[:, g % 4, :], m, 0.0, None, ALU.max).then_inc(ms_free, 1)
                if g >= 1:
                    elu_end(dve, g - 1, own, did, after)
            elu_end(dve, 15, own, did, after)
            normalise(X, X)
            dve.sem_inc(x_ready, 1)
            if upto == 1:
                return

            dve.sem_inc(n_made, 1)
            did(dve.reciprocal(cols[:, 10:11], cols[:, 8:9]))
            after(did(dve.reciprocal(cols[:, 11:12], cols[:, 9:10])))
            after(did(dve.tensor_scalar(cols[:, 11:12], cols[:, 11:12], -(0.5 ** 0.5), None, ALU.mult)))
            after(did(dve.tensor_tensor(cols[:, 12:13], cols[:, 10:11], cols[:, 11:12], ALU.mult)))
            dve.sem_inc(inv_made, 1)
            dve.wait_ge(l2c_in, 16)
            dve.wait_ge(dd_made, 1)
            n_m = 114 + 8
            for g in range(8):
                dve.wait_ge(ms_full, n_m + g + 1)
                m = bank(4 + (n_m + g) % 4).rearrange("p (t c) -> p t c", c=P)
                dve.tensor_tensor(V[:, 4 * g:4 * g + 4, :], m, BB.unsqueeze(1).broadcast_to([P, 4, P]), ALU.add)\
                    .then_inc(ms_free, 1)
            dve.wait_ge(ms_free, n_m + 8)
            dve.sem_inc(v_ready, 1)

            def newton(k, n):
                dve.wait_ge(t_made, 8 * n + (k + 1))
                dve.scalar_tensor_tensor(out=U[:, k, :], in0=T[:, k % 2, :], scalar=2.0, in1=U[:, k, :],
                                         op0=ALU.subtract, op1=ALU.mult).then_inc(n_made, 1)

            def square(k, n):
                i = 2 * DVE_SQUARES.index(k)
                u = U[:, k, :]
                dve.wait_ge(n_made, 8 * n + (k + 2))
                dve.tensor_scalar(u, u, cols[:, 11:12], cols[:, 12:13], ALU.mult, ALU.add).then_inc(sq_own, 1)
                dve.wait_ge(sq_own, len(DVE_SQUARES) * n + (i // 2 + 1))
                dve.tensor_tensor(u, u, u, ALU.mult).then_inc(sqd_made, 1)

            def cut(k, n):
                b, jj = k // 2, k % 2
                a = A[b][:, jj * HALF:(jj + 1) * HALF]
                dve.wait_ge(a_in[b], 16 * n + 16 * (USES_L2 + A_L1 + 1))
                dve.scalar_tensor_tensor(out=a, in0=a, scalar=0.5, in1=a, op0=ALU.is_lt, op1=ALU.mult)\
                    .then_inc(s_own, 1)
                dve.wait_ge(s_own, 8 * n + (k + 1))
                if isinstance(n, int):
                    col, diag = (8 * n + k) % 16 * P, (n % 4) // 2 * P
                    d, dd = a[:, col:col + P], DD[:, diag:diag + P]
                else:
                    d = A[b][:, ds(dve.snap((n * 8 + k) % 16 * P + jj * HALF, max_val=31 * P), P)]
                    dd = DD[:, ds(dve.snap((n % 4) // 2 * P, max_val=P), P)]
                dve.tensor_tensor(d, d, dd, ALU.mult).then_inc(s_made, 1)

            def newtons(first, n):
                for k in range(first, first + 4):
                    newton(k, n)
                    if k in DVE_SQUARES:
                        square(k, n)

            def cuts(first, n):
                for k in range(first, first + 4):
                    cut(k, n)

            cuts(0, 0)
            cuts(4, 0)
            newtons(0, 0)
            with dve.Fori(0, 2 * ITERS - 1) as n:
                for first in range(0, 8, 4):
                    cuts(first, n + 1)
                    newtons(4 - first, n if first == 0 else n + 1)
            newtons(4, 2 * ITERS - 1)
            add_misc(n_m + 8)
            normalise(X, X)
            dve.sem_inc(x_ready, 1)
            if upto == 2:
                return

            own_l = [0]

            def lists(ins, n=None):
                own_l[0] += 1
                ins.then_inc(lw, 1)
                dve.wait_ge(lw, own_l[0] if n is None else n + own_l[0])
                if n is not None:
                    settled(dve)

            dve.wait_ge(cand_in, 16)
            dve.wait_ge(seg_made, 2)
            lists(dve.tensor_reduce(bad[:, 1:2], cand2.rearrange("p t (j e) -> p (t j) e", e=8)[:, :, 7], AX.X, ALU.max))
            lists(dve.memset(bad[:, 2:3], 0.0))
            base = own_l[0]
            STEPS = 9
            with dve.Fori(0, NT) as t:
                own_l[0] = base
                at_ = t * STEPS
                c = cand2[:, ds(t, 1), :].squeeze(1)
                lists(dve.scalar_tensor_tensor(out=K1, in0=c, scalar=0.0, in1=segb, op0=ALU.is_gt, op1=ALU.mult), at_)
                lists(dve.tensor_tensor(K1, K1, c, ALU.add), at_)
                lists(dve.max(m8x[:, 0:8], K1), at_)
                lists(dve.match_replace(out=K2, in_to_replace=m8x[:, 0:8], in_values=K1, imm_value=0.0), at_)
                lists(dve.max(m8x[:, 8:16], K2), at_)
                lists(dve.match_replace(out=K1, in_to_replace=m8x[:, 8:16], in_values=K2, imm_value=0.0), at_)
                lists(dve.max(m8x[:, 16:24], K1), at_)
                lists(dve.tensor_copy(LST[:, ds(t, 1), :].squeeze(1), m8x[:, 0:REST]), at_)
                lists(dve.tensor_tensor(bad[:, 2:3], bad[:, 2:3], m8x[:, REST:REST + 1], ALU.max), at_)
            own_l[0] = base + STEPS * NT
            flat = LST.rearrange("p t e -> p (t e)")
            tmp = r1[:, 0:NT * REST]
            lists(dve.tensor_scalar(tmp, flat, 0.0, float(N + 1), ALU.is_equal, ALU.mult))
            lists(dve.tensor_copy(lists_any.rearrange("p (t g) -> p t g", t=NT), LST[:, :, 0:REST:STEP]))
            dve.scalar_tensor_tensor(out=IDX.rearrange("p t e -> p (t e)"), in0=flat, scalar=-1.0, in1=tmp,
                                     op0=ALU.add, op1=ALU.add).then_inc(idx_made, 1)
            dve.memset(K1[:, 0:P], 0.0).then_inc(zero_made, 1)

            dve.wait_ge(v_ready, 8)
            dve.wait_ge(idx_made, 1)
            dve.wait_ge(part_a, 1)
            Vf = V[:, :, :].rearrange("p t c -> p (t c)")
            dve.tensor_tensor(r1, Vf, OP[:, 0, :, :].rearrange("p t c -> p (t c)"), ALU.subtract).then_inc(part_d, 1)
            dve.wait_ge(part_d, 1)
            dve.wait_ge(part_a, 2)
            dve.tensor_tensor(r1, r1, OP[:, 1, :, :].rearrange("p t c -> p (t c)"), ALU.subtract).then_inc(part_d, 1)
            dve.wait_ge(tab_out, 32)
            dve.wait_ge(ot_ready, 51)
            dve.wait_ge(v_ready, 8)
            after(did(dve.memset(OT[:, :], 0.0)))
            dve.sem_inc(px_free, 2)
            more = [dve.alloc_register(f"more{w}") for w in range(2)]
            for w in range(2):
                dve.reg_mov(more[w], 0)
            dve.wait_ge(used_made, 2)
            after(did(dve.tensor_reduce(rowm, lists_all.rearrange("p (t g) -> p t g", t=NT)[:, :, (REST - SPARE) // STEP:],
                                        AX.X, ALU.add)))
            after(did(dve.tensor_copy(steps, rowm)))

            def landed(t, w, r):
                dve.wait_ge(g_in[w], 16 * (REST - SPARE) * r + 16 * (REST - SPARE))
                dve.wait_ge(g_seen[w], SPARE // STEP * r + SPARE // STEP)
                cell = steps[0:1, t:t + 1] if isinstance(t, int) else steps[0:1, ds(t, 1)]
                taken = dve.value_load(cell, min_val=0, max_val=SPARE // STEP)
                dve.reg_add(more[w], more[w], dve.to_reg(dve.snap(taken * (16 * STEP))))
                with dve.If(taken > 0):
                    dve.wait_ge(g_more[w], more[w])
                    settled(dve)
                with dve.Else():
                    pass

            def greatest(t, w, part):
                c = slice(part * P // 4, (part + 1) * P // 4)
                v = V[:, t, c] if isinstance(t, int) else V[:, ds(t, 1), c].squeeze(1)
                ins = dve.tensor_reduce(v, G[:, w, :, c].rearrange("p k c -> p c k"), AX.X, ALU.max)
                if part == 3:
                    ins.then_inc(g_used[w], 1)

            with dve.Fori(0, 2 * ITERS) as n:
                half = OT[:, ds(n // ITERS * HALF, HALF)]
                for g in range(NGRP):
                    b = g // (2 * SLOTS)
                    full = 2 * SLOTS - 1
                    if g % (2 * SLOTS) == full:
                        dve.wait_ge(a_out[b], n + (USES_POOL + 1))
                    else:
                        dve.wait_ge(px_full, n * (NBUF * full) + (b * full + g % (2 * SLOTS) + 1))
                    dve.wait_ge(px_free, NGRP * n + (g + 2))
                    src = PS[:, 4 * (g % 2) * BANK:(4 * (g % 2) + 4) * BANK]
                    dve.tensor_tensor(half, half, src, ALU.max).then_inc(px_free, 1)
                    w = (g // 4 + 1) % 2
                    if g > 3:
                        t = dve.snap(4 * n + (g // 4 - 1))
                        if g % 4 == 0:
                            landed(t, w, dve.snap(2 * n + (g // 4 - 1) // 2))
                        greatest(t, w, g % 4)
                    else:
                        with dve.If(n > 0):
                            t = dve.snap((4 * n + (NT - 1)) % NT)
                            if g % 4 == 0:
                                landed(t, w, dve.snap((2 * n + (NT // 2 - 1)) % (NT // 2)))
                            greatest(t, w, g % 4)
                        with dve.Else():
                            pass
            landed(NT - 1, 1, NT // 2 - 1)
            for part in range(4):
                greatest(NT - 1, 1, part)
            dve.wait_ge(px_free, NGRP * 2 * ITERS + 2)
            for w in range(2):
                dve.wait_ge(g_used[w], NT // 2)
            dve.sem_inc(x_ready, 1)
            n_m = 162
            for g in range(8):
                dve.wait_ge(ms_full, n_m + g + 1)
                m = bank(4 + (n_m + g) % 4).rearrange("p (t c) -> p t c", c=P)
                dve.tensor_tensor(V[:, 4 * g:4 * g + 4, :], V[:, 4 * g:4 * g + 4, :], m, ALU.max)\
                    .then_inc(ms_free, 1)
            dve.wait_ge(ms_free, n_m + 8)
            after(did(dve.tensor_reduce(rowm, V[:, :, :], AX.X, ALU.max)))
            after(did(dve.tensor_reduce(bad[:, 3:4], rowm, AX.X, ALU.min)))
            after(did(dve.tensor_scalar(bad[:, 3:4], bad[:, 3:4], 0.0, None, ALU.is_equal)))
            after(did(dve.tensor_reduce(bad[:, 0:1], bad[:, 1:4], AX.X, ALU.max)))
            dve.sem_inc(bad_made, 1)
            dve.wait_ge(bad_all, 1)
            dve.tensor_scalar(bad[:, 8:9].bitcast(I32), bad[:, 4:5], limit, None, ALU.is_gt).then_inc(flag2, 1)
            dve.wait_ge(flag2, 1)
            flag = dve.value_load(bad[0:1, 8:9].bitcast(I32), min_val=0, max_val=1)
            with dve.If(flag > 0):
                tmpv = A[2][:, :].rearrange("p (c j) -> p c j", j=32)
                part = A[3][:, 0:P]
                msk = A[3][:, P:P + 32]
                has = A[3][:, 2 * P:2 * P + 1]
                hc = A[3][:, 2 * P + 1:2 * P + 2]
                with dve.Fori(0, NT) as t:
                    v = V[:, ds(t, 1), :].squeeze(1)
                    t0 = t * (5 * 4 * NT + 4)
                    dve.tensor_copy(v, K1[:, 0:P]).then_inc(dn, 1)
                    dve.memset(has, 0.0).then_inc(dn, 1)
                    with dve.Fori(0, 4 * NT) as c:
                        c0 = t0 + c * 5
                        dve.wait_ge(dn, t0 + 2)
                        dve.wait_ge(dn_in, 32 * (t * (4 * NT) + c + 1))
                        dve.tensor_scalar(msk, A[1][:, 0:32], 0.0, None, ALU.not_equal).then_inc(dn, 1)
                        dve.wait_ge(dn, c0 + 3)
                        dve.tensor_tensor(tmpv, A[0][:, :].rearrange("p (j c) -> p c j", c=P),
                                          msk.unsqueeze(1).broadcast_to([P, P, 32]), ALU.mult).then_inc(dn, 1)
                        dve.tensor_reduce(hc, msk, AX.X, ALU.max).then_inc(dn, 1)
                        dve.wait_ge(dn, c0 + 5)
                        dve.sem_inc(dn_used, 2)
                        dve.tensor_reduce(part, tmpv, AX.X, ALU.max).then_inc(dn, 1)
                        dve.tensor_tensor(has, has, hc, ALU.max).then_inc(dn, 1)
                        dve.wait_ge(dn, c0 + 7)
                        dve.tensor_tensor(v, v, part, ALU.max).then_inc(dnv, 1)
                        dve.wait_ge(dnv, t * (4 * NT) + c + 1)
                    t1 = t0 + 5 * 4 * NT
                    dve.tensor_scalar(has, has, -1.0, BIG, ALU.add, ALU.mult).then_inc(dn, 1)
                    dve.wait_ge(dn, t1 + 3)
                    dve.tensor_scalar(v, v, has, None, ALU.add).then_inc(dn, 1)
                    dve.wait_ge(dn, t1 + 4)
            with dve.Else():
                pass
            after(did(dve.tensor_tensor(X[:, :, :], X[:, :, :], V[:, :, :], ALU.add)))
            normalise(X, X)
            dve.sem_inc(x_ready, 1)


_INS = ["x", "xT", "adj", "adjT", "W1", "f1", "W2", "f2", "ff0", "ff0T", "ff1T", "attc", "g1", "b1", "g2", "b2",
        "L2W", "L2B", "mu", "sigma", "L3W", "L3b"]


def laid_out(x, adj, L0_gnn_W1, L0_gnn_f1, L0_gnn_W2, L0_gnn_f2, L1_gnn_ff0_w, L1_gnn_ff1_w, L1_gnn_attn_w,
             L1_gnn_g1, L1_gnn_b1, L1_gnn_g2, L1_gnn_b2, L2_gnn_W, L2_gnn_B, L2_gnn_mu, L2_gnn_sigma,
             L3_gnn_weight, L3_gnn_bias):
    import numpy as np

    def a(v):
        return np.asarray(v)

    return {
        "x": a(x), "xT": a(x).T, "adj": a(adj), "adjT": a(adj).T,
        "W1": a(L0_gnn_W1), "f1": a(L0_gnn_f1).reshape(NT, P).T, "W2": a(L0_gnn_W2),
        "f2": a(L0_gnn_f2).reshape(NT, P).T,
        "ff0": a(L1_gnn_ff0_w), "ff0T": a(L1_gnn_ff0_w).transpose(0, 2, 1),
        "ff1T": a(L1_gnn_ff1_w).transpose(0, 2, 1),
        "attc": a(L1_gnn_attn_w).reshape(4, P).T,
        "g1": a(L1_gnn_g1).reshape(P, 1), "b1": a(L1_gnn_b1).reshape(P, 1),
        "g2": a(L1_gnn_g2).reshape(P, 1), "b2": a(L1_gnn_b2).reshape(P, 1),
        "L2W": a(L2_gnn_W), "L2B": a(L2_gnn_B).reshape(1, P),
        "mu": a(L2_gnn_mu), "sigma": a(L2_gnn_sigma),
        "L3W": a(L3_gnn_weight), "L3b": a(L3_gnn_bias).reshape(P, 1),
    }


def kernel(**inputs):
    import numpy as np
    import concourse.bacc as bacc
    from concourse.bass_utils import run_bass_kernel_spmd as run

    nc = bacc.Bacc("TRN2", target_bir_lowering=False, num_devices=1)
    arrays, args = {}, []
    for name, v in laid_out(**inputs).items():
        arrays[f"in_{name}"] = np.ascontiguousarray(v)
        args.append(nc.dram_tensor(f"in_{name}", v.shape, mybir.dt.from_np(v.dtype), kind="ExternalInput").ap())
    args.append(nc.dram_tensor("out", (N, P), F32, kind="ExternalOutput").ap())
    program(nc, *args)
    r = run(nc, [arrays], core_ids=[0])
    return r.results[0]["out"]
```

```python
from contextlib import ExitStack

import concourse.bass as bass
from concourse import mybir

P = 128
N = 4096
NT = N // P
HALF = N // 2
BANK = 512
NBUF = 4
ITERS = HALF // BANK
SLOTS = 2
REST = 16
SPARE = 8
STEP = 2
QC = 1024
RANK = 200.0
DVE_SQUARES = (0, 2, 4, 6)
POOL_BOTH = range(1, 32, 2)
SPREAD = 60.0
EPS = 1e-5
BIG = 3.4028234663852886e38
TINY = 1e-15

F32 = mybir.dt.float32
BF16 = mybir.dt.bfloat16
FP8 = mybir.dt.float8e4
I32 = mybir.dt.int32
U32 = mybir.dt.uint32
ALU = mybir.AluOpType
ACT = mybir.ActivationFunctionType
AX = mybir.AxisListType
RMAX = bass.bass_isa.ReduceOp.max
ds = bass.ds

USES_L0 = 0
USES_L2 = 4 * 2 * ITERS
USES_L3 = USES_L2 + 2 * ITERS
USES_POOL = USES_L3 + 2 * ITERS
L1_LOADS = 4 * 8


def program(nc, x, xT, adj, adjT, W1, f1, W2, f2, ff0, ff0T, ff1T, attc, g1, b1, g2, b2,
            L2W, L2B, mu, sigma, L3W, L3b, out):
    with ExitStack() as ctx:
        def sb(name, shape, dt=F32):
            return ctx.enter_context(nc.sbuf_tensor(name, shape, dt))

        def sem(name):
            return ctx.enter_context(nc.semaphore(name))

        onehot_d = nc.dram_tensor("onehot_d", (SLOTS * NT * 2 * P, HALF // 4), F32, kind="Internal").ap()
        cand_d = nc.dram_tensor("cand_d", (P, NT * NT * 8), BF16, kind="Internal").ap()
        smax_d = nc.dram_tensor("smax_d", (2 * NT, P), F32, kind="Internal").ap()
        table_d = nc.dram_tensor("table_d", (N + P, P), F32, kind="Internal").ap()

        A = [sb(f"A{b}", [P, N]) for b in range(NBUF)]
        X = sb("X", [P, NT, P])
        V = sb("V", [P, NT, P])
        OT = sb("OT", [P, N])
        VS = sb("VS", [P, NBUF, 2, P])
        ident = sb("ident", [P, P])
        notid = sb("notid", [P, P])
        identb = sb("identb", [P, P], BF16)
        rankw = sb("rankw", [P, P], BF16)
        Wt = sb("Wt", [P, 4, P])
        RH = sb("RH", [P, 2 * P + 5])
        ff1s = sb("ff1s", [P, 2, P])
        cols = sb("cols", [P, 16])
        SRt = sb("SRt", [P, 2, P])
        fcol = sb("fcol", [P, 2, NT])
        st6 = sb("st6", [P, 2, NT, 6])
        mv = sb("mv", [P, 2, NT, 2])
        rstd = sb("rstd", [P, 2, NT])
        REGION = 21184
        R = sb("R", [P, REGION])

        def region(at, words, dt=F32):
            v = R[:, at:at + words]
            return v if dt == F32 else v.bitcast(dt)

        PS = ctx.enter_context(nc.psum_tensor("PS", [P, 8 * BANK], F32))
        acc = PS[:, 0:4 * BANK]

        def bank(k, n=BANK):
            return PS[:, k * BANK:k * BANK + n]

        w1_in = sem("w1_in")
        w_in = sem("w_in")
        x_in = sem("x_in")
        consts = sem("consts")
        a_in = [sem(f"a_in{b}") for b in range(NBUF)]
        a_out = [sem(f"a_out{b}") for b in range(NBUF)]
        vs_in = [sem(f"vs_in{b}") for b in range(NBUF)]
        v_ready = sem("v_ready")
        acc_free = sem("acc_free")
        ot_ready = sem("ot_ready")
        ms_full = sem("ms_full")
        ms_free = sem("ms_free")
        mk = [sem(f"mk{w}") for w in range(2)]
        y_done = sem("y_done")
        y_act = sem("y_act")
        k_made = sem("k_made")
        t_done = sem("t_done")
        m8_done = sem("m8_done")
        c_cp = [sem(f"c_cp{w}") for w in range(2)]
        s_st = [[sem(f"s_st{w}{k}") for k in range(2)] for w in range(2)]
        cand_out = sem("cand_out")
        dv = sem("dv")
        ln_var = sem("ln_var")
        ln_std = sem("ln_std")
        ln_mean = sem("ln_mean")
        ln_dve = sem("ln_dve")
        ln_act = sem("ln_act")
        x_ready = sem("x_ready")
        out_st = sem("out_st")
        h_made = sem("h_made")
        sr_made = sem("sr_made")
        ext_made = sem("ext_made")
        ext_all = sem("ext_all")
        flag_made = sem("flag_made")
        gen_in = sem("gen_in")
        gen_used = sem("gen_used")
        mx_made = sem("mx_made")
        mxt_made = sem("mxt_made")
        smax_out = sem("smax_out")
        smax_in = sem("smax_in")
        src_full = sem("src_full")
        src_used = sem("src_used")
        b_made = sem("b_made")
        q_made = sem("q_made")
        mask_made = sem("mask_made")
        r_made = sem("r_made")
        p_dve = sem("p_dve")
        p_pool = sem("p_pool")
        row_exp = sem("row_exp")
        dst_exp = sem("dst_exp")
        p_used = sem("p_used")
        rd_made = sem("rd_made")
        att_out = sem("att_out")
        qt_made = sem("qt_made")
        e_neg = sem("e_neg")
        e_exp = sem("e_exp")
        e_used = sem("e_used")
        row_neg = sem("row_neg")
        ch_rows = sem("ch_rows")
        ch = sem("ch")
        gen_own = sem("gen_own")
        gen_row = sem("gen_row")
        gen_q = sem("gen_q")
        l2c_in = sem("l2c_in")
        dd_made = sem("dd_made")
        lnr = sem("lnr")
        u_made = sem("u_made")
        t_made = sem("t_made")
        n_made = sem("n_made")
        sq_made = sem("sq_made")
        sqd_made = sem("sqd_made")
        sq_own = sem("sq_own")
        e_made = sem("e_made")
        s_own = sem("s_own")
        s_made = sem("s_made")
        inv_made = sem("inv_made")
        cand_in = sem("cand_in")
        seg_made = sem("seg_made")
        lw = sem("lw")
        idx_made = sem("idx_made")
        used_made = sem("used_made")
        zero_made = sem("zero_made")
        tab_out = sem("tab_out")
        part_a = sem("part_a")
        part_d = sem("part_d")
        ix_cp = sem("ix_cp")
        g_in = [sem(f"g_in{w}") for w in range(2)]
        g_more = [sem(f"g_more{w}") for w in range(2)]
        g_seen = [sem(f"g_seen{w}") for w in range(2)]
        g_used = [sem(f"g_used{w}") for w in range(2)]
        px_full = sem("px_full")
        px_free = sem("px_free")
        bad_made = sem("bad_made")
        bad_all = sem("bad_all")
        flag2 = sem("flag2")
        dn_in = sem("dn_in")
        dn_used = sem("dn_used")
        dn = sem("dn")
        dnv = sem("dnv")

        block = ctx.enter_context(nc.Block())

        def settled(engine):
            engine.nop(nofuse=True)

        class Run:
            def __init__(self):
                self.n = 0

        Vb = region(0, 4096).rearrange("p (t c) -> p t c", c=P)
        Mk = region(4096, 2048, BF16).rearrange("p (w n) -> p w n", w=2)
        M01 = region(6144, 2048, BF16).rearrange("p (w n) -> p w n", w=2)
        Kb = region(8192, 512, BF16).rearrange("p (w n) -> p w n", w=2)
        SB = region(8704, 2048, FP8).rearrange("p (w k n) -> p w k n", w=2, k=2)
        SBw = region(8704, 2048).rearrange("p (w k n) -> p w k n", w=2, k=2)
        m8 = region(10752, 128, BF16).rearrange("p (w t e) -> p w t e", w=2, e=8)
        cand = region(10880, 4096, BF16).rearrange("p (t j e) -> p t j e", t=NT, j=NT)
        xT_s = OT

        HW = 2 * P + 5
        Hs = region(0, NT * HW).rearrange("p (t c) -> p t c", c=HW)
        at = NT * HW
        Bx = region(at, 4 * QC).rearrange("p (k e n) -> p k e n", k=2, e=2)
        at += 4 * QC
        QA = region(at, 6 * QC).rearrange("p (w k n) -> p w k n", w=3, k=2)
        QB = region(at + 6 * QC, 2 * QC).rearrange("p (k n) -> p k n", k=2)
        QT = region(at, 8 * QC).rearrange("p (k n) -> p k n", k=2)
        at += 8 * QC
        dst2 = region(at, 2 * NT).rearrange("p (t k) -> p t k", k=2)
        MX = region(at + 2 * NT, 2 * NT).rearrange("p (k t) -> p k t", k=2)
        MXT = region(at + 4 * NT, P)
        ext = region(at + 4 * NT + P, 24)
        at += 4 * NT + P + 24
        attw = region(at, 4)
        rden = region(at + 4, 16)
        assert at + 20 <= REGION
        Mt = VS[:, :, :, :].rearrange("p a b c -> p (a b c)").bitcast(BF16).rearrange("p (w n) -> p w n", w=2)

        U = region(0, 8 * HALF).rearrange("p (w n) -> p w n", w=8)
        T = region(8 * HALF, 2 * HALF).rearrange("p (w n) -> p w n", w=2)
        BB = region(10 * HALF, P)
        DD = region(10 * HALF + 3 * P, 2 * P)

        OP = region(0, 3 * NT * P // 2, BF16).rearrange("p (e t c) -> p e t c", e=3, t=NT)
        OPw = region(0, 3 * NT * P // 2).rearrange("p (e t c) -> p e t c", e=3, t=NT)
        HOTW = HALF * SLOTS // 2
        pat = 3 * NT * P // 2
        cand2 = region(pat, 4096, BF16).rearrange("p (t n) -> p t n", t=NT)
        r1 = region(pat + 4096, 4096)
        G = region(pat + 8192, 2 * REST * P).rearrange("p (w k c) -> p w k c", w=2, k=REST)
        pat += 8192 + 2 * REST * P
        LST = region(pat, NT * REST).rearrange("p (t e) -> p t e", e=REST)
        IDX = region(pat + NT * REST, NT * REST, U32).rearrange("p (t e) -> p t e", e=REST)
        pat += 2 * NT * REST
        K1 = region(pat, 256)
        K2 = region(pat + 256, 256)
        segb = region(pat + 512, 256)
        segi = region(pat + 768, 256, I32)
        pat += 1024
        m8x = region(pat, 32)
        ixs = region(pat + 32, 2 * REST, U32).rearrange("p (w e) -> p w e", w=2)
        bad = region(pat + 64, 16)
        rowm = region(pat + 80, NT)
        assert pat + 80 + NT <= REGION
        steps = m8x.bitcast(I32)
        assert NT * REST // STEP <= 256
        lists_any, lists_all, used = K2[:, 0:NT * REST // STEP], segb[:, 0:NT * REST // STEP], segi[:, 0:NT * REST // STEP]
        e_t = region(4 * HALF, 4 * BANK).rearrange("p (w n) -> p w n", w=4)

        def by_pool(s):
            return s + 1 + sum(i <= s for i in POOL_BOTH)

        def by_dve(s):
            return s + 1 - sum(i <= s for i in POOL_BOTH)

        def v_of(p):
            return V[:, :, :] if p % 2 == 0 else Vb

        def swapped(p):
            return 1 if p >= 2 else 0

        def blk(h, it, b):
            return (16 * h + 8 * it + 2 * b) % NT

        NGRP = NBUF * 2 * SLOTS
        A_L1 = 2 * ITERS

        @block.sync
        def _(sp):
            sp.dma_start(xT_s[:, :], xT).then_inc(x_in, 16)

            def load_A(b, j, h):
                sp.dma_start(A[b][:, :].rearrange("p (k n) -> p k n", k=2),
                             adjT[ds(j * P, 2 * P), ds(h * HALF, HALF)].rearrange("(k p) n -> p k n", p=P))\
                    .then_inc(a_in[b], 16)

            def load_V(b, j, v):
                sp.dma_start(VS[:, b, :, :], v[:, ds(j, 2), :]).then_inc(vs_in[b], 16)

            def product_loads(u0, v, swap, ready, units, aofs=0):
                for b in range(NBUF):
                    if aofs and b == 0:
                        sp.wait_ge(mask_made, L1_LOADS * 4)
                    sp.wait_ge(a_out[b], u0)
                    if units and b % 2 == 0:
                        sp.wait_ge(mk[b // 2], u0)
                    load_A(b, blk(0, 0, b ^ swap), 0)
                sp.wait_ge(v_ready, ready - 1 if units else ready)
                for b in range(NBUF):
                    load_V(b, blk(0, 0, b ^ swap), v)
                sp.wait_ge(v_ready, ready)
                with sp.Fori(1, 2 * ITERS) as n:
                    h = sp.snap(n // ITERS)
                    first = sp.snap((n * 8 + h * 16) % NT, max_val=NT - 8)
                    for b in range(NBUF):
                        j = sp.snap(first + 2 * (b ^ swap), max_val=NT - 2)
                        sp.wait_ge(a_out[b], n + u0)
                        if units and b % 2 == 0:
                            sp.wait_ge(mk[b // 2], n + u0)
                        load_A(b, j, h)
                        load_V(b, j, v)

            for p in range(4):
                product_loads(USES_L0 + 2 * ITERS * p, v_of(p), swapped(p), 2 * p + 2, True)
                if p == 0:
                    sp.dma_start(X[:, :, :], x.rearrange("(t p) c -> p t c", p=P)).then_inc(x_in, 16)
            for w in range(2):
                sp.wait_ge(c_cp[w], USES_L2)
            sp.dma_start(cand_d, cand.rearrange("p t j e -> p (t j e)")).then_inc(cand_out, 16)

            def load_chunk(b, q, j0):
                sp.dma_start(A[b][:, :].rearrange("p (k n) -> p k n", k=4),
                             adjT[ds(j0 * P, 4 * P), ds(q * QC, QC)].rearrange("(k p) n -> p k n", p=P))\
                    .then_inc(a_in[b], 16)

            sp.wait_ge(flag_made, 1)
            flag = sp.value_load(ext[0:1, 12:13].bitcast(I32), min_val=0, max_val=1)
            for b in range(NBUF):
                sp.wait_ge(a_out[b], USES_L2)
            with sp.If(flag > 0):
                for k in range(2):
                    sp.dma_start(smax_d[k * NT:(k + 1) * NT, :].rearrange("t p -> p t"),
                                 Hs[:, :, 2 * P + 2 + 2 * k], allow_slow_non_contiguous=True).then_inc(gen_in, 16)
                sp.wait_ge(gen_in, 32)
                for k in range(2):
                    sp.dma_start(A[1 + k][:, :],
                                 smax_d[k * NT:(k + 1) * NT, :].rearrange("(a t) p -> a (t p)", a=1).partition_broadcast(P))\
                        .then_inc(gen_in, 16)
                with sp.Fori(0, NT) as t:
                    sp.wait_ge(gen_used, t)
                    sp.dma_start(A[0][:, :], adj[ds(t * P, P), :]).then_inc(gen_row, 16)
                sp.wait_ge(gen_used, NT)
            with sp.Else():
                pass
            sp.wait_ge(mxt_made, 1)
            sp.dma_start(smax_d, MXT[0:2 * NT, :]).then_inc(smax_out, 16)
            sp.wait_ge(smax_out, 16)
            for b in range(NBUF):
                load_chunk(b, 0, 4 * b)
            with sp.Fori(0, 4) as q:
                with sp.If(flag > 0):
                    sp.wait_ge(q_made, 64 * q)
                    for k in range(2):
                        sp.dma_start(Bx[:, k, 1, :],
                                     smax_d[ds(k * NT + 8 * q, 8), :].rearrange("(a t) p -> a (t p)", a=1).partition_broadcast(P))\
                            .then_inc(smax_in, 16)
                with sp.Else():
                    pass
                for n in range(4, 8):
                    sp.wait_ge(mask_made, 32 * q + (4 * (n - 4) + 4))
                    load_chunk(n % NBUF, q, sp.snap((8 * q + 4 * n) % NT, max_val=NT - 4))
                with sp.If(q < 3):
                    for n in range(4):
                        sp.wait_ge(mask_made, 32 * q + (4 * (n + 4) + 4))
                        load_chunk(n, sp.snap((q + 1) % 4), sp.snap((8 * q + (4 * n + 8)) % NT, max_val=NT - 4))
                with sp.Else():
                    pass
            def finish(n):
                sp.wait_ge(x_ready, n)
                sp.dma_start(out.rearrange("(t p) c -> p t c", p=P), X[:, :, :]).then_inc(out_st, 16)
                sp.wait_ge(out_st, 16)


            sp.wait_ge(mask_made, L1_LOADS * 4)
            for b in range(NBUF):
                load_A(b, 2 * b, 0)
            sp.wait_ge(x_ready, 2)
            sp.dma_start(BB, L2B.partition_broadcast(P)).then_inc(l2c_in, 16)
            sp.wait_ge(v_ready, 10)
            for b in range(NBUF):
                load_V(b, 2 * b, V[:, :, :])
            with sp.Fori(1, 2 * ITERS) as n:
                h = sp.snap(n // ITERS)
                first = sp.snap((n * 8 + h * 16) % NT, max_val=NT - 8)
                for step in range(NBUF + 2):
                    if step < NBUF:
                        sp.wait_ge(t_made, 8 * n + (2 * step - 6))
                        load_A(step, sp.snap(first + 2 * step, max_val=NT - 2), h)
                    if step >= 2:
                        b = step - 2
                        sp.wait_ge(a_out[b], n + USES_L2)
                        load_V(b, sp.snap(first + 2 * b, max_val=NT - 2), V[:, :, :])

            for b in range(NBUF):
                sp.wait_ge(a_out[b], USES_L3)
            sp.dma_start(cand2.rearrange("p t n -> p (t n)"), cand_d).then_inc(cand_in, 16)
            product_loads(USES_L3, V[:, :, :], 0, 11, False)
            sp.wait_ge(zero_made, 1)
            sp.dma_start(table_d[N:N + P, :], K1[:, 0:P]).then_inc(tab_out, 16)
            sp.wait_ge(v_ready, 12)
            sp.dma_start(table_d[0:N, :].rearrange("(t p) c -> p t c", p=P), V[:, :, :]).then_inc(tab_out, 16)
            one_v = onehot_d.rearrange("(k j h p) n -> p k j h n", k=SLOTS, j=NT, h=2)
            with sp.Fori(0, 2 * ITERS) as n:
                h = sp.snap(n // ITERS)
                for b in range(NBUF):
                    sp.wait_ge(a_out[b], n + USES_POOL)
                    j = sp.snap((n * 8 + 2 * b) % NT, max_val=NT - 2)
                    dst = A[b][:, 0:HOTW].rearrange("p (k j n) -> p k j n", k=SLOTS, j=2)
                    for k in range(SLOTS):
                        sp.dma_start(dst[:, k, :, :], one_v[:, k, ds(j, 2), ds(h, 1), :].rearrange("p j h n -> p j (h n)"))\
                            .then_inc(a_in[b], 16)
                    if b == 0:
                        sp.wait_ge(part_a, 3)
                    sp.dma_start(A[b][:, HOTW:HOTW + 3 * P].rearrange("p (e j c) -> p e j c", e=3, j=2),
                                 OPw[:, :, ds(j, 2), :]).then_inc(a_in[b], 16)
            sp.wait_ge(flag2, 1)
            flag = sp.value_load(bad[0:1, 8:9].bitcast(I32), min_val=0, max_val=1)
            with sp.If(flag > 0):
                with sp.Fori(0, NT) as t:
                    with sp.Fori(0, NT * 4) as c:
                        sp.wait_ge(dn_used, 2 * (t * (NT * 4) + c))
                        sp.dma_start(A[0][:, :], table_d[ds(c * 32, 32), :].rearrange("(a j) c -> a (j c)", a=1)
                                     .partition_broadcast(P)).then_inc(dn_in, 16)
                        sp.dma_start(A[1][:, 0:32], adj[ds(t * P, P), ds(c * 32, 32)]).then_inc(dn_in, 16)
            with sp.Else():
                pass
            finish(5)

        @block.gpsimd
        def _(pool):
            n = Run()

            def step(ins):
                n.n += 1
                ins.then_inc(consts, 1)
                pool.wait_ge(consts, n.n)

            pool.dma_start(Wt[:, 0, :], W1).then_inc(w1_in, 16)
            step(pool.memset(ident[:, :], 0.0))
            step(pool.affine_select(out=ident[:, :], in_=ident[:, :], compare_op=ALU.not_equal, fill=1.0,
                                    base=0, pattern=[[-1, P]], channel_multiplier=1))
            step(pool.memset(notid[:, :], 1.0))
            step(pool.affine_select(out=notid[:, :], in_=notid[:, :], compare_op=ALU.not_equal, fill=0.0,
                                    base=0, pattern=[[-1, P]], channel_multiplier=1))
            rk = R[:, 0:P]
            step(pool.memset(rk, -1.0))
            step(pool.affine_select(out=rk, in_=rk, compare_op=ALU.is_gt, fill=0.0,
                                    base=0, pattern=[[1, P]], channel_multiplier=-1))
            step(pool.affine_select(out=rk, in_=rk, compare_op=ALU.not_equal, fill=RANK,
                                    base=0, pattern=[[-1, P]], channel_multiplier=1))
            step(pool.tensor_copy(rankw[:, :], rk))
            step(pool.tensor_copy(identb[:, :], ident[:, :]))
            step(pool.memset(cols[:, 5:6], EPS))
            step(pool.memset(cols[:, 7:8], 1.0 - RANK))
            step(pool.memset(cols[:, 13:14], TINY))
            step(pool.iota(cols[:, 14:15].bitcast(I32), pattern=[[0, 1]], base=1, channel_multiplier=1))
            step(pool.tensor_copy(cols[:, 6:7], cols[:, 14:15].bitcast(I32)))
            pool.dma_start(Wt[:, 1, :], W2).then_inc(w_in, 16)
            pool.dma_start(Wt[:, 2, :], L2W).then_inc(w_in, 16)
            pool.dma_start(Wt[:, 3, :], L3W).then_inc(w_in, 16)
            pool.dma_start(fcol[:, 0, :], f1).then_inc(w_in, 16)
            pool.dma_start(fcol[:, 1, :], f2).then_inc(w_in, 16)
            for c, src in enumerate((g1, b1, g2, b2, L3b)):
                pool.dma_start(cols[:, c:c + 1], src).then_inc(w_in, 16)
            pool.dma_start(cols[:, 8:9], mu.partition_broadcast(P)).then_inc(w_in, 16)
            pool.dma_start(cols[:, 9:10], sigma.partition_broadcast(P)).then_inc(w_in, 16)
            pool.dma_start(RH[:, 0:P], ff0T[0]).then_inc(w_in, 16)
            pool.dma_start(RH[:, P + 1:2 * P + 1], ff0T[1]).then_inc(w_in, 16)
            pool.dma_start(ff1s[:, :, :], ff1T.rearrange("k c o -> c k o")).then_inc(w_in, 16)

            for p in range(4):
                with pool.Fori(0, 2 * ITERS) as n:
                    it = pool.snap(n + 2 * ITERS * p)
                    h = pool.snap(n // ITERS)
                    first = pool.snap((n * 8 + h * 16) % NT, max_val=NT - 8)
                    for w in range(2):
                        row = pool.snap(((first + 2 * ((2 * w) ^ swapped(p)) + p % 2) * 2 + h) * P, max_val=(2 * NT - 1) * P)
                        pool.wait_ge(y_act, 8 * it + (4 * w + 5))
                        pool.dma_start(onehot_d[ds(row, P), :], SBw[:, w, 0, :]).then_inc(s_st[w][0], 16)
                        pool.wait_ge(k_made, 8 * it + (4 * w + 4))
                        pool.dma_start(onehot_d[ds(row + 2 * NT * P, P), :], SBw[:, w, 1, :])\
                            .then_inc(s_st[w][1], 16)
            for w in range(2):
                for k in range(2):
                    pool.wait_ge(s_st[w][k], 16 * USES_L2)
            pool.wait_ge(x_ready, 1)
            pool.wait_ge(cand_out, 16)
            pool.dma_start(QB[:, 0, 0:2 * P].rearrange("p (k c) -> p k c", k=2),
                           ff0.rearrange("k o c -> o k c")).then_inc(w_in, 16)
            pool.dma_start(attw, attc).then_inc(w_in, 16)
            pool.wait_ge(ext_made, 1)
            pool.partition_all_reduce(ext[:, 4:8], ext[:, 0:4], P, RMAX).then_inc(ext_all, 1)
            with pool.Fori(0, 4) as q:
                for s in range(32):
                    pool.wait_ge(r_made, 64 * q + (2 * s + 2))
                    pool.wait_ge(mask_made, 32 * q + (s + 1))
                    for k in range(0 if s in POOL_BOTH else 1, 2):
                        pool.tensor_tensor(QA[:, s % 3, k, :], QA[:, s % 3, k, :], Mt[:, s % 2, :], ALU.mult)\
                            .then_inc(p_pool, 1)

            pool.wait_ge(att_out, 64)
            pool.tensor_copy(DD[:, 0:P], notid[:, :])
            pool.memset(DD[:, P:2 * P], 1.0).then_inc(dd_made, 1)
            with pool.Fori(0, 2 * ITERS) as n:
                for k in range(8):
                    b, jj = k // 2, k % 2
                    pool.wait_ge(u_made, 8 * n + (k + 1))
                    pool.wait_ge(n_made, 8 * n + k)
                    pool.tensor_tensor(T[:, k % 2, :], A[b][:, jj * HALF:(jj + 1) * HALF], U[:, k, :], ALU.mult)\
                        .then_inc(t_made, 1)

            for b in range(NBUF):
                pool.wait_ge(a_out[b], USES_L3)
            pool.iota(segi.rearrange("p (s e) -> p s e", e=8), pattern=[[P, NT], [0, 8]], base=0,
                      channel_multiplier=0).then_inc(seg_made, 1)
            pool.wait_ge(seg_made, 1)
            pool.tensor_copy(segb, segi).then_inc(seg_made, 1)
            pool.wait_ge(idx_made, 1)
            pool.partition_all_reduce(lists_all, lists_any, P, RMAX).then_inc(used_made, 1)
            pool.wait_ge(used_made, 1)
            pool.tensor_scalar(lists_all, lists_all, 0.0, None, ALU.is_gt).then_inc(used_made, 1)
            pool.wait_ge(used_made, 2)
            pool.tensor_copy(used, lists_all).then_inc(used_made, 1)
            pool.wait_ge(used_made, 3)
            pool.wait_ge(tab_out, 32)
            with pool.Fori(0, NT // 2) as n:
                for w in range(2):
                    pool.wait_ge(g_used[w], n)
                    pool.tensor_copy(ixs[:, w, :], IDX[:, ds(2 * n + w, 1), :].squeeze(1)).then_inc(ix_cp, 1)
                    pool.wait_ge(ix_cp, 2 * n + (w + 1))
                    settled(pool)
                    def gather(e, landed):
                        pool.indirect_dma_start(G[:, w, e, :], None, table_d,
                                                bass.IndirectOffsetOnAxis(ap=ixs[:, w, e:e + 1], axis=0))\
                            .then_inc(landed, 16)

                    for e in range(REST - SPARE):
                        gather(e, g_in[w])
                    for e in range(REST - SPARE, REST, STEP):
                        some = pool.value_load(used[0:1, ds(pool.snap((2 * n + w) * (REST // STEP) + e // STEP), 1)],
                                               min_val=0, max_val=1)
                        with pool.If(some > 0):
                            for i in range(STEP):
                                gather(e + i, g_more[w])
                            pool.sem_inc(g_seen[w], 1)
                        with pool.Else():
                            pool.memset(G[:, w, e:e + STEP, :], 0.0).then_inc(g_seen[w], 1)
            pool.wait_ge(bad_made, 1)
            pool.partition_all_reduce(bad[:, 4:5], bad[:, 0:1], P, RMAX).then_inc(bad_all, 1)

        @block.tensor
        def _(pe):
            ms = Run()

            drained = [0]

            def drain():
                pe.wait_ge(ms_free, ms.n)
                drained[0] = ms.n

            def misc(n=BANK):
                if ms.n - 3 > drained[0]:
                    pe.wait_ge(ms_free, ms.n - 3)
                k = 4 + ms.n % 4
                ms.n += 1
                return bank(k, n)

            def transposes(src, norm=0):
                for g in range(8):
                    if norm:
                        pe.wait_ge(ln_act if g % 2 else ln_dve, 4 * (norm - 1) + g // 2 + 1)
                    m = misc()
                    for k in range(4):
                        t = 4 * g + k
                        last = pe.transpose(m[:, k * P:(k + 1) * P], src(t), ident[:, :])
                    last.then_inc(ms_full, 1)

            def features(lhsT, rhs):
                for g in range(8):
                    m = misc()
                    for k in range(4):
                        last = pe.matmul(m[:, k * P:(k + 1) * P], lhsT(4 * g + k), rhs, start=True, stop=True)
                    last.then_inc(ms_full, 1)

            def unit_step(w, s, it):
                g = 8 * it + (4 * w + s)
                if s < 4:
                    if s == 0:
                        pe.wait_ge(mk[w], it + 1)
                    pe.wait_ge(y_act, g)
                    pe.matmul(bank(4 + s % 2), rankw[:, :], M01[:, w, s * BANK:(s + 1) * BANK],
                              start=True, stop=True).then_inc(y_done, 1)
                if s > 0:
                    pe.wait_ge(k_made, g)
                    pe.wait_ge(m8_done, g - 1)
                    half = (s - 1) % 2
                    tb = bank(6 + half).bitcast(BF16)[:, 0:BANK]
                    for k in range(4):
                        last = pe.transpose(tb[:, k * P:(k + 1) * P],
                                            Kb[:, half, k * P:(k + 1) * P], identb[:, :])
                    last.then_inc(t_done, 1)

            UNIT_AT = {2 + 3 * s + 16 * w: (w, s) for w in range(2) for s in range(5)}

            def product(u0, aofs=0, p=None, weights=False):
                def turned_half(h):
                    pe.wait_ge(y_act, (u0 + ITERS * (h + 1)) * 8 + 1)
                    pe.wait_ge(m8_done, (u0 + ITERS * (h + 1)) * 8 + 1)
                    for k in range(4):
                        pe.wait_ge(acc_free, 4 * h + (8 * p + k + 1))
                        for i in range(4):
                            at, m = k * BANK + i * P, bank(4 + k)[:, i * P:(i + 1) * P]
                            if p == 1:
                                last = pe.matmul(m, OT[:, at:at + P], Wt[:, 1, :], start=True, stop=True)
                            else:
                                last = pe.transpose(m, OT[:, at:at + P], ident[:, :])
                        last.then_inc(ms_full, 1)

                with pe.Fori(0, 2) as h:
                    pe.wait_ge(acc_free, 4 * (u0 // (2 * ITERS)) * 2 + 4 * h)

                    def one(it, first, last):
                        u = pe.snap(h * ITERS + it)
                        for b in range(NBUF):
                            if not weights:
                                pe.wait_ge(a_in[b], 16 * u + 16 * (u0 + 1 + aofs))
                            pe.wait_ge(vs_in[b], 16 * u + 16 * (u0 + 1))
                            for m in range(8):
                                jj, k = m // 4, m % 4
                                if weights:
                                    if k == 0:
                                        pe.wait_ge(e_made, 8 * u + (2 * b + jj + 1))
                                    rhs = U[:, 2 * b + jj, k * BANK:(k + 1) * BANK]
                                else:
                                    rhs = A[b][:, jj * HALF + k * BANK:jj * HALF + (k + 1) * BANK]
                                ins = pe.matmul(bank(k), VS[:, b, jj, :], rhs,
                                                start=first and b == 0 and jj == 0,
                                                stop=last and b == NBUF - 1 and jj == 1)
                                if m == 7:
                                    ins.then_inc(a_out[b], 1)
                                if first and p is not None and 8 * b + m == 2:
                                    pe.wait_ge(ms_free, 4 * h + (8 * p + 8))
                                if p is not None and 8 * b + m in UNIT_AT:
                                    unit_step(*UNIT_AT[8 * b + m], u + u0)

                    one(0, True, False)
                    with pe.Fori(1, ITERS - 1) as it:
                        one(it, False, False)
                    one(ITERS - 1, False, True)
                    if p is not None:
                        turned_half(h)

            pe.wait_ge(x_in, 16)
            pe.wait_ge(w1_in, 16)
            features(lambda t: xT_s[:, t * P:(t + 1) * P], Wt[:, 0, :])
            pe.wait_ge(w_in, 16 * 15)
            pe.wait_ge(consts, 14)
            for p in range(4):
                product(2 * ITERS * p, p=p)
                ms.n += 8
            drain()

            transposes(lambda t: V[:, t, :], norm=2)
            pe.wait_ge(w_in, 16 * 17)
            m = misc()
            for k in range(2):
                last = pe.matmul(m[:, 2 * k:2 * k + 2], QB[:, 0, k * P:(k + 1) * P], attw[:, 2 * k:2 * k + 2],
                                 start=True, stop=True)
            last.then_inc(ms_full, 1)
            pe.wait_ge(ot_ready, 1)
            pe.wait_ge(sr_made, 1)
            for t in range(NT):
                m = misc(HW)
                pe.matmul(m, OT[:, t * P:(t + 1) * P], RH[:, :], start=True, stop=True).then_inc(ms_full, 1)
            pe.wait_ge(mx_made, 1)
            drain()
            m = misc(P)
            pe.transpose(m[0:2 * NT, :], MX.rearrange("p k t -> p (k t)"), ident[:, :]).then_inc(ms_full, 1)
            drain()

            def source_rows(q, k, used):
                pe.wait_ge(src_used, used)
                for e in range(2):
                    last = pe.matmul(bank(6 + e), SRt[:, k, :], OT[:, ds(q * QC + e * BANK, BANK)],
                                     start=True, stop=True)
                last.then_inc(src_full, 1)

            def region_of(k, it):
                r = 8 * k + it
                return PS[:, (r // 3) * BANK + (r % 3) * (P + 1):(r // 3) * BANK + (r % 3 + 1) * (P + 1)]

            ROWS_AT = ((26, 1), (31, 0))
            pe.wait_ge(h_made, 1)
            pe.sem_inc(p_used, 4)
            for k in range(2):
                source_rows(0, k, k)
            with pe.Fori(0, 4) as q:
                pe.wait_ge(att_out, 16 * q)
                for s in range(32):
                    j = pe.snap((8 * q + s) % NT, max_val=NT - 1)
                    for k in range(2):
                        if k == 1:
                            pe.wait_ge(p_pool, by_pool(31) * q + by_pool(s))
                        elif s in POOL_BOTH:
                            pe.wait_ge(p_pool, by_pool(31) * q + (by_pool(s) - 1))
                        else:
                            pe.wait_ge(p_dve, by_dve(31) * q + by_dve(s))
                        for it in range(8):
                            last = pe.matmul(region_of(k, it), QA[:, s % 3, k, it * P:(it + 1) * P],
                                             Hs[:, ds(j, 1), k * P:k * P + P + 1],
                                             start=s == 0 and (8 * k + it) % 3 == 0, stop=s == 31,
                                             skip_group_check=True)
                        last.then_inc(p_used, 1)
                        if (s, k) in ROWS_AT:
                            with pe.If(q < 3):
                                head = ROWS_AT.index((s, k))
                                source_rows(pe.snap((q + 1) % 4), head, 2 * q + (2 + head))
                            with pe.Else():
                                pass

            for k in range(2):
                src = V[:, :, :] if k == 0 else OT[:, :].rearrange("p (t c) -> p t c", c=P)
                transposes(lambda t: src[:, t, :], norm=3 + k)
            drain()
            for k in range(2):
                pe.wait_ge(qt_made, k + 1)
                features(lambda t: QT[:, k, t * P:(t + 1) * P], ff1s[:, k, :])
            drain()

            transposes(lambda t: X[:, t, :], norm=5)
            drain()
            pe.wait_ge(ot_ready, 2)
            features(lambda t: OT[:, t * P:(t + 1) * P], Wt[:, 2, :])
            product(USES_L2, weights=True)
            pe.wait_ge(ot_ready, 10)
            drain()
            transposes(lambda t: OT[:, t * P:(t + 1) * P])
            drain()

            transposes(lambda t: X[:, t, :], norm=6)
            drain()
            pe.wait_ge(ot_ready, 11)
            features(lambda t: OT[:, t * P:(t + 1) * P], Wt[:, 3, :])
            product(USES_L3, aofs=A_L1)
            pe.wait_ge(ot_ready, 19)
            drain()
            transposes(lambda t: OT[:, t * P:(t + 1) * P])
            drain()
            with pe.Fori(0, 2 * ITERS) as n:
                for b in range(NBUF):
                    pe.wait_ge(a_in[b], 48 * n + (16 * (USES_POOL + A_L1) + 48))
                    ob = A[b][:, HOTW:HOTW + 3 * P].bitcast(BF16).rearrange("p (e j c) -> p e j c", e=3, j=2)
                    hot = A[b][:, 0:HOTW].bitcast(FP8).rearrange("p (k j n) -> p k j n", k=SLOTS, j=2)
                    for jj in range(2):
                        for k in range(SLOTS):
                            g = (b * 2 + jj) * SLOTS + k
                            pe.wait_ge(px_free, NGRP * n + (g + 1))
                            settled(pe)
                            for e in range(3):
                                for c in range(4):
                                    last = pe.matmul(bank(4 * (g % 2) + c), ob[:, e, jj, :],
                                                     hot[:, k, jj, c * BANK:(c + 1) * BANK],
                                                     start=e == 0, stop=e == 2)
                            if g % (2 * SLOTS) == 2 * SLOTS - 1:
                                last.then_inc(a_out[b], 1)
                            else:
                                last.then_inc(px_full, 1)
            pe.wait_ge(px_free, NGRP * 2 * ITERS + 2)
            pe.wait_ge(x_ready, 4)
            transposes(lambda t: OT[:, t * P:(t + 1) * P])

        def half_out(act, n, u0, func, **kw):
            if isinstance(n, int):
                act.wait_ge(a_out[NBUF - 1], u0 + n + 1)
                for k in range(4):
                    at = n // ITERS * HALF + k * BANK
                    act.activation(OT[:, at:at + BANK], bank(k), func, **kw).then_inc(acc_free, 1)
                return
            with act.If(n == ITERS - 1):
                act.wait_ge(a_out[NBUF - 1], u0 + ITERS)
                for k in range(4):
                    act.activation(OT[:, k * BANK:(k + 1) * BANK], bank(k), func, **kw).then_inc(acc_free, 1)
            with act.Else():
                pass

        @block.scalar
        def _(act):
            ms = Run()

            def misc(n=BANK):
                ms.n += 1
                act.wait_ge(ms_full, ms.n)
                return bank(4 + (ms.n - 1) % 4, n)

            act.wait_ge(consts, 14)
            act.sem_inc(y_act, 1)

            def unit_chunk(w, s, it):
                act.wait_ge(y_done, 8 * it + (4 * w + s + 1))
                settled(act)
                if s == 0:
                    act.wait_ge(s_st[w][0], 16 * it)
                    settled(act)
                act.activation(SB[:, w, 0, s * BANK:(s + 1) * BANK], bank(4 + s % 2), ACT.Relu,
                               bias=cols[:, 7:8], saturate=False).then_inc(y_act, 1)

            def keep_cand(w, it, h, j):
                act.wait_ge(m8_done, 8 * it + (4 * w + 5))
                dst = cand.rearrange("p (h t) j e -> p h t j e", h=2)
                act.activation(dst[:, ds(h, 1), :, ds(j, 1), :], m8[:, w, :, :].unsqueeze(1), ACT.Copy)\
                    .then_inc(c_cp[w], 1)

            def rows_to(v, h, scale):
                for k in range(4):
                    act.wait_ge(ms_full, 4 * h + (ms.n + k + 1))
                    m = bank(4 + k)
                    if scale is None:
                        act.activation(v[:, ds(act.snap(16 * h + 4 * k), 4), :],
                                       m.rearrange("p (t c) -> p t c", c=P), ACT.Copy).then_inc(ms_free, 1)
                        continue
                    for i in range(4):
                        t = act.snap(16 * h + (4 * k + i))
                        ins = act.activation(v[:, ds(t, 1), :].squeeze(1), m[:, i * P:(i + 1) * P], ACT.Copy,
                                             scale=scale[:, ds(t, 1)])
                    ins.then_inc(ms_free, 1)
                act.wait_ge(ms_free, 4 * h + (ms.n + 4))
                act.sem_inc(v_ready, 1)

            def evacuate(u0, func, p=None, rows=None, **kw):
                with act.Fori(0, 2) as h:
                    if p is not None:
                        with act.Fori(0, ITERS) as k:
                            it = act.snap(h * ITERS + k + 2 * ITERS * p)
                            first = act.snap((h * 16 + k * 8) % NT, max_val=NT - 8)
                            jb = [act.snap(first + 2 * ((2 * w) ^ swapped(p)) + p % 2) for w in range(2)]
                            for w in range(2):
                                for s in range(4):
                                    unit_chunk(w, s, it)
                                    if w == 1 and s == 1:
                                        keep_cand(0, it, h, jb[0])
                            keep_cand(1, it, h, jb[1])
                    act.wait_ge(a_out[NBUF - 1], u0 + ITERS + ITERS * h)
                    for k in range(4):
                        to = OT[:, k * BANK:(k + 1) * BANK] if p is not None else \
                            OT[:, ds(h * HALF + k * BANK, BANK)]
                        act.activation(to, bank(k), func, **kw).then_inc(acc_free, 1)
                    if rows is not None:
                        rows_to(rows[0], h, rows[1])

            def to_v(v, scale=None, last=True):
                for g in range(8):
                    m = misc()
                    if scale is None:
                        act.activation(v[:, 4 * g:4 * g + 4, :], m.rearrange("p (t c) -> p t c", c=P),
                                       ACT.Copy).then_inc(ms_free, 1)
                    else:
                        for k in range(4):
                            t = 4 * g + k
                            ins = act.activation(v[:, t, :], m[:, k * P:(k + 1) * P], ACT.Copy,
                                                 scale=scale[:, t:t + 1])
                        ins.then_inc(ms_free, 1)
                act.wait_ge(ms_free, ms.n)
                act.sem_inc(v_ready, 1)

            to_v(v_of(0))
            act.sem_inc(v_ready, 1)
            evacuate(0, ACT.Copy, p=0, rows=(v_of(1), fcol[:, 0, :]))
            ms.n += 8
            evacuate(2 * ITERS, ACT.Relu, p=1, rows=(v_of(2), None))
            ms.n += 8
            evacuate(4 * ITERS, ACT.Copy, p=2, rows=(v_of(3), fcol[:, 1, :]))
            ms.n += 8
            evacuate(6 * ITERS, ACT.Copy, p=3)
            def normalise(n, dst, src, slot=0):
                act.wait_ge(ln_var, n)
                act.activation(rstd[:, slot, :], rstd[:, slot, :], ACT.Sqrt).then_inc(ln_std, 1)
                act.wait_ge(ln_mean, n)
                for g in range(1, 8, 2):
                    for t in range(4 * g, 4 * g + 4):
                        ins = act.activation(dst[:, t, :], src[:, t, :], ACT.Identity,
                                             scale=rstd[:, slot, t:t + 1], bias=st6[:, slot, t, 0:1])
                    ins.then_inc(ln_act, 1)

            normalise(1, X, X)

            def turned(dst, scale, bias):
                for g in range(8):
                    m = misc()
                    act.activation(dst[:, g * BANK:(g + 1) * BANK], m, ACT.Identity, scale=scale, bias=bias)\
                        .then_inc(ms_free, 1)
                act.wait_ge(ms_free, ms.n)

            normalise(2, V, X)
            ms.n += 8
            turned(OT, cols[:, 0:1], cols[:, 1:2])
            act.sem_inc(ot_ready, 1)
            m = misc(4)
            act.activation(RH[:, 2 * P + 1:2 * P + 5], m, ACT.Copy).then_inc(ms_free, 1)
            act.wait_ge(ms_free, ms.n)
            act.sem_inc(sr_made, 1)
            for t in range(NT):
                m = misc(HW)
                act.activation(Hs[:, t, :], m, ACT.Copy).then_inc(ms_free, 1)
            act.wait_ge(ms_free, ms.n)
            act.sem_inc(h_made, 1)
            ms.n += 1
            def step_free(q, s):
                if s != 2:
                    act.wait_ge(p_used, 64 * q + (2 + 2 * s if s < 2 else 2 * s))

            act.wait_ge(mxt_made, 1)
            flag = act.value_load(ext[0:1, 12:13].bitcast(I32), min_val=0, max_val=1)
            with act.If(flag > 0):
                with act.Fori(0, 4) as q:
                    for s in range(32):
                        j = act.snap((8 * q + s) % NT, max_val=NT - 1)
                        step_free(q, s)
                        for k in range(2):
                            if s == 0:
                                act.wait_ge(b_made, 2 * q + (k + 1))
                                act.wait_ge(r_made, 64 * q)
                            else:
                                act.wait_ge(r_made, 64 * q + (2 * s - 1 + k))
                            act.activation(QA[:, s % 3, k, :], Bx[:, k, 0, :], ACT.Exp,
                                           bias=Hs[:, ds(j, 1), 2 * P + 2 + 2 * k:2 * P + 3 + 2 * k].squeeze(1))
                            act.activation(QB[:, k, :], Bx[:, k, 1, :], ACT.Exp,
                                           bias=dst2[:, ds(j, 1), k:k + 1].squeeze(1)).then_inc(q_made, 1)
            with act.Else():
                for k in range(2):
                    act.activation(MX[:, k, :], Hs[:, :, 2 * P + 2 + 2 * k], ACT.Exp, bias=ext[:, k:k + 1])\
                        .then_inc(dst_exp, 1)
                    act.activation(dst2[:, :, k], dst2[:, :, k], ACT.Exp, bias=ext[:, 2 + k:3 + k])\
                        .then_inc(dst_exp, 1)
                act.wait_ge(dst_exp, 4)
                with act.Fori(0, 4) as q:
                    for s in range(32):
                        j = act.snap((8 * q + s) % NT, max_val=NT - 1)
                        step_free(q, s)
                        for k in range(2):
                            if s == 0:
                                src = PS[:, 6 * BANK:8 * BANK]
                                act.wait_ge(src_full, 2 * q + (k + 1))
                                act.wait_ge(q_made, 64 * q + k)
                                act.activation(Bx[:, k, 0, :], src, ACT.Relu, scale=-0.99,
                                               bias=ext[:, 16 + k:17 + k]).then_inc(row_neg, 1)
                                act.wait_ge(r_made, 64 * q)
                                act.activation(Bx[:, k, 1, :], src, ACT.Relu, scale=0.99,
                                               bias=ext[:, 18 + k:19 + k]).then_inc(row_neg, 1)
                                act.wait_ge(row_neg, 4 * q + (2 * k + 2))
                                act.sem_inc(src_used, 1)
                                act.activation(Bx[:, k, :, :], Bx[:, k, :, :], ACT.Exp, scale=-1.0)\
                                    .then_inc(row_exp, 1)
                                act.wait_ge(row_exp, 2 * q + (k + 1))
                            act.activation(QA[:, s % 3, k, :], Bx[:, k, 0, :], ACT.Copy,
                                           scale=MX[:, k, ds(j, 1)]).then_inc(q_made, 1)
            OTr = OT[:, :].rearrange("p (t c) -> p t c", c=P)
            for k, rows in enumerate((V, OTr)):
                normalise(3 + k, rows, rows, k)
                turned(QT[:, k, :], cols[:, 2:3], cols[:, 3:4])
                act.sem_inc(qt_made, 1)
            for g in range(17):
                if g < 16:
                    act.wait_ge(ms_full, ms.n + g + 1)
                    if g >= 4:
                        act.wait_ge(e_used, g - 3)
                    act.activation(e_t[:, g % 4, :], bank(4 + (ms.n + g) % 4), ACT.Relu, scale=-1.0)\
                        .then_inc(e_neg, 1)
                if g >= 1:
                    act.wait_ge(e_neg, g)
                    act.activation(e_t[:, (g - 1) % 4, :], e_t[:, (g - 1) % 4, :], ACT.Exp, scale=-1.0)\
                        .then_inc(e_exp, 1)
            ms.n += 16
            def guess(k, n, step):
                b, jj = k // 2, k % 2
                if step == 0:
                    act.wait_ge(s_made, 8 * n + (k + 1))
                    act.wait_ge(a_out[b], n + USES_L2)
                    act.activation(U[:, k, :], A[b][:, jj * HALF:(jj + 1) * HALF], ACT.Ln, bias=cols[:, 13:14])\
                        .then_inc(lnr, 1)
                else:
                    act.wait_ge(lnr, 8 * n + (k + 1))
                    act.activation(U[:, k, :], U[:, k, :], ACT.Exp, scale=-1.0).then_inc(u_made, 1)

            for k in range(4):
                guess(k, 0, 0)
            normalise(5, X, X)

            for g in range(8):
                m = misc()
                act.activation(OT[:, g * BANK:(g + 1) * BANK], m, ACT.Copy).then_inc(ms_free, 1)
            act.wait_ge(ms_free, ms.n)
            act.sem_inc(ot_ready, 1)
            ms.n += 8
            act.wait_ge(inv_made, 1)

            def weight(k, n, step):
                if step == 0:
                    if k in DVE_SQUARES:
                        return
                    act.wait_ge(n_made, 8 * n + (k + 2))
                    act.activation(U[:, k, :], U[:, k, :], ACT.Square, scale=cols[:, 11:12], bias=cols[:, 12:13])\
                        .then_inc(sq_made, 1)
                else:
                    if k in DVE_SQUARES:
                        act.wait_ge(sqd_made, len(DVE_SQUARES) * n + (DVE_SQUARES.index(k) + 1))
                    else:
                        rest = [i for i in range(8) if i not in DVE_SQUARES]
                        act.wait_ge(sq_made, len(rest) * n + (rest.index(k) + 1))
                    act.activation(U[:, k, :], U[:, k, :], ACT.Exp, scale=-1.0).then_inc(e_made, 1)

            def batch(first, n, before):
                if before is not None:
                    for k in range(first, first + 4):
                        guess(k, n, 0)
                for k in range(4):
                    guess(first + k, n, 1)
                    if before is not None:
                        for step in range(2):
                            weight(4 - first + k, before, step)

            batch(0, 0, None)
            with act.Fori(0, 2 * ITERS - 1) as n:
                batch(4, n, n)
                batch(0, n + 1, n)
                half_out(act, n, USES_L2, ACT.Copy)
            batch(4, 2 * ITERS - 1, 2 * ITERS - 1)
            for k in range(4, 8):
                for step in range(2):
                    weight(k, 2 * ITERS - 1, step)
            half_out(act, 2 * ITERS - 1, USES_L2, ACT.Copy)
            act.wait_ge(acc_free, 40)
            act.sem_inc(ot_ready, 8)
            ms.n += 8
            normalise(6, X, X)

            for g in range(8):
                m = misc()
                act.activation(OT[:, g * BANK:(g + 1) * BANK], m, ACT.Copy).then_inc(ms_free, 1)
            act.wait_ge(ms_free, ms.n)
            act.sem_inc(ot_ready, 1)
            to_v(V[:, :, :])
            evacuate(USES_L3, ACT.Relu, bias=cols[:, 4:5])
            act.wait_ge(acc_free, 48)
            act.sem_inc(ot_ready, 8)
            to_v(V[:, :, :])
            act.activation(OP[:, 0, :, :], V[:, :, :], ACT.Copy).then_inc(part_a, 1)
            r1v = r1.rearrange("p (t c) -> p t c", c=P)
            act.wait_ge(part_d, 1)
            act.activation(OP[:, 1, :, :], r1v, ACT.Copy).then_inc(part_a, 1)
            act.wait_ge(part_d, 2)
            act.activation(OP[:, 2, :, :], r1v, ACT.Copy).then_inc(part_a, 1)
            normalise(7, X, X)
        @block.vector
        def _(dve):
            own = Run()
            ms = Run()
            lns = Run()

            def did(ins):
                own.n += 1
                ins.then_inc(dv, 1)
                return own.n

            def after(n):
                dve.wait_ge(dv, n)

            dve.wait_ge(consts, 14)
            dve.sem_inc(m8_done, 1)

            def unit(w, it, p):
                dve.wait_ge(a_in[2 * w], 16 * it + 16)
                a = A[2 * w][:, :]
                jj = p % 2
                a = a[:, jj * HALF:(jj + 1) * HALF]
                dve.tensor_scalar(Mk[:, w, :], a, 0.0, cols[:, 6:7], ALU.not_equal, ALU.mult)
                dve.tensor_scalar(M01[:, w, :], a, 0.0, None, ALU.not_equal).then_inc(mk[w], 1)
                dve.wait_ge(s_st[w][1], 16 * it)
                dve.wait_ge(c_cp[w], it)
                dve.wait_ge(mk[w], it + 1)
                for s in range(5):
                    g = 8 * it + (4 * w + s)
                    if s < 4:
                        dve.wait_ge(y_act, g + 2)
                        settled(dve)
                        y = bank(4 + s % 2)
                        dve.tensor_scalar(SB[:, w, 1, s * BANK:(s + 1) * BANK], y, RANK - 1, None,
                                          ALU.is_equal, saturate=False)
                        dve.scalar_tensor_tensor(out=Kb[:, s % 2, :], in0=y, scalar=RANK - 1.5,
                                                 in1=Mk[:, w, s * BANK:(s + 1) * BANK],
                                                 op0=ALU.is_lt, op1=ALU.mult).then_inc(k_made, 1)
                    if s > 0:
                        dve.wait_ge(t_done, g)
                        settled(dve)
                        half = (s - 1) % 2
                        tb = bank(6 + half).bitcast(BF16)[:, 0:BANK]
                        for k in range(4):
                            last = dve.max(m8[:, w, 4 * (s - 1) + k, :], tb[:, k * P:(k + 1) * P])
                        last.then_inc(m8_done, 1)

            for p in range(3):
                with dve.Fori(2 * ITERS * p, 2 * ITERS * (p + 1)) as it:
                    unit(0, it, p)
                    unit(1, it, p)
            dve.wait_ge(x_in, 32)
            with dve.Fori(0, 2) as h:
                with dve.Fori(0, ITERS) as k:
                    it = dve.snap(h * ITERS + k + 6 * ITERS)
                    unit(0, it, 3)
                    unit(1, it, 3)
                for k in range(4):
                    dve.wait_ge(ms_full, 4 * h + (8 * 4 + k + 1))
                    xx = X[:, ds(dve.snap(16 * h + 4 * k), 4), :]
                    dve.tensor_tensor(xx, xx, bank(4 + k).rearrange("p (t c) -> p t c", c=P), ALU.add)\
                        .then_inc(ms_free, 1)
            dve.wait_ge(ms_free, 8 * 5)

            def normalise(dst, src, slot=0):
                lns.n += 1
                last = 0
                for t in range(NT):
                    last = did(dve.bn_stats(st6[:, slot, t, :], src[:, t, :]))
                after(last)
                for t in range(NT):
                    last = did(dve.bn_aggr(mv[:, slot, t, :], st6[:, slot, t, :]))
                after(last)
                dve.tensor_scalar(rstd[:, slot, :], mv[:, slot, :, 1], EPS, None, ALU.add).then_inc(ln_var, 1)
                dve.wait_ge(ln_std, lns.n)
                after(did(dve.reciprocal(rstd[:, slot, :], rstd[:, slot, :])))
                dve.scalar_tensor_tensor(out=st6[:, slot, :, 0], in0=mv[:, slot, :, 0], scalar=-1.0,
                                         in1=rstd[:, slot, :], op0=ALU.mult, op1=ALU.mult).then_inc(ln_mean, 1)
                for g in range(0, 8, 2):
                    for t in range(4 * g, 4 * g + 4):
                        ins = dve.tensor_scalar(dst[:, t, :], src[:, t, :], mv[:, slot, t, 0:1],
                                                rstd[:, slot, t:t + 1], ALU.subtract, ALU.mult)
                    ins.then_inc(ln_dve, 1)
                dve.wait_ge(ln_dve, 4 * lns.n)
                dve.wait_ge(ln_act, 4 * lns.n)

            def add_misc(n0):
                for g in range(8):
                    dve.wait_ge(ms_full, n0 + g + 1)
                    m = bank(4 + (n0 + g) % 4).rearrange("p (t c) -> p t c", c=P)
                    dve.tensor_tensor(X[:, 4 * g:4 * g + 4, :], X[:, 4 * g:4 * g + 4, :], m, ALU.add)\
                        .then_inc(ms_free, 1)
                dve.wait_ge(ms_free, n0 + 8)

            normalise(X, X)
            dve.sem_inc(x_ready, 1)

            after(did(dve.memset(RH[:, P:P + 1], 0.0)))
            normalise(V, X)
            dve.sem_inc(v_ready, 1)
            dve.wait_ge(sr_made, 1)
            after(did(dve.memset(SRt[:, :, :], 1.0)))
            for k in range(2):
                last = did(dve.tensor_scalar(SRt[:, k, :], SRt[:, k, :], RH[:, 2 * P + 1 + 2 * k:2 * P + 2 + 2 * k],
                                             None, ALU.mult))
            after(last)
            dve.wait_ge(h_made, 1)
            dsts = Hs[:, :, 2 * P + 2:2 * P + 5:2].rearrange("p t k -> p k t")
            did(dve.memset(Hs[:, :, P:P + 1], 1.0))
            did(dve.tensor_scalar(dst2.rearrange("p t k -> p k t"), dsts, 0.01, None, ALU.mult))
            did(dve.tensor_reduce(ext[:, 0:2], dsts, AX.X, ALU.max))
            after(did(dve.tensor_reduce(ext[:, 2:4], dsts, AX.X, ALU.min)))
            dve.tensor_scalar(ext[:, 2:4], ext[:, 2:4], -1.0, None, ALU.mult).then_inc(ext_made, 1)
            dve.wait_ge(ext_all, 1)
            did(dve.tensor_scalar(ext[:, 0:2], ext[:, 4:6], -1.0, None, ALU.mult))
            did(dve.tensor_scalar(ext[:, 2:4], ext[:, 4:6], -0.01, None, ALU.mult))
            did(dve.tensor_scalar(ext[:, 16:18], ext[:, 4:6], -0.99, None, ALU.mult))
            did(dve.tensor_scalar(ext[:, 18:20], ext[:, 4:6], 0.99, None, ALU.mult))
            after(did(dve.tensor_tensor(ext[:, 8:10], ext[:, 4:6], ext[:, 6:8], ALU.add)))
            after(did(dve.tensor_reduce(ext[:, 10:11], ext[:, 8:10], AX.X, ALU.max)))
            dve.tensor_scalar(ext[:, 12:13].bitcast(I32), ext[:, 10:11], SPREAD, None, ALU.is_gt)\
                .then_inc(flag_made, 1)
            after(did(dve.memset(MX[:, :, :], 0.0)))
            for k in range(2):
                last = did(dve.tensor_scalar(MX[:, k, :], MX[:, k, :], ext[:, 4 + k:5 + k], None, ALU.add))
            after(last)
            dve.wait_ge(flag_made, 1)
            flag = dve.value_load(ext[0:1, 12:13].bitcast(I32), min_val=0, max_val=1)
            with dve.If(flag > 0):
                dve.wait_ge(gen_in, 16 * 4)
                for k in range(2):
                    dve.tensor_scalar(A[1 + k][:, :], A[1 + k][:, :], ext[:, 6 + k:7 + k], None, ALU.add)\
                        .then_inc(gen_own, 1)
                dve.wait_ge(gen_own, 2)
                with dve.Fori(0, NT) as t:
                    dve.wait_ge(gen_row, 16 * t + 16)
                    for k in range(2):
                        c = 2 + t * 6 + 3 * k
                        dve.scalar_tensor_tensor(out=A[3][:, :], in0=A[0][:, :], scalar=0.0, in1=A[1 + k][:, :],
                                                 op0=ALU.is_gt, op1=ALU.mult).then_inc(gen_own, 1)
                        dve.wait_ge(gen_own, c + 1)
                        dve.tensor_reduce(ext[:, 13:14], A[3][:, :], AX.X, ALU.max).then_inc(gen_own, 1)
                        dve.wait_ge(gen_own, c + 2)
                        ins = dve.scalar_tensor_tensor(out=MX[:, k, ds(t, 1)], in0=ext[:, 13:14],
                                                       scalar=ext[:, 6 + k:7 + k],
                                                       in1=Hs[:, ds(t, 1), 2 * P + 2 + 2 * k:2 * P + 3 + 2 * k].squeeze(1),
                                                       op0=ALU.subtract, op1=ALU.max).then_inc(gen_own, 1)
                        dve.wait_ge(gen_own, c + 3)
                    dve.sem_inc(gen_used, 1)
            with dve.Else():
                pass
            dve.sem_inc(mx_made, 1)
            n_m = 8 * 6 + 1 + NT
            dve.wait_ge(ms_full, n_m + 1)
            dve.tensor_copy(MXT[0:2 * NT, :], bank(4 + n_m % 4)[0:2 * NT, 0:P]).then_inc(ms_free, 1)
            dve.wait_ge(ms_free, n_m + 1)
            dve.sem_inc(mxt_made, 1)

            def region_of(k, it):
                r = 8 * k + it
                return PS[:, (r // 3) * BANK + (r % 3) * (P + 1):(r // 3) * BANK + (r % 3 + 1) * (P + 1)]

            OTr = OT[:, :].rearrange("p (t c) -> p t c", c=P)

            def row_parts(q):
                dve.wait_ge(smax_in, 32 * q + 32)
                dve.wait_ge(q_made, 64 * q)
                for k in range(2):
                    dve.wait_ge(src_full, 2 * q + (k + 1))
                    src = PS[:, 6 * BANK:8 * BANK]
                    b1_, b2_ = Bx[:, k, 0, :], Bx[:, k, 1, :]
                    dve.tensor_tensor(b1_, src, b2_, ALU.add).then_inc(ch_rows, 1)
                    dve.wait_ge(ch_rows, 6 * q + (3 * k + 1))
                    dve.scalar_tensor_tensor(out=b2_, in0=b1_, scalar=0.01, in1=b1_, op0=ALU.mult, op1=ALU.max)\
                        .then_inc(ch_rows, 1)
                    dve.wait_ge(ch_rows, 6 * q + (3 * k + 2))
                    dve.tensor_tensor(b1_, src, b2_, ALU.subtract).then_inc(ch_rows, 1)
                    dve.scalar_tensor_tensor(out=b2_, in0=src, scalar=0.01, in1=b2_, op0=ALU.mult,
                                             op1=ALU.subtract).then_inc(b_made, 1)
                    dve.wait_ge(ch_rows, 6 * q + (3 * k + 3))
                    dve.wait_ge(b_made, 2 * q + (k + 1))
                    dve.sem_inc(src_used, 1)

            def mask_of(q, s):
                b, w = (s // 4) % NBUF, s % 2
                if s % 4 == 0:
                    dve.wait_ge(a_in[b], 16 * (USES_L2 + s // 16 + 1) + 32 * q)
                dve.wait_ge(p_pool, by_pool(31) * q + (by_pool(s - 2) if s > 1 else 0))
                dve.tensor_scalar(Mt[:, w, :], A[b][:, (s % 4) * QC:(s % 4 + 1) * QC], 0.0, None, ALU.is_gt)\
                    .then_inc(mask_made, 1)
                dve.wait_ge(mask_made, 32 * q + (s + 1))
                if s < 8:
                    d = Mt[:, w, s * P:(s + 1) * P]
                    dve.tensor_tensor(d, d, identb[:, :], ALU.max).then_inc(ch, 1)
                    dve.wait_ge(ch, 8 * q + (1 + s))

            def chunks(general):
                if general:
                    row_parts(0)
                else:
                    dve.wait_ge(dst_exp, 4)
                with dve.Fori(0, 4) as q:
                    for s in range(32):
                        w = s % 3
                        j = dve.snap((8 * q + s) % NT, max_val=NT - 1)
                        if s == 0:
                            mask_of(q, 0)
                        for k in range(2):
                            dve.wait_ge(q_made, 64 * q + (2 * s + k + 1))
                            if s == 0 and not general:
                                dve.wait_ge(row_exp, 2 * q + (k + 1))
                            if not general:
                                dve.scalar_tensor_tensor(out=QA[:, w, k, :], in0=Bx[:, k, 1, :],
                                                         scalar=dst2[:, ds(j, 1), k:k + 1].squeeze(1),
                                                         in1=QA[:, w, k, :], op0=ALU.mult, op1=ALU.max)\
                                    .then_inc(r_made, 1)
                                continue
                            if general:
                                dve.tensor_scalar(QB[:, k, :], QB[:, k, :], 1.0, None, ALU.min).then_inc(gen_q, 1)
                                dve.wait_ge(gen_q, 64 * q + (2 * s + k + 1))
                            dve.scalar_tensor_tensor(out=QA[:, w, k, :], in0=QA[:, w, k, :], scalar=1.0,
                                                     in1=QB[:, k, :], op0=ALU.min, op1=ALU.max).then_inc(r_made, 1)
                        if s not in POOL_BOTH:
                            dve.wait_ge(r_made, 64 * q + (2 * s + 1))
                            dve.tensor_tensor(QA[:, w, 0, :], QA[:, w, 0, :], Mt[:, s % 2, :], ALU.mult)\
                                .then_inc(p_dve, 1)
                        if s < 31:
                            mask_of(q, s + 1)
                    if general:
                        with dve.If(q < 3):
                            row_parts(dve.snap(q + 1))
                        with dve.Else():
                            pass
                    dve.wait_ge(p_used, 64 * q + 68)
                    for k in range(2):
                        for it in range(8):
                            r = region_of(k, it)
                            dve.reciprocal(rden[:, 8 * k + it:8 * k + it + 1],
                                           r[:, P:P + 1] if k == 0 else r[:, 0:1]).then_inc(rd_made, 1)
                    for k in range(2):
                        for it in range(8):
                            r = region_of(k, it)
                            dve.wait_ge(rd_made, 16 * q + (8 * k + it + 1))
                            dst = V if k == 0 else OTr
                            dve.scalar_tensor_tensor(out=dst[:, ds(8 * q + it, 1), :].squeeze(1),
                                                     in0=r[:, 0:P] if k == 0 else r[:, 1:P + 1],
                                                     scalar=rden[:, 8 * k + it:8 * k + it + 1],
                                                     in1=X[:, ds(8 * q + it, 1), :].squeeze(1),
                                                     op0=ALU.mult, op1=ALU.add).then_inc(att_out, 1)
                    dve.wait_ge(att_out, 16 * q + 16)

            with dve.If(flag > 0):
                chunks(True)
            with dve.Else():
                chunks(False)
            normalise(V, V, 0)
            normalise(OTr, OTr, 1)
            n_m += 1 + 16
            def cut(k, n):
                b, jj = k // 2, k % 2
                a = A[b][:, jj * HALF:(jj + 1) * HALF]
                dve.wait_ge(a_in[b], 16 * n + 16 * (USES_L2 + A_L1 + 1))
                dve.scalar_tensor_tensor(out=a, in0=a, scalar=0.5, in1=a, op0=ALU.is_lt, op1=ALU.mult)\
                    .then_inc(s_own, 1)
                dve.wait_ge(s_own, 8 * n + (k + 1))
                if isinstance(n, int):
                    col, diag = (8 * n + k) % 16 * P, (n % 4) // 2 * P
                    d, dd = a[:, col:col + P], DD[:, diag:diag + P]
                else:
                    d = A[b][:, ds(dve.snap((n * 8 + k) % 16 * P + jj * HALF, max_val=31 * P), P)]
                    dd = DD[:, ds(dve.snap((n % 4) // 2 * P, max_val=P), P)]
                dve.tensor_tensor(d, d, dd, ALU.mult).then_inc(s_made, 1)

            after(did(dve.tensor_scalar(X[:, :, :], X[:, :, :], -1.0, None, ALU.add)))
            dve.wait_ge(dd_made, 1)
            for k in range(4):
                cut(k, 0)
            for g in range(17):
                if g < 16:
                    dve.wait_ge(e_exp, g + 1)
                    e = e_t[:, g % 4, :]
                    dve.scalar_tensor_tensor(out=e, in0=bank(4 + (n_m + g) % 4), scalar=0.0, in1=e,
                                             op0=ALU.max, op1=ALU.add).then_inc(ms_free, 1)
                if g >= 1:
                    i = g - 1
                    dve.wait_ge(ms_free, n_m + i + 1)
                    if i >= 8:
                        dve.wait_ge(e_used, i - 7)
                    xx = X[:, 4 * (i % 8):4 * (i % 8) + 4, :]
                    dve.scalar_tensor_tensor(out=xx, in0=e_t[:, i % 4, :].rearrange("p (t c) -> p t c", c=P),
                                             scalar=0.5, in1=xx, op0=ALU.mult, op1=ALU.add).then_inc(e_used, 1)
            dve.wait_ge(e_used, 16)
            normalise(X, X)
            dve.sem_inc(x_ready, 1)

            dve.sem_inc(n_made, 1)
            did(dve.reciprocal(cols[:, 10:11], cols[:, 8:9]))
            after(did(dve.reciprocal(cols[:, 11:12], cols[:, 9:10])))
            after(did(dve.tensor_scalar(cols[:, 11:12], cols[:, 11:12], -(0.5 ** 0.5), None, ALU.mult)))
            after(did(dve.tensor_tensor(cols[:, 12:13], cols[:, 10:11], cols[:, 11:12], ALU.mult)))
            dve.sem_inc(inv_made, 1)
            dve.wait_ge(l2c_in, 16)
            n_m = 114 + 8
            for g in range(8):
                dve.wait_ge(ms_full, n_m + g + 1)
                m = bank(4 + (n_m + g) % 4).rearrange("p (t c) -> p t c", c=P)
                dve.tensor_tensor(V[:, 4 * g:4 * g + 4, :], m, BB.unsqueeze(1).broadcast_to([P, 4, P]), ALU.add)\
                    .then_inc(ms_free, 1)
            dve.wait_ge(ms_free, n_m + 8)
            dve.sem_inc(v_ready, 1)

            def newton(k, n):
                dve.wait_ge(t_made, 8 * n + (k + 1))
                dve.scalar_tensor_tensor(out=U[:, k, :], in0=T[:, k % 2, :], scalar=2.0, in1=U[:, k, :],
                                         op0=ALU.subtract, op1=ALU.mult).then_inc(n_made, 1)

            def square(k, n):
                i = 2 * DVE_SQUARES.index(k)
                u = U[:, k, :]
                dve.wait_ge(n_made, 8 * n + (k + 2))
                dve.tensor_scalar(u, u, cols[:, 11:12], cols[:, 12:13], ALU.mult, ALU.add).then_inc(sq_own, 1)
                dve.wait_ge(sq_own, len(DVE_SQUARES) * n + (i // 2 + 1))
                dve.tensor_tensor(u, u, u, ALU.mult).then_inc(sqd_made, 1)

            def newtons(first, n):
                for k in range(first, first + 4):
                    newton(k, n)
                    if k in DVE_SQUARES:
                        square(k, n)

            def cuts(first, n):
                for k in range(first, first + 4):
                    cut(k, n)

            cuts(4, 0)
            newtons(0, 0)
            with dve.Fori(0, 2 * ITERS - 1) as n:
                for first in range(0, 8, 4):
                    cuts(first, n + 1)
                    newtons(4 - first, n if first == 0 else n + 1)
            newtons(4, 2 * ITERS - 1)
            add_misc(n_m + 8)
            normalise(X, X)
            dve.sem_inc(x_ready, 1)

            own_l = [0]

            def lists(ins, n=None):
                own_l[0] += 1
                ins.then_inc(lw, 1)
                dve.wait_ge(lw, own_l[0] if n is None else n + own_l[0])
                if n is not None:
                    settled(dve)

            dve.wait_ge(cand_in, 16)
            dve.wait_ge(seg_made, 2)
            lists(dve.tensor_reduce(bad[:, 1:2], cand2.rearrange("p t (j e) -> p (t j) e", e=8)[:, :, 7], AX.X, ALU.max))
            lists(dve.memset(bad[:, 2:3], 0.0))
            base = own_l[0]
            STEPS = 9
            with dve.Fori(0, NT) as t:
                own_l[0] = base
                at_ = t * STEPS
                c = cand2[:, ds(t, 1), :].squeeze(1)
                lists(dve.scalar_tensor_tensor(out=K1, in0=c, scalar=0.0, in1=segb, op0=ALU.is_gt, op1=ALU.mult), at_)
                lists(dve.tensor_tensor(K1, K1, c, ALU.add), at_)
                lists(dve.max(m8x[:, 0:8], K1), at_)
                lists(dve.match_replace(out=K2, in_to_replace=m8x[:, 0:8], in_values=K1, imm_value=0.0), at_)
                lists(dve.max(m8x[:, 8:16], K2), at_)
                lists(dve.match_replace(out=K1, in_to_replace=m8x[:, 8:16], in_values=K2, imm_value=0.0), at_)
                lists(dve.max(m8x[:, 16:24], K1), at_)
                lists(dve.tensor_copy(LST[:, ds(t, 1), :].squeeze(1), m8x[:, 0:REST]), at_)
                lists(dve.tensor_tensor(bad[:, 2:3], bad[:, 2:3], m8x[:, REST:REST + 1], ALU.max), at_)
            own_l[0] = base + STEPS * NT
            flat = LST.rearrange("p t e -> p (t e)")
            tmp = r1[:, 0:NT * REST]
            lists(dve.tensor_scalar(tmp, flat, 0.0, float(N + 1), ALU.is_equal, ALU.mult))
            lists(dve.tensor_copy(lists_any.rearrange("p (t g) -> p t g", t=NT), LST[:, :, 0:REST:STEP]))
            dve.scalar_tensor_tensor(out=IDX.rearrange("p t e -> p (t e)"), in0=flat, scalar=-1.0, in1=tmp,
                                     op0=ALU.add, op1=ALU.add).then_inc(idx_made, 1)
            dve.memset(K1[:, 0:P], 0.0).then_inc(zero_made, 1)

            dve.wait_ge(v_ready, 12)
            dve.wait_ge(idx_made, 1)
            dve.wait_ge(part_a, 1)
            Vf = V[:, :, :].rearrange("p t c -> p (t c)")
            dve.tensor_tensor(r1, Vf, OP[:, 0, :, :].rearrange("p t c -> p (t c)"), ALU.subtract).then_inc(part_d, 1)
            dve.wait_ge(part_d, 1)
            dve.wait_ge(part_a, 2)
            dve.tensor_tensor(r1, r1, OP[:, 1, :, :].rearrange("p t c -> p (t c)"), ALU.subtract).then_inc(part_d, 1)
            dve.wait_ge(tab_out, 32)
            dve.wait_ge(ot_ready, 19)
            dve.wait_ge(v_ready, 12)
            after(did(dve.memset(OT[:, :], 0.0)))
            dve.sem_inc(px_free, 2)
            more = [dve.alloc_register(f"more{w}") for w in range(2)]
            for w in range(2):
                dve.reg_mov(more[w], 0)
            dve.wait_ge(used_made, 2)
            after(did(dve.tensor_reduce(rowm, lists_all.rearrange("p (t g) -> p t g", t=NT)[:, :, (REST - SPARE) // STEP:],
                                        AX.X, ALU.add)))
            after(did(dve.tensor_copy(steps, rowm)))

            def landed(t, w, r):
                dve.wait_ge(g_in[w], 16 * (REST - SPARE) * r + 16 * (REST - SPARE))
                dve.wait_ge(g_seen[w], SPARE // STEP * r + SPARE // STEP)
                cell = steps[0:1, t:t + 1] if isinstance(t, int) else steps[0:1, ds(t, 1)]
                taken = dve.value_load(cell, min_val=0, max_val=SPARE // STEP)
                dve.reg_add(more[w], more[w], dve.to_reg(dve.snap(taken * (16 * STEP))))
                with dve.If(taken > 0):
                    dve.wait_ge(g_more[w], more[w])
                    settled(dve)
                with dve.Else():
                    pass

            def greatest(t, w, part):
                c = slice(part * P // 4, (part + 1) * P // 4)
                v = V[:, t, c] if isinstance(t, int) else V[:, ds(t, 1), c].squeeze(1)
                ins = dve.tensor_reduce(v, G[:, w, :, c].rearrange("p k c -> p c k"), AX.X, ALU.max)
                if part == 3:
                    ins.then_inc(g_used[w], 1)

            with dve.Fori(0, 2 * ITERS) as n:
                half = OT[:, ds(n // ITERS * HALF, HALF)]
                for g in range(NGRP):
                    b = g // (2 * SLOTS)
                    full = 2 * SLOTS - 1
                    if g % (2 * SLOTS) == full:
                        dve.wait_ge(a_out[b], n + (USES_POOL + 1))
                    else:
                        dve.wait_ge(px_full, n * (NBUF * full) + (b * full + g % (2 * SLOTS) + 1))
                    dve.wait_ge(px_free, NGRP * n + (g + 2))
                    src = PS[:, 4 * (g % 2) * BANK:(4 * (g % 2) + 4) * BANK]
                    dve.tensor_tensor(half, half, src, ALU.max).then_inc(px_free, 1)
                    w = (g // 4 + 1) % 2
                    if g > 3:
                        t = dve.snap(4 * n + (g // 4 - 1))
                        if g % 4 == 0:
                            landed(t, w, dve.snap(2 * n + (g // 4 - 1) // 2))
                        greatest(t, w, g % 4)
                    else:
                        with dve.If(n > 0):
                            t = dve.snap((4 * n + (NT - 1)) % NT)
                            if g % 4 == 0:
                                landed(t, w, dve.snap((2 * n + (NT // 2 - 1)) % (NT // 2)))
                            greatest(t, w, g % 4)
                        with dve.Else():
                            pass
            landed(NT - 1, 1, NT // 2 - 1)
            for part in range(4):
                greatest(NT - 1, 1, part)
            dve.wait_ge(px_free, NGRP * 2 * ITERS + 2)
            for w in range(2):
                dve.wait_ge(g_used[w], NT // 2)
            dve.sem_inc(x_ready, 1)
            n_m = 162
            for g in range(8):
                dve.wait_ge(ms_full, n_m + g + 1)
                m = bank(4 + (n_m + g) % 4).rearrange("p (t c) -> p t c", c=P)
                dve.tensor_tensor(V[:, 4 * g:4 * g + 4, :], V[:, 4 * g:4 * g + 4, :], m, ALU.max)\
                    .then_inc(ms_free, 1)
            dve.wait_ge(ms_free, n_m + 8)
            after(did(dve.tensor_reduce(rowm, V[:, :, :], AX.X, ALU.max)))
            after(did(dve.tensor_reduce(bad[:, 3:4], rowm, AX.X, ALU.min)))
            after(did(dve.tensor_scalar(bad[:, 3:4], bad[:, 3:4], 0.0, None, ALU.is_equal)))
            after(did(dve.tensor_reduce(bad[:, 0:1], bad[:, 1:4], AX.X, ALU.max)))
            dve.sem_inc(bad_made, 1)
            dve.wait_ge(bad_all, 1)
            dve.tensor_scalar(bad[:, 8:9].bitcast(I32), bad[:, 4:5], 0.0, None, ALU.is_gt).then_inc(flag2, 1)
            dve.wait_ge(flag2, 1)
            flag = dve.value_load(bad[0:1, 8:9].bitcast(I32), min_val=0, max_val=1)
            with dve.If(flag > 0):
                tmpv = A[2][:, :].rearrange("p (c j) -> p c j", j=32)
                part = A[3][:, 0:P]
                msk = A[3][:, P:P + 32]
                has = A[3][:, 2 * P:2 * P + 1]
                hc = A[3][:, 2 * P + 1:2 * P + 2]
                with dve.Fori(0, NT) as t:
                    v = V[:, ds(t, 1), :].squeeze(1)
                    t0 = t * (5 * 4 * NT + 4)
                    dve.tensor_copy(v, K1[:, 0:P]).then_inc(dn, 1)
                    dve.memset(has, 0.0).then_inc(dn, 1)
                    with dve.Fori(0, 4 * NT) as c:
                        c0 = t0 + c * 5
                        dve.wait_ge(dn, t0 + 2)
                        dve.wait_ge(dn_in, 32 * (t * (4 * NT) + c + 1))
                        dve.tensor_scalar(msk, A[1][:, 0:32], 0.0, None, ALU.not_equal).then_inc(dn, 1)
                        dve.wait_ge(dn, c0 + 3)
                        dve.tensor_tensor(tmpv, A[0][:, :].rearrange("p (j c) -> p c j", c=P),
                                          msk.unsqueeze(1).broadcast_to([P, P, 32]), ALU.mult).then_inc(dn, 1)
                        dve.tensor_reduce(hc, msk, AX.X, ALU.max).then_inc(dn, 1)
                        dve.wait_ge(dn, c0 + 5)
                        dve.sem_inc(dn_used, 2)
                        dve.tensor_reduce(part, tmpv, AX.X, ALU.max).then_inc(dn, 1)
                        dve.tensor_tensor(has, has, hc, ALU.max).then_inc(dn, 1)
                        dve.wait_ge(dn, c0 + 7)
                        dve.tensor_tensor(v, v, part, ALU.max).then_inc(dnv, 1)
                        dve.wait_ge(dnv, t * (4 * NT) + c + 1)
                    t1 = t0 + 5 * 4 * NT
                    dve.tensor_scalar(has, has, -1.0, BIG, ALU.add, ALU.mult).then_inc(dn, 1)
                    dve.wait_ge(dn, t1 + 3)
                    dve.tensor_scalar(v, v, has, None, ALU.add).then_inc(dn, 1)
                    dve.wait_ge(dn, t1 + 4)
            with dve.Else():
                pass
            after(did(dve.tensor_tensor(X[:, :, :], X[:, :, :], V[:, :, :], ALU.add)))
            normalise(X, X)
            dve.sem_inc(x_ready, 1)


_INS = ["x", "xT", "adj", "adjT", "W1", "f1", "W2", "f2", "ff0", "ff0T", "ff1T", "attc", "g1", "b1", "g2", "b2",
        "L2W", "L2B", "mu", "sigma", "L3W", "L3b"]


def laid_out(x, adj, L0_gnn_W1, L0_gnn_f1, L0_gnn_W2, L0_gnn_f2, L1_gnn_ff0_w, L1_gnn_ff1_w, L1_gnn_attn_w,
             L1_gnn_g1, L1_gnn_b1, L1_gnn_g2, L1_gnn_b2, L2_gnn_W, L2_gnn_B, L2_gnn_mu, L2_gnn_sigma,
             L3_gnn_weight, L3_gnn_bias):
    import numpy as np

    def a(v):
        return np.asarray(v)

    return {
        "x": a(x), "xT": a(x).T, "adj": a(adj), "adjT": a(adj).T,
        "W1": a(L0_gnn_W1), "f1": a(L0_gnn_f1).reshape(NT, P).T, "W2": a(L0_gnn_W2),
        "f2": a(L0_gnn_f2).reshape(NT, P).T,
        "ff0": a(L1_gnn_ff0_w), "ff0T": a(L1_gnn_ff0_w).transpose(0, 2, 1),
        "ff1T": a(L1_gnn_ff1_w).transpose(0, 2, 1),
        "attc": a(L1_gnn_attn_w).reshape(4, P).T,
        "g1": a(L1_gnn_g1).reshape(P, 1), "b1": a(L1_gnn_b1).reshape(P, 1),
        "g2": a(L1_gnn_g2).reshape(P, 1), "b2": a(L1_gnn_b2).reshape(P, 1),
        "L2W": a(L2_gnn_W), "L2B": a(L2_gnn_B).reshape(1, P),
        "mu": a(L2_gnn_mu), "sigma": a(L2_gnn_sigma),
        "L3W": a(L3_gnn_weight), "L3b": a(L3_gnn_bias).reshape(P, 1),
    }


def kernel(**inputs):
    import numpy as np
    import concourse.bacc as bacc
    from concourse.bass_utils import run_bass_kernel_spmd as run

    nc = bacc.Bacc("TRN2", target_bir_lowering=False, num_devices=1)
    arrays, args = {}, []
    for name, v in laid_out(**inputs).items():
        arrays[f"in_{name}"] = np.ascontiguousarray(v)
        args.append(nc.dram_tensor(f"in_{name}", v.shape, mybir.dt.from_np(v.dtype), kind="ExternalInput").ap())
    args.append(nc.dram_tensor("out", (N, P), F32, kind="ExternalOutput").ap())
    program(nc, *args)
    r = run(nc, [arrays], core_ids=[0])
    return r.results[0]["out"]
```
